# Optimizing a Trainium2 kernel written in Bass

```python
import numpy as np
import jax
import jax.numpy as jnp

def _softmax(x, axis=-1):
    return jax.nn.softmax(x, axis=axis)

def _gelu(x):
    return jax.nn.gelu(x, approximate=True)

def _silu(x):
    return jax.nn.silu(x)

def _sigmoid(x):
    return jax.nn.sigmoid(x)

def _layernorm(x, axis=-1, eps=1e-05):
    m = jnp.mean(x, axis=axis, keepdims=True)
    v = jnp.var(x, axis=axis, keepdims=True)
    return (x - m) / jnp.sqrt(v + eps)

def _scatter_add(tgt, idx, src, axis=0):
    return tgt.at[idx].add(src)

def _segment_sum(src, seg, n):
    return jax.ops.segment_sum(src, seg, n)
kernel_name = 'mk_decoder_postln_d1_seqx_r8_986c12'

def setup_inputs(seed: int=0):
    np.random.seed(seed)
    _w = jnp.asarray

    def _rec_inputs():
        import jax
        import jax.numpy as jnp
        _rk = jax.random.key(seed)
        x = -0.0003929 + 0.9999 * jax.random.normal(jax.random.fold_in(_rk, 1), (8, 128, 512), jnp.float32)
        _lenS = 128 - jax.random.randint(jax.random.fold_in(_rk, 7), (8,), 0, max(1, 128 // 4) + 1, jnp.int32)
        _lenS2 = 128 - jax.random.randint(jax.random.fold_in(_rk, 8), (8,), 0, max(1, 128 // 4) + 1, jnp.int32)
        _ctx_4096P = jax.random.normal(jax.random.fold_in(_rk, 11), (8, 16, 512), jnp.float32)
        _ctx_4096c = jax.random.dirichlet(jax.random.fold_in(_rk, 511), 0.3 * jnp.ones((16,), jnp.float32), (8, 128))
        _ctx_4096t = jnp.einsum('bsk,bkd->bsd', _ctx_4096c, _ctx_4096P)
        _ctx_4096t = _ctx_4096t * jax.lax.rsqrt(jnp.mean(jnp.square(_ctx_4096t)) + 1e-12) * 0.953939
        ctx_4096 = 2.81802e-05 + 1.00001 * (_ctx_4096t + 0.3 * jax.random.normal(jax.random.fold_in(_rk, 611), (8, 128, 512), jnp.float32))
        _validS = jnp.arange(128)[None, :] < _lenS[:, None]
        _validS2 = jnp.arange(128)[None, :] < _lenS2[:, None]
        _causal = jnp.tril(jnp.ones((128, 128), dtype=bool))
        mask_BxSxS2_ff0 = jnp.where(jnp.ones((8, 128, 128), dtype=bool), 0.0, -1000000000.0).astype(jnp.float32)
        return (x, ctx_4096, mask_BxSxS2_ff0)
    x, ctx_4096, mask_BxSxS2_ff0 = _rec_inputs()

    def _L0_attn_setup():
        import math
        import jax, jax.numpy as jnp
        import numpy as np
        N_HEADS = 32
        ALIBI_BIAS_MAX = 8

        def _alibi_slopes(n_heads, alibi_bias_max=8):
            _n = 2 ** math.ceil(math.log2(n_heads))
            m = jnp.arange(1, _n + 1, dtype=jnp.float32) * (alibi_bias_max / _n)
            slopes = 1.0 / jnp.power(2.0, m)
            if _n != n_heads:
                slopes = jnp.concatenate([slopes[1::2], slopes[::2]])[:n_heads]
            return slopes
        key = jax.random.key(seed)
        k1, k2, k3 = jax.random.split(key, 3)
        B, S, D = (1, 256, 512)
        x = jax.random.normal(k1, (B, S, D), dtype=jnp.float32)
        w_qkv = jax.random.normal(k2, (3 * D, D), dtype=jnp.float32) * 0.02
        b_qkv = jnp.zeros((3 * D,), dtype=jnp.float32)
        w_out = jax.random.normal(k3, (D, D), dtype=jnp.float32) * 0.02
        b_out = jnp.zeros((D,), dtype=jnp.float32)
        return {'x': x, 'w_qkv': w_qkv, 'b_qkv': b_qkv, 'w_out': w_out, 'b_out': b_out}
    _L0_attn_all = _L0_attn_setup()
    _L0_attn_in = {k: v for k, v in _L0_attn_all.items() if k in ('w_qkv', 'b_qkv', 'w_out', 'b_out')}
    del _L0_attn_all

    def _L0_xattn_setup():
        import jax, jax.numpy as jnp
        import numpy as np
        BS, SEQ, D_MODEL = (4, 128, 512)
        N_Q_HEADS, N_KV_HEADS, D_K, D_V = (32, 8, 128, 128)
        ROPE_BASE = 10000.0

        def _rotate_half(x):
            x1, x2 = jnp.split(x, 2, axis=-1)
            return jnp.concatenate([-x2, x1], axis=-1)

        def _apply_rope(x, pos0):
            d = x.shape[-1]
            seq = x.shape[2]
            inv_freq = 1.0 / ROPE_BASE ** (jnp.arange(0, d, 2, dtype=jnp.float32) / d)
            pos = (pos0 + jnp.arange(seq)).astype(jnp.float32)
            ang = pos[:, None] * inv_freq[None, :]
            cos = jnp.concatenate([jnp.cos(ang), jnp.cos(ang)], axis=-1)
            sin = jnp.concatenate([jnp.sin(ang), jnp.sin(ang)], axis=-1)
            return x * cos[None, None] + _rotate_half(x) * sin[None, None]
        key = jax.random.key(seed)
        ks = jax.random.split(key, 8)
        w_scale = 0.02
        return {'query': jax.random.normal(ks[0], (BS, SEQ, D_MODEL), dtype=jnp.float32), 'key': jax.random.normal(ks[1], (BS, SEQ, D_MODEL), dtype=jnp.float32), 'value': jax.random.normal(ks[2], (BS, SEQ, D_MODEL), dtype=jnp.float32), 'mask': jnp.zeros((BS, SEQ, SEQ), dtype=jnp.float32), 'wq': jax.random.normal(ks[3], (D_MODEL, N_Q_HEADS * D_K), dtype=jnp.float32) * w_scale, 'wk': jax.random.normal(ks[4], (D_MODEL, N_KV_HEADS * D_K), dtype=jnp.float32) * w_scale, 'wv': jax.random.normal(ks[5], (D_MODEL, N_KV_HEADS * D_V), dtype=jnp.float32) * w_scale, 'wo': jax.random.normal(ks[6], (N_Q_HEADS * D_V, D_MODEL), dtype=jnp.float32) * w_scale, 'curr_seq_pos': 0}
    _L0_xattn_all = _L0_xattn_setup()
    _L0_xattn_in = {k: v for k, v in _L0_xattn_all.items() if k in ('wq', 'wk', 'wv', 'wo')}
    del _L0_xattn_all

    def _L0_ffn_setup():
        import jax, jax.numpy as jnp
        import numpy as np
        HID, INT, LAT, NE, K = (512, 1024, 256, 8, 2)
        LN_EPS = 1e-05

        def _layernorm(x, gamma, beta):
            mu = jnp.mean(x, axis=-1, keepdims=True)
            var = jnp.var(x, axis=-1, keepdims=True)
            return (x - mu) * jax.lax.rsqrt(var + LN_EPS) * gamma + beta
        key = jax.random.key(seed)
        ks = jax.random.split(key, 8)
        s = lambda d: 1.0 / np.sqrt(d)
        return {'hidden_states': jax.random.normal(ks[0], (4, 256, HID), jnp.float32), 'gate_w': jax.random.normal(ks[1], (HID, NE), jnp.float32) * s(HID), 'up_w': jax.random.normal(ks[2], (HID, INT), jnp.float32) * s(HID), 'down_w': jax.random.normal(ks[3], (INT, HID), jnp.float32) * s(INT), 'fc1_w': jax.random.normal(ks[4], (HID, LAT), jnp.float32) * s(HID), 'fc2_w': jax.random.normal(ks[5], (LAT, HID), jnp.float32) * s(LAT), 'expert_w': jax.random.normal(ks[6], (LAT, LAT), jnp.float32), 'ln_gamma': jnp.ones((HID,), jnp.float32), 'ln_beta': jnp.zeros((HID,), jnp.float32)}
    _L0_ffn_all = _L0_ffn_setup()
    _L0_ffn_in = {k: v for k, v in _L0_ffn_all.items() if k in ('gate_w', 'up_w', 'down_w', 'fc1_w', 'fc2_w', 'expert_w', 'ln_gamma', 'ln_beta')}
    del _L0_ffn_all
    return {'x': x, 'ctx_4096': ctx_4096, 'mask_BxSxS2_ff0': mask_BxSxS2_ff0, 'L0_attn_w_qkv': _L0_attn_in['w_qkv'], 'L0_attn_b_qkv': _L0_attn_in['b_qkv'], 'L0_attn_w_out': _L0_attn_in['w_out'], 'L0_attn_b_out': _L0_attn_in['b_out'], 'L0_xattn_wq': _L0_xattn_in['wq'], 'L0_xattn_wk': _L0_xattn_in['wk'], 'L0_xattn_wv': _L0_xattn_in['wv'], 'L0_xattn_wo': _L0_xattn_in['wo'], 'L0_ffn_gate_w': _L0_ffn_in['gate_w'], 'L0_ffn_up_w': _L0_ffn_in['up_w'], 'L0_ffn_down_w': _L0_ffn_in['down_w'], 'L0_ffn_fc1_w': _L0_ffn_in['fc1_w'], 'L0_ffn_fc2_w': _L0_ffn_in['fc2_w'], 'L0_ffn_expert_w': _L0_ffn_in['expert_w'], 'L0_ffn_ln_gamma': _L0_ffn_in['ln_gamma'], 'L0_ffn_ln_beta': _L0_ffn_in['ln_beta']}

def reference(x, ctx_4096, mask_BxSxS2_ff0, L0_attn_w_qkv, L0_attn_b_qkv, L0_attn_w_out, L0_attn_b_out, L0_xattn_wq, L0_xattn_wk, L0_xattn_wv, L0_xattn_wo, L0_ffn_gate_w, L0_ffn_up_w, L0_ffn_down_w, L0_ffn_fc1_w, L0_ffn_fc2_w, L0_ffn_expert_w, L0_ffn_ln_gamma, L0_ffn_ln_beta):
    import jax
    import jax.numpy as jnp

    def _L0_attn_ref(x, w_qkv, b_qkv, w_out, b_out):
        import math
        import jax, jax.numpy as jnp
        import numpy as np
        N_HEADS = 32
        ALIBI_BIAS_MAX = 8

        def _alibi_slopes(n_heads, alibi_bias_max=8):
            _n = 2 ** math.ceil(math.log2(n_heads))
            m = jnp.arange(1, _n + 1, dtype=jnp.float32) * (alibi_bias_max / _n)
            slopes = 1.0 / jnp.power(2.0, m)
            if _n != n_heads:
                slopes = jnp.concatenate([slopes[1::2], slopes[::2]])[:n_heads]
            return slopes
        B, S, D = x.shape
        H = N_HEADS
        hd = D // H
        qkv = jnp.einsum('bsd,od->bso', x, w_qkv) + b_qkv
        q, k, v = jnp.split(qkv, 3, axis=-1)
        q = q.reshape(B, S, H, hd)
        k = k.reshape(B, S, H, hd)
        v = v.reshape(B, S, H, hd)
        scale = 1.0 / math.sqrt(hd)
        scores = jnp.einsum('bqhd,bkhd->bhqk', q, k) * scale
        slopes = _alibi_slopes(H, ALIBI_BIAS_MAX)
        positions = jnp.arange(1 - S, 1, dtype=jnp.float32)
        alibi = slopes[:, None] * positions[None, :]
        scores = scores + alibi[None, :, None, :]
        causal = jnp.arange(S)[:, None] >= jnp.arange(S)[None, :]
        scores = jnp.where(causal[None, None, :, :], scores, jnp.float32(-1000000000.0))
        attn = jax.nn.softmax(scores, axis=-1)
        out = jnp.einsum('bhqk,bkhd->bqhd', attn, v).reshape(B, S, D)
        return jnp.einsum('bsd,od->bso', out, w_out) + b_out

    def _L0_xattn_ref(query, key, value, mask, wq, wk, wv, wo, curr_seq_pos):
        import jax, jax.numpy as jnp
        import numpy as np
        BS, SEQ, D_MODEL = (4, 128, 512)
        N_Q_HEADS, N_KV_HEADS, D_K, D_V = (32, 8, 128, 128)
        ROPE_BASE = 10000.0

        def _rotate_half(x):
            x1, x2 = jnp.split(x, 2, axis=-1)
            return jnp.concatenate([-x2, x1], axis=-1)

        def _apply_rope(x, pos0):
            d = x.shape[-1]
            seq = x.shape[2]
            inv_freq = 1.0 / ROPE_BASE ** (jnp.arange(0, d, 2, dtype=jnp.float32) / d)
            pos = (pos0 + jnp.arange(seq)).astype(jnp.float32)
            ang = pos[:, None] * inv_freq[None, :]
            cos = jnp.concatenate([jnp.cos(ang), jnp.cos(ang)], axis=-1)
            sin = jnp.concatenate([jnp.sin(ang), jnp.sin(ang)], axis=-1)
            return x * cos[None, None] + _rotate_half(x) * sin[None, None]
        bs, sq, _ = query.shape
        n_groups = N_Q_HEADS // N_KV_HEADS
        q = (query @ wq).reshape(bs, sq, N_Q_HEADS, D_K).transpose((0, 2, 1, 3))
        sk = key.shape[1]
        k = (key @ wk).reshape(bs, sk, N_KV_HEADS, 1, D_K)
        k = jnp.repeat(k, n_groups, axis=3).reshape(bs, sk, N_Q_HEADS, D_K).transpose((0, 2, 1, 3))
        v = (value @ wv).reshape(bs, sk, N_KV_HEADS, 1, D_V)
        v = jnp.repeat(v, n_groups, axis=3).reshape(bs, sk, N_Q_HEADS, D_V).transpose((0, 2, 1, 3))
        scale = jnp.sqrt(jnp.float32(D_K))
        q = _apply_rope(q, curr_seq_pos)
        k = _apply_rope(k, curr_seq_pos)
        raw = jnp.einsum('bhqd,bhkd->bhqk', q, k) / scale
        masked = raw + mask[:bs, None, curr_seq_pos:curr_seq_pos + sq, :sk]
        attn = jax.nn.softmax(masked, axis=-1)
        out = jnp.einsum('bhqk,bhkd->bhqd', attn, v)
        out = out.transpose((0, 2, 1, 3)).reshape(bs, sq, N_Q_HEADS * D_V)
        return out @ wo

    def _L0_ffn_ref(hidden_states, gate_w, up_w, down_w, fc1_w, fc2_w, expert_w, ln_gamma, ln_beta):
        import jax, jax.numpy as jnp
        import numpy as np
        HID, INT, LAT, NE, K = (512, 1024, 256, 8, 2)
        LN_EPS = 1e-05

        def _layernorm(x, gamma, beta):
            mu = jnp.mean(x, axis=-1, keepdims=True)
            var = jnp.var(x, axis=-1, keepdims=True)
            return (x - mu) * jax.lax.rsqrt(var + LN_EPS) * gamma + beta
        logits = jnp.einsum('bsh,he->bse', hidden_states, gate_w)
        routing_weights, selected_experts = jax.lax.top_k(logits, K)
        h = jax.nn.relu(jnp.einsum('bsh,hi->bsi', hidden_states, up_w)) ** 2
        shared_out = jnp.einsum('bsi,ih->bsh', h, down_w)
        x_latent = jnp.einsum('bsh,hl->bsl', hidden_states, fc1_w)
        expert_out = jnp.einsum('bsl,lm->bsm', x_latent, expert_w)
        moe_out = expert_out * jnp.sum(routing_weights, axis=-1, keepdims=True)
        routed_out = jnp.einsum('bsl,lh->bsh', moe_out, fc2_w)
        return _layernorm(shared_out + routed_out, ln_gamma, ln_beta)
    x = _layernorm(x + _L0_attn_ref(x, L0_attn_w_qkv, L0_attn_b_qkv, L0_attn_w_out, L0_attn_b_out), axis=-1)
    x = _layernorm(x + _L0_xattn_ref(x, ctx_4096, ctx_4096, mask_BxSxS2_ff0, L0_xattn_wq, L0_xattn_wk, L0_xattn_wv, L0_xattn_wo, 0), axis=-1)
    x = _layernorm(x + _L0_ffn_ref(x, L0_ffn_gate_w, L0_ffn_up_w, L0_ffn_down_w, L0_ffn_fc1_w, L0_ffn_fc2_w, L0_ffn_expert_w, L0_ffn_ln_gamma, L0_ffn_ln_beta), axis=-1)
    return x

_drawn_inputs = setup_inputs


def setup_inputs(seed=0):
    import zlib

    import numpy as np

    out = dict(_drawn_inputs(seed))
    spreads = {'L0_attn_b_qkv': (0.0, 0.1),
     'L0_attn_b_out': (0.0, 0.1),
     'L0_ffn_ln_gamma': (1.0, 0.2),
     'L0_ffn_ln_beta': (0.0, 0.1)}
    factors = {'L0_xattn_wq': 3.12, 'L0_xattn_wk': 3.123}
    for name, (base, spread) in spreads.items():
        noise = np.random.default_rng([zlib.crc32(name.encode()), seed]).standard_normal(out[name].shape)
        drawn = base * np.exp(spread * noise) if base else spread * noise
        out[name] = jnp.asarray(drawn.astype(out[name].dtype))
    for name, factor in factors.items():
        out[name] = (out[name] * factor).astype(out[name].dtype)
    return out
```

```python
from contextlib import ExitStack

import concourse.bass as bass
from concourse import mybir

F32 = mybir.dt.float32
F32R = mybir.dt.float32r
ALU = mybir.AluOpType
ACT = mybir.ActivationFunctionType
AX = mybir.AxisListType

P = 128
B = 8
S = 128
D = 512
C = D // P
NT = B * S
HALF = NT // 2
HS = 32
DH = D // HS
HG = 4
NG = 8
EPS = 1e-5

PASSES = ((0, 0), (0, 1), (1, 0))


def product(eng, out, stationary, moving, first, last):
    for n, (i, j) in enumerate(PASSES):
        mm = eng.matmul(out, stationary[i], moving[j], start=first and n == 0,
                        stop=last and n == len(PASSES) - 1)
    return mm


def layer_norm(eng, z, out, stats, moments, rstd, sems, count):
    s_stats, s_moments, s_var, s_rstd = sems
    eng.bn_stats(stats, z).then_inc(s_stats, 1)
    eng.wait_ge(s_stats, count)
    eng.bn_aggr(moments, stats).then_inc(s_moments, 1)
    eng.wait_ge(s_moments, count)
    eng.tensor_scalar(moments[:, 1:2], moments[:, 1:2], EPS, None, ALU.add).then_inc(s_var, 1)
    eng.wait_ge(s_rstd, count)
    return eng.tensor_scalar(out, z, moments[:, 0:1], rstd, ALU.subtract, ALU.mult)


def inverse_root(eng, moments, rstd, power, sems, count):
    eng.wait_ge(sems[2], count)
    eng.tensor_tensor(rstd, moments[:, 1:2], power, ALU.pow).then_inc(sems[3], 1)


def wait(eng, sem, value):
    if not isinstance(value, int) or value > 0:
        eng.wait_ge(sem, value)


def project_self(nc, xT_d, wqkv_d, bqk_d, bv_d, q, k, vhl):
    RING = 3
    NX = C * 2
    NW = C * 3
    pieces = [("x", c, 0) for c in range(C)] + [("w", c, 0) for c in range(C)] + \
             [("w", c, 1) for c in range(C)] + [("x", c, 1) for c in range(C)] + \
             [("w", c, 2) for c in range(C)]
    at = {p: n for n, p in enumerate(pieces)}
    tiles = [("qk", m, h) for h in range(2) for m in range(2 * C)] + [("v", b, 0) for b in range(B)]
    order = [t for t in tiles if t[0] == "qk" and t[2] == 0] + [t for t in tiles if t[0] == "qk" and t[2] == 1] + \
            [t for t in tiles if t[0] == "v"]
    BANKS = 4
    with ExitStack() as ctx:
        sb = lambda name, shape, dt=F32: ctx.enter_context(nc.sbuf_tensor("A_" + name, shape, dt))
        sem = lambda name: ctx.enter_context(nc.semaphore("A_" + name))
        stage = sb("stage", [P, RING, D])
        xT = [sb("xT" + s, [P, C, NT], F32R) for s in ("h", "l")]
        w = [sb("w" + s, [P, C, 3 * D], F32R) for s in ("h", "l")]
        bqk = sb("bqk", [P, 2 * C])
        bv = sb("bv", [P, D])
        val = sb("val", [P, 2, D])
        acc = [ctx.enter_context(nc.psum_tensor(f"A_acc{i}", [P, D], F32)) for i in range(BANKS)]
        s_piece = [sem(f"piece{i}") for i in range(RING)]
        s_bias, s_hi, s_lo, s_acc = sem("bias"), sem("hi"), sem("lo"), sem("acc")
        s_val, s_vhi, s_vlo = sem("val"), sem("vhi"), sem("vlo")
        block = ctx.enter_context(nc.Block())

        def place(t, piece):
            kind, c, n = piece
            return t[:, c, n * D:(n + 1) * D]

        @block.sync
        def _(eng):
            for n, piece in enumerate(pieces):
                if n >= RING:
                    eng.wait_ge(s_lo, n - RING + 1)
                src = xT_d if piece[0] == "x" else wqkv_d
                eng.dma_start(stage[:, n % RING, :], place(src, piece)).then_inc(s_piece[n % RING], 16)
                if n == 0:
                    eng.dma_start(bqk[:, :], bqk_d).then_inc(s_bias, 16)
                    eng.dma_start(bv[:, :], bv_d).then_inc(s_bias, 16)

        @block.scalar
        def _(eng):
            def piece_hi(n):
                eng.wait_ge(s_piece[n % RING], 16 * (n // RING + 1))
                dst = xT if pieces[n][0] == "x" else w
                eng.activation(place(dst[0], pieces[n]), stage[:, n % RING, :], ACT.Copy).then_inc(s_hi, 1)

            def tile_hi(i):
                kind, m, h = order[i]
                eng.wait_ge(s_val, i + 1)
                src = val[:, i % 2, :]
                if kind == "qk":
                    dst = (q if m < C else k)[0][:, m % C, h * HALF:(h + 1) * HALF]
                else:
                    dst = vhl[:, m, :, 0:DH]
                    src = src.rearrange("p (h d) -> p h d", d=DH)
                eng.activation(dst, src, ACT.Copy).then_inc(s_vhi, 1)

            ahead = 12
            for n in range(ahead):
                piece_hi(n)
            for i in range(len(order)):
                if ahead + i < len(pieces):
                    piece_hi(ahead + i)
                tile_hi(i)

        @block.tensor
        def _(eng):
            for i, (kind, m, h) in enumerate(order):
                out = acc[i % BANKS][:, :]
                if i >= BANKS:
                    eng.wait_ge(s_val, i - BANKS + 1)
                for c in range(C):
                    if kind == "qk":
                        eng.wait_ge(s_lo, max(at["w", c, m // C], at["x", c, h]) + 1)
                        st = [t[:, c, m * P:(m + 1) * P] for t in w]
                        mv = [t[:, c, h * HALF:(h + 1) * HALF] for t in xT]
                    else:
                        eng.wait_ge(s_lo, at["w", c, 2] + 1)
                        st = [t[:, c, m * S:(m + 1) * S] for t in xT]
                        mv = [t[:, c, 2 * D:3 * D] for t in w]
                    mm = product(eng, out, st, mv, c == 0, c == C - 1)
                mm.then_inc(s_acc, 1)

        @block.vector
        def _(eng):
            def piece_lo(n):
                eng.wait_ge(s_hi, n + 1)
                dst = xT if pieces[n][0] == "x" else w
                eng.tensor_tensor(place(dst[1], pieces[n]), stage[:, n % RING, :],
                                  place(dst[0], pieces[n]).bitcast(F32), ALU.subtract).then_inc(s_lo, 1)

            def tile(i):
                kind, m, h = order[i]
                eng.wait_ge(s_acc, i + 1)
                if i >= 2:
                    eng.wait_ge(s_vlo, i - 1)
                out = val[:, i % 2, :]
                if i == 0:
                    eng.wait_ge(s_bias, 32)
                if kind == "v":
                    eng.tensor_tensor(out, acc[i % BANKS][:, :], bv[:, :], ALU.add).then_inc(s_val, 1)
                elif m < C:
                    eng.tensor_scalar(out, acc[i % BANKS][:, :], bqk[:, m:m + 1], DH ** -0.5,
                                      ALU.add, ALU.mult).then_inc(s_val, 1)
                else:
                    eng.tensor_scalar(out, acc[i % BANKS][:, :], bqk[:, m:m + 1], None,
                                      ALU.add).then_inc(s_val, 1)

            ahead = 12
            for n in range(ahead):
                piece_lo(n)
            for i in range(len(order)):
                if ahead + i < len(pieces):
                    piece_lo(ahead + i)
                tile(i)

        @block.gpsimd
        def _(eng):
            for i, (kind, m, h) in enumerate(order):
                eng.wait_ge(s_vhi, i + 1)
                src = val[:, i % 2, :]
                if kind == "qk":
                    t = q if m < C else k
                    hi, lo = (t[j][:, m % C, h * HALF:(h + 1) * HALF] for j in range(2))
                else:
                    src = src.rearrange("p (h d) -> p h d", d=DH)
                    hi, lo = vhl[:, m, :, 0:DH], vhl[:, m, :, DH:2 * DH]
                eng.tensor_tensor(lo, src, hi.bitcast(F32), ALU.subtract).then_inc(s_vlo, 1)


def attend_self(nc, x_d, alibi_d, wout_d, bout_d, ident, q, k, vhl, x1):
    LT, LV = 2, 4
    NS = B * NG
    PAIR = NG // 2
    LOADS = 16 * (2 * 8 + 2)
    with ExitStack() as ctx:
        sb = lambda name, shape, dt=F32: ctx.enter_context(nc.sbuf_tensor("B_" + name, shape, dt))
        pb = lambda name: ctx.enter_context(nc.psum_tensor("B_" + name, [P, D], F32))
        sem = lambda name: ctx.enter_context(nc.semaphore("B_" + name))
        qs = [sb("qs" + s, [P, C, S], F32R) for s in ("h", "l")]
        kd = [sb("kd" + s, [P, C, 8, S], F32R) for s in ("h", "l")]
        alibi = sb("alibi", [P, HS, S])
        wout = [sb("wout" + s, [P, C, D], F32R) for s in ("h", "l")]
        prob = sb("prob", [P, 4, HG * S])
        bout = prob[:, 3, :]
        pT = [sb("pT" + s, [P, 2, HG * S], F32R) for s in ("h", "l")]
        top = sb("top", [P, 2, HG])
        carrier = sb("carrier", [P, 1])
        ntop = sb("ntop", [P, 4, HG])
        total = sb("total", [P, HS])
        rden = sb("rden", [P, HS])
        ohl = sb("ohl", [P, 16, DH])
        o = sb("o", [P, HS, DH])
        oT = [sb("oT" + s, [P, C, S], F32R) for s in ("h", "l")]
        wst = sb("wst", [P, D])
        sc = [pb("sc0"), pb("sc1")]
        tp = [pb("tp0"), pb("tp1")]
        ov = [pb("ov0"), pb("ov1")]
        ot, yb = pb("ot"), pb("yb")
        s_zero, s_x, s_alibi, s_wst, s_bout = sem("zero"), sem("x"), sem("alibi"), sem("wst"), sem("bout")
        s_whi, s_wlo, s_xb = sem("whi"), sem("wlo"), sem("xb")
        s_load = [sem("load0"), sem("load1")]
        s_sc, s_top, s_ntop, s_exp = sem("sc"), sem("top"), sem("ntop"), sem("exp")
        s_tp, s_phi, s_plo, s_pv = sem("tp"), sem("phi"), sem("plo"), sem("pv")
        s_rden, s_ohl, s_oadd, s_o = sem("rden"), sem("ohl"), sem("oadd"), sem("o")
        s_ot, s_ohi, s_olo, s_y, s_z = sem("ot"), sem("ohi"), sem("olo"), sem("y"), sem("z")
        block = ctx.enter_context(nc.Block())

        def live(b, G, lag=0):
            return not isinstance(b, int) or 0 <= NG * b + G - lag < NS

        def follows(b):
            return not isinstance(b, int) or 1 <= b <= B

        def loop(eng, step):
            for G in range(NG):
                step(0, G)
            with eng.Fori(1, B) as b:
                for G in range(NG):
                    step(b, G)
            for G in range(NG):
                step(B, G)

        @block.sync
        def _(eng):
            for c in range(C):
                eng.dma_start(alibi[:, c * 8:(c + 1) * 8, :], alibi_d[:, c * 8:(c + 1) * 8, :]).then_inc(s_alibi, 16)
            eng.dma_start(x1[:, :, :], x_d).then_inc(s_x, 16)
            eng.dma_start(bout, bout_d).then_inc(s_bout, 16)
            for c in range(C):
                if c:
                    eng.wait_ge(s_wlo, c)
                eng.dma_start(wst[:, :], wout_d[:, c, :]).then_inc(s_wst, 16)

            def load(b, pair):
                cs = slice(2 * pair, 2 * pair + 2)
                if not isinstance(b, int):
                    eng.wait_ge(s_sc, NG * (b - 1) + PAIR * (pair + 1))
                for j in range(2):
                    eng.dma_start(qs[j][:, cs, :].bitcast(F32), q[j][:, cs, bass.ts(b, S)].bitcast(F32)).then_inc(s_load[pair], 16)
                    for r in range(8):
                        rows = slice(r * DH, (r + 1) * DH)
                        eng.dma_start(kd[j][rows, cs, r, :].bitcast(F32),
                                      k[j][rows, cs, bass.ts(b, S)].bitcast(F32)).then_inc(s_load[pair], 16)

            eng.wait_ge(s_zero, 2)
            for pair in range(2):
                load(0, pair)
            with eng.Fori(1, B) as b:
                for pair in range(2):
                    load(b, pair)

        @block.gpsimd
        def _(eng):
            eng.wait_ge(s_x, 16)
            eng.wait_ge(s_bout, 16)
            eng.tensor_tensor(x1[:, :, :], x1[:, :, :], bout.unsqueeze(1).broadcast_to([P, B, D]),
                              ALU.add).then_inc(s_xb, 1)

        @block.scalar
        def _(eng):
            def step(b, G):
                n = NG * b + G
                if G == 6 and follows(b):
                    eng.wait_ge(s_ot, b)
                    wait(eng, s_y, b - 1)
                    eng.activation(oT[0][:, :, :], ot[:, :].rearrange("p (c s) -> p c s", c=C),
                                   ACT.Copy).then_inc(s_ohi, 1)
                if live(b, G, LT):
                    eng.wait_ge(s_tp, n - LT + 1)
                    wait(eng, s_pv, n - LT - 1)
                    eng.activation(pT[0][:, G % 2, :], tp[G % 2][:, :], ACT.Copy).then_inc(s_phi, 1)
                if live(b, G):
                    eng.wait_ge(s_ntop, n + 1)
                    if G % 4 == 0:
                        wait(eng, s_rden, 2 * b - 1 + G // 4)
                    for h in range(HG):
                        e = prob[:, G % 4, h * S:(h + 1) * S]
                        last = eng.activation(e, e, ACT.Exp, bias=ntop[:, G % 4, h:h + 1], scale=1.0,
                                              accum_out=total[:, HG * G + h:HG * G + h + 1])
                    last.then_inc(s_exp, 1)
                if G in (0, 4) and follows(b):
                    eng.wait_ge(s_pv, n - LV)
                    wait(eng, s_oadd, 2 * b - 2 + G // 4)
                    eng.activation(ohl[:, :, :],
                                   ov[G // 4][:, :].rearrange("p (h t d) -> p h t d", t=2, d=DH)[:, :, 1, :],
                                   ACT.Copy).then_inc(s_ohl, 1)

            for c in range(C):
                eng.wait_ge(s_wst, 16 * (c + 1))
                eng.activation(wout[0][:, c, :], wst[:, :], ACT.Copy).then_inc(s_whi, 1)
            loop(eng, step)

        @block.tensor
        def _(eng):
            def step(b, G):
                n = NG * b + G
                if live(b, G):
                    if G % PAIR == 0:
                        eng.wait_ge(s_load[G // PAIR], LOADS * (b + 1))
                    wait(eng, s_top, n - 1)
                    c, cols = G // 2, slice(4 * (G % 2), 4 * (G % 2) + 4)
                    product(eng, sc[G % 2][:, :].rearrange("p (h s) -> p h s", h=HG), [t[:, c, :] for t in qs],
                            [t[:, c, cols, :] for t in kd], True, True).then_inc(s_sc, 1)
                if live(b, G, LV):
                    g, bb = (G - LV) % NG, b if G >= LV else b - 1
                    m = n - LV
                    eng.wait_ge(s_phi, m + 1)
                    eng.wait_ge(s_plo, m + 1)
                    if g % 4 == 0:
                        wait(eng, s_oadd, 2 * bb - 1 + g // 4)
                    for h in range(HG):
                        head = HG * g + h
                        at = (head % 16) * 2 * DH
                        out = ov[g // 4]
                        v = vhl[:, bass.ds(bb, 1), head, :].rearrange("p a d -> p (a d)")
                        eng.matmul(out[:, at:at + 2 * DH], pT[0][:, G % 2, h * S:(h + 1) * S], v,
                                   start=True, stop=False)
                        mm = eng.matmul(out[:, at:at + DH], pT[1][:, G % 2, h * S:(h + 1) * S], v[:, 0:DH],
                                        start=False, stop=True)
                    mm.then_inc(s_pv, 1)
                if live(b, G, LT):
                    m = n - LT
                    eng.wait_ge(s_exp, m + 1)
                    wait(eng, s_phi, m - 1)
                    wait(eng, s_plo, m - 1)
                    for h in range(HG):
                        mm = eng.transpose(tp[G % 2][:, h * S:(h + 1) * S],
                                           prob[:, (G - LT) % 4, h * S:(h + 1) * S], ident)
                    mm.then_inc(s_tp, 1)
                if G == 5 and follows(b):
                    eng.wait_ge(s_o, 2 * b)
                    wait(eng, s_olo, b - 1)
                    for c in range(C):
                        mm = eng.transpose(ot[:, c * P:(c + 1) * P],
                                           o[:, 8 * c:8 * c + 8, :].rearrange("p h d -> p (h d)"), ident)
                    mm.then_inc(s_ot, 1)
                if G == 6 and follows(b):
                    eng.wait_ge(s_ohi, b)
                    eng.wait_ge(s_olo, b)
                    wait(eng, s_z, b - 1)
                    for c in range(C):
                        mm = product(eng, yb[:, :], [t[:, c, :] for t in oT], [t[:, c, :] for t in wout],
                                     c == 0, c == C - 1)
                    mm.then_inc(s_y, 1)

            eng.wait_ge(s_wlo, C)
            loop(eng, step)

        @block.vector
        def _(eng):
            def step(b, G):
                n = NG * b + G
                if live(b, G):
                    eng.wait_ge(s_sc, n + 1)
                    wait(eng, s_tp, n - 3)
                    eng.memset(carrier[:, :], 0.0)
                    for h in range(HG):
                        last = eng.tensor_tensor_reduce(
                            prob[:, G % 4, h * S:(h + 1) * S], sc[G % 2][:, h * S:(h + 1) * S],
                            alibi[:, HG * G + h, :], 1.0, -3e38, ALU.add, ALU.max, top[:, G % 2, h:h + 1])
                    last.then_inc(s_top, 1)
                    eng.wait_ge(s_top, n + 1)
                    wait(eng, s_exp, n - 3)
                    eng.tensor_scalar(ntop[:, G % 4, :], top[:, G % 2, :], -1.0, None, ALU.mult).then_inc(s_ntop, 1)
                if G == 6 and follows(b):
                    eng.wait_ge(s_ohi, b)
                    eng.tensor_tensor(oT[1][:, :, :], ot[:, :].rearrange("p (c s) -> p c s", c=C),
                                      oT[0][:, :, :].bitcast(F32), ALU.subtract).then_inc(s_olo, 1)
                if live(b, G, LT):
                    m = n - LT
                    eng.wait_ge(s_phi, m + 1)
                    eng.tensor_tensor(pT[1][:, G % 2, :], tp[G % 2][:, :], pT[0][:, G % 2, :].bitcast(F32),
                                      ALU.subtract).then_inc(s_plo, 1)
                if G in (0, 4) and live(b, G, 1):
                    half = 1 - G // 4
                    eng.wait_ge(s_exp, n)
                    eng.reciprocal(rden[:, 16 * half:16 * half + 16],
                                   total[:, 16 * half:16 * half + 16]).then_inc(s_rden, 1)
                if G in (0, 4) and follows(b):
                    half, done = G // 4, 2 * b - 1 + G // 4
                    heads = slice(16 * half, 16 * half + 16)
                    eng.wait_ge(s_ohl, done)
                    wait(eng, s_ot, b - 1)
                    eng.tensor_tensor(o[:, heads, :],
                                      ov[half][:, :].rearrange("p (h t d) -> p h t d", t=2, d=DH)[:, :, 0, :],
                                      ohl[:, :, :], ALU.add).then_inc(s_oadd, 1)
                    eng.wait_ge(s_oadd, done)
                    eng.wait_ge(s_rden, done)
                    eng.tensor_tensor(o[:, heads, :], o[:, heads, :],
                                      rden[:, heads].unsqueeze(2).broadcast_to([P, 16, DH]),
                                      ALU.mult).then_inc(s_o, 1)
                if G == 7 and follows(b):
                    eng.wait_ge(s_y, b)
                    row = x1[:, bass.ds(b - 1, 1), :].rearrange("p a d -> p (a d)")
                    eng.tensor_tensor(row, yb[:, :], row, ALU.add).then_inc(s_z, 1)

            for j in range(2):
                eng.memset(kd[j][:, :, :, :].bitcast(F32), 0.0).then_inc(s_zero, 1)
            for c in range(C):
                eng.wait_ge(s_whi, c + 1)
                eng.tensor_tensor(wout[1][:, c, :], wst[:, :], wout[0][:, c, :].bitcast(F32),
                                  ALU.subtract).then_inc(s_wlo, 1)
            eng.wait_ge(s_alibi, 16 * C)
            eng.wait_ge(s_xb, 1)
            loop(eng, step)


def turn(nc, name, x_nat, xT, ident, power):
    with ExitStack() as ctx:
        sb = lambda s, shape: ctx.enter_context(nc.sbuf_tensor(f"{name}_{s}", shape, F32))
        sem = lambda s: ctx.enter_context(nc.semaphore(f"{name}_{s}"))
        tp = [ctx.enter_context(nc.psum_tensor(f"{name}_tp{i}", [P, D], F32)) for i in range(4)]
        stats, moments, rstd = sb("stats", [P, 6]), sb("moments", [P, 2]), sb("rstd", [P, 1])
        s_ln, s_tp, s_hi, s_lo = sem("ln"), sem("tp"), sem("hi"), sem("lo")
        ln_sems = (sem("stats"), sem("moments"), sem("var"), sem("rstd"))
        chunks = lambda t: t.rearrange("p (c s) -> p c s", c=C)
        block = ctx.enter_context(nc.Block())

        @block.tensor
        def _(eng):
            for b in range(B):
                eng.wait_ge(s_ln, b + 1)
                wait(eng, s_lo, b - 3)
                for c in range(C):
                    mm = eng.transpose(tp[b % 4][:, c * S:(c + 1) * S], x_nat[:, b, c * P:(c + 1) * P], ident)
                mm.then_inc(s_tp, 1)

        @block.scalar
        def _(eng):
            for b in range(B):
                eng.wait_ge(s_tp, b + 1)
                eng.activation(xT[0][:, :, b * S:(b + 1) * S], chunks(tp[b % 4][:, :]), ACT.Copy).then_inc(s_hi, 1)

        @block.vector
        def _(eng):
            def lo(b):
                eng.wait_ge(s_hi, b + 1)
                tok = slice(b * S, (b + 1) * S)
                eng.tensor_tensor(xT[1][:, :, tok], chunks(tp[b % 4][:, :]), xT[0][:, :, tok].bitcast(F32),
                                  ALU.subtract).then_inc(s_lo, 1)

            for b in range(B + 1):
                if b < B:
                    row = x_nat[:, b, :]
                    layer_norm(eng, row, row, stats[:, :], moments[:, :], rstd[:, :], ln_sems, b + 1).then_inc(s_ln, 1)
                if b:
                    lo(b - 1)

        @block.gpsimd
        def _(eng):
            for b in range(B):
                inverse_root(eng, moments[:, :], rstd[:, :], power, ln_sems, b + 1)


def attend_cross(nc, ctxT_d, wq_d, wk_d, wv_d, wo_d, mask_d, trig_d, ident, xT, y):
    G, Q = NG, HG
    NS = G * B
    RING = 5
    STEPS = {0: (0, 1), 1: (2,), 2: (3, 4), 3: (5,)}
    K, V, TILES = 4, 5, 6
    PER = 10
    with ExitStack() as ctx:
        sb = lambda name, shape, dt=F32: ctx.enter_context(nc.sbuf_tensor("C_" + name, shape, dt))
        pb = lambda name: ctx.enter_context(nc.psum_tensor("C_" + name, [P, D], F32))
        sem = lambda name: ctx.enter_context(nc.semaphore("C_" + name))
        pair = lambda name, shape: [sb(name + s, shape, F32R) for s in ("h", "l")]
        cT = pair("cT", [P, C, NT])
        q = pair("q", [P, Q, NT])
        k = pair("k", [P, NT])
        v = pair("v", [P, B, P])
        w = pair("w", [P, TILES, D])
        wo = pair("wo", [P, Q, D])
        stage = sb("stage", [P, RING, D])
        o = pair("o", [P, Q * S])
        pT = pair("pT", [P, Q * S])
        prob = sb("prob", [P, 2, Q * S])
        t1 = sb("t1", [P, 2, D])
        t2 = sb("t2", [P, D])
        trig = sb("trig", [P, 4, S])
        mask = sb("mask", [P, B, S])
        carrier = sb("carrier", [P, 1])
        top, ntop = sb("top", [P, 2, Q]), sb("ntop", [P, 2, Q])
        total, rden = sb("total", [P, 2, Q]), sb("rden", [P, 2, Q])
        sc = [pb("sc0"), pb("sc1")]
        tp, ov, yb, vp = pb("tp"), pb("ov"), pb("yb"), pb("vp")
        pj = [pb("pj0"), pb("pj1")]
        s_const = sem("const")
        s_piece = [sem(f"piece{i}") for i in range(RING)]
        s_whi, s_wlo, s_wolo = sem("whi"), sem("wlo"), sem("wolo")
        s_chi, s_clo = sem("chi"), sem("clo")
        s_pj, s_cos, s_sin, s_sum, s_qhi, s_qlo = sem("pj"), sem("cos"), sem("sin"), sem("sum"), sem("qhi"), sem("qlo")
        s_vt, s_vp, s_vhi, s_vlo = sem("vt"), sem("vp"), sem("vhi"), sem("vlo")
        s_sc, s_top, s_ntop, s_exp, s_rden, s_norm = sem("sc"), sem("top"), sem("ntop"), sem("exp"), sem("rden"), sem("norm")
        s_tp, s_phi, s_plo, s_pv, s_ohi, s_olo = sem("tp"), sem("phi"), sem("plo"), sem("pv"), sem("ohi"), sem("olo")
        s_y, s_add = sem("y"), sem("add")
        NX = 2 * C
        FIRST = NX + TILES
        vt = t2
        block = ctx.enter_context(nc.Block())

        def live(g, s, lag=0):
            return not isinstance(g, int) or 0 <= B * g + s - lag < NS

        def loop(eng, step):
            for s in range(B):
                step(0, s)
            with eng.Fori(1, G - 1) as g:
                for s in range(B):
                    step(g, s)
            for g in (G - 1, G):
                for s in range(B):
                    step(g, s)

        def projects(g, s):
            return not isinstance(g, int) or g < G - 1 or (g == G - 1 and s < 4)

        def half_cycle(g, s):
            return 2 * g + 1 + s // 4

        def where(H_half, j):
            cols = slice(H_half * HALF, (H_half + 1) * HALF)
            return [t[:, j, cols] for t in q] if j < K else [t[:, cols] for t in k]

        def lo_of(g, j):
            return TILES * g + j + 1

        SPLITS = {1: [("wo", h) for h in range(Q)], 2: [("w", 0), ("w", 1)], 3: [("w", 2), ("w", 3)],
                  4: [("w", K)], 5: [("w", V)]}

        def splits(g, s):
            return [x for x in SPLITS.get(s, ()) if not isinstance(g, int) or g < G - 1 or (g == G - 1 and x[0] == "wo")]

        def slot(what):
            kind, j = what
            return (FIRST + (j if kind == "wo" else Q + j)) % RING

        def landed(eng, g, what):
            kind, j = what
            at = FIRST + (j if kind == "wo" else Q + j)
            eng.wait_ge(s_piece[at % RING], 16 * (at // RING + 1 + (PER // RING) * g))

        @block.sync
        def _(eng):
            for n in range(FIRST):
                wait(eng, s_clo if n - RING < NX else s_wlo, n - RING + 1 if n - RING < NX else n - RING - NX + 1)
                src = ctxT_d[:, n // 2, n % 2 * HALF:(n % 2 + 1) * HALF] if n < NX else \
                    (wq_d[0, :, n - NX, :] if n < NX + K else (wk_d if n == NX + K else wv_d)[0])
                eng.dma_start(stage[:, n % RING, :], src).then_inc(s_piece[n % RING], 16)
                if n == 0:
                    eng.dma_start(trig[:, :, :], trig_d).then_inc(s_const, 16)
                    eng.dma_start(mask[:, :, :], mask_d).then_inc(s_const, 16)

            def cycle(g, last=False):
                for j in range(Q if last else PER):
                    what = ("wo", j) if j < Q else ("w", j - Q)
                    if j < RING:
                        eng.wait_ge(s_wlo, lo_of(g, j + 1))
                    elif j < PER - 1:
                        eng.wait_ge(s_wolo, Q * g + j - RING + 1)
                    else:
                        eng.wait_ge(s_wlo, lo_of(g + 1, 0))
                    src = wo_d[bass.ds(g, 1), :, j, :] if j < Q else \
                        wq_d[bass.ds(g + 1, 1), :, j - Q, :] if j < Q + K else (wk_d if j == Q + K else wv_d)[bass.ds(g + 1, 1)]
                    eng.dma_start(stage[:, slot(what), :], src.rearrange("a p n -> (a p) n")).then_inc(s_piece[slot(what)], 16)

            cycle(0)
            with eng.Fori(1, G - 1) as g:
                cycle(g)
            cycle(G - 1, last=True)

        def split_target(what):
            kind, j = what
            return [t[:, j, :] for t in (wo if kind == "wo" else w)]

        @block.scalar
        def _(eng):
            def tile_hi(H, half, j):
                r = 5 * H + j
                eng.wait_ge(s_sum, r + 1)
                eng.activation(where(half, j)[0], t1[:, j % 2, :], ACT.Copy).then_inc(s_qhi, 1)

            def value_out(H):
                eng.wait_ge(s_pj, TILES * H + V + 1)
                eng.wait_ge(s_sum, 5 * H + 5)
                eng.activation(vt[:, :], pj[V % 2][:, :], ACT.Copy).then_inc(s_vt, 1)

            def value_hi(H, half):
                eng.wait_ge(s_vp, H + 1)
                eng.activation(v[0][:, 4 * half:4 * half + 4, :], vp[:, :].rearrange("p (b d) -> p b d", b=4),
                               ACT.Copy).then_inc(s_vhi, 1)

            def step(g, s):
                n = B * g + s
                H = half_cycle(g, s)
                u, half = s % 4, 1 - s // 4
                if live(g, s, 1):
                    eng.wait_ge(s_tp, n)
                    wait(eng, s_pv, n - 1)
                    eng.activation(pT[0][:, :], tp[:, :], ACT.Copy).then_inc(s_phi, 1)
                if u == 0 and live(g, s):
                    value_hi(H - 1, 1 - half)
                if live(g, s):
                    eng.wait_ge(s_ntop, n + 1)
                    wait(eng, s_rden, n - 1)
                    for h in range(Q):
                        e = prob[:, s % 2, h * S:(h + 1) * S]
                        last = eng.activation(e, e, ACT.Exp, bias=ntop[:, s % 2, h:h + 1], scale=1.0,
                                              accum_out=total[:, s % 2, h:h + 1])
                    last.then_inc(s_exp, 1)
                if live(g, s, 1):
                    eng.wait_ge(s_pv, n)
                    wait(eng, s_y, n - 1)
                    eng.activation(o[0][:, :], ov[:, :], ACT.Copy).then_inc(s_ohi, 1)
                if projects(g, s):
                    for j in STEPS.get(u - 1, ()):
                        if j < V:
                            tile_hi(H, half, j)
                for what in splits(g, s):
                    landed(eng, g, what)
                    if what[0] == "wo":
                        wait(eng, s_y, B * g)
                    else:
                        eng.wait_ge(s_pj, TILES * (2 * g + 1) + what[1] + 1)
                    eng.activation(split_target(what)[0], stage[:, slot(what), :], ACT.Copy).then_inc(s_whi, 1)
                if projects(g, s) and u == 3:
                    value_out(H)

            for n in range(NX):
                eng.wait_ge(s_piece[n % RING], 16 * (n // RING + 1))
                eng.activation(cT[0][:, n // 2, n % 2 * HALF:(n % 2 + 1) * HALF], stage[:, n % RING, :],
                               ACT.Copy).then_inc(s_chi, 1)
            for j in range(TILES):
                n = NX + j
                eng.wait_ge(s_piece[n % RING], 16 * (n // RING + 1))
                eng.activation(w[0][:, j, :], stage[:, n % RING, :], ACT.Copy).then_inc(s_whi, 1)
            for j in range(V):
                tile_hi(0, 0, j)
            value_out(0)
            loop(eng, step)

        @block.tensor
        def _(eng):
            def project(H, g, half, j):
                i = TILES * H + j
                eng.wait_ge(s_whi, PER * g + j + 1)
                eng.wait_ge(s_wlo, lo_of(g, j))
                if j == 0:
                    wait(eng, s_sin, 5 * H)
                elif j == 1:
                    wait(eng, s_vt, H)
                else:
                    eng.wait_ge(s_sin, 5 * H + j - 1)
                cols = slice(half * HALF, (half + 1) * HALF)
                for c in range(C):
                    mm = product(eng, pj[j % 2][:, :], [t[:, j, c * P:(c + 1) * P] for t in w],
                                 [t[:, c, cols] for t in (xT if j < K else cT)], c == 0, c == C - 1)
                mm.then_inc(s_pj, 1)

            def turn_values(H):
                eng.wait_ge(s_vt, H + 1)
                wait(eng, s_vlo, H)
                for t in range(4):
                    mm = eng.transpose(vp[:, t * P:(t + 1) * P], vt[:, t * S:(t + 1) * S], ident)
                mm.then_inc(s_vp, 1)

            def step(g, s):
                n = B * g + s
                H = half_cycle(g, s)
                u, half = s % 4, 1 - s // 4
                if live(g, s):
                    if u == 0:
                        eng.wait_ge(s_qlo, 5 * H)
                    wait(eng, s_top, n - 1)
                    tok = slice(s * S, (s + 1) * S)
                    for h in range(Q):
                        mm = product(eng, sc[s % 2][:, h * S:(h + 1) * S], [t[:, h, tok] for t in q],
                                     [t[:, tok] for t in k], True, True)
                    mm.then_inc(s_sc, 1)
                if live(g, s, 1):
                    eng.wait_ge(s_norm, n)
                    wait(eng, s_plo, n - 1)
                    for h in range(Q):
                        mm = eng.transpose(tp[:, h * S:(h + 1) * S], prob[:, (s - 1) % 2, h * S:(h + 1) * S], ident)
                    mm.then_inc(s_tp, 1)
                if u == 0 and live(g, s):
                    turn_values(H - 1)
                if live(g, s, 2):
                    m = n - 2
                    eng.wait_ge(s_ohi, m + 1)
                    eng.wait_ge(s_olo, m + 1)
                    wait(eng, s_add, m)
                    if s == 2:
                        eng.wait_ge(s_wolo, Q * (g + 1))
                    for h in range(Q):
                        mm = product(eng, yb[:, :], [t[:, h * S:(h + 1) * S] for t in o],
                                     [t[:, h, :] for t in wo], h == 0, h == Q - 1)
                    mm.then_inc(s_y, 1)
                if live(g, s, 1):
                    m = n - 1
                    eng.wait_ge(s_phi, m + 1)
                    eng.wait_ge(s_plo, m + 1)
                    wait(eng, s_olo, m)
                    if (s - 1) % 4 == 0:
                        eng.wait_ge(s_vlo, 2 * g + 1 + s // 4)
                    mm = product(eng, ov[:, :], [t[:, (s - 1) % B, :] for t in v], [t[:, :] for t in pT], True, True)
                    mm.then_inc(s_pv, 1)
                if projects(g, s):
                    for j in STEPS[u]:
                        project(H, g + s // 4, half, j)

            eng.wait_ge(s_clo, NX)
            for j in range(TILES):
                project(0, 0, 0, j)
            loop(eng, step)

        @block.vector
        def _(eng):
            def rotate(H, j):
                r = 5 * H + j
                bank = pj[j % 2]
                cos, sin = (trig[:, 2 * (j == K) + i, :].unsqueeze(1).broadcast_to([P, 4, S]) for i in range(2))
                split = lambda t: t.rearrange("p (b s) -> p b s", b=4)
                eng.wait_ge(s_pj, TILES * H + j + 1)
                wait(eng, s_qlo, r if j == 0 else r - 2 if j == 1 else r - 1)
                eng.tensor_tensor(split(t1[:, j % 2, :]), split(bank[:, :]), cos, ALU.mult).then_inc(s_cos, 1)
                wait(eng, s_sum, r)
                if j == 0:
                    wait(eng, s_vp, H)
                eng.tensor_tensor(split(t2[0:64, :]), split(bank[64:128, :]), sin[0:64], ALU.mult)
                eng.tensor_tensor(split(t2[64:128, :]), split(bank[0:64, :]), sin[64:128], ALU.mult).then_inc(s_sin, 1)

            def step(g, s):
                n = B * g + s
                H = half_cycle(g, s)
                u, half = s % 4, 1 - s // 4
                if live(g, s):
                    eng.wait_ge(s_sc, n + 1)
                    wait(eng, s_tp, n - 1)
                    eng.memset(carrier[:, :], 0.0)
                    for h in range(Q):
                        last = eng.tensor_tensor_reduce(
                            prob[:, s % 2, h * S:(h + 1) * S], sc[s % 2][:, h * S:(h + 1) * S], mask[:, s, :],
                            1.0, -3.4e38, ALU.add, ALU.max, top[:, s % 2, h:h + 1])
                    last.then_inc(s_top, 1)
                    eng.wait_ge(s_top, n + 1)
                    wait(eng, s_exp, n - 1)
                    eng.tensor_scalar(ntop[:, s % 2, :], top[:, s % 2, :], -1.0, None, ALU.mult).then_inc(s_ntop, 1)
                if live(g, s, 1):
                    eng.wait_ge(s_phi, n)
                    eng.tensor_tensor(pT[1][:, :], tp[:, :], pT[0][:, :].bitcast(F32), ALU.subtract).then_inc(s_plo, 1)
                if u == 0 and live(g, s):
                    eng.wait_ge(s_vhi, H)
                    vs = [t[:, 4 * (1 - half):4 * (1 - half) + 4, :] for t in v]
                    eng.tensor_tensor(vs[1], vp[:, :].rearrange("p (b d) -> p b d", b=4), vs[0].bitcast(F32),
                                      ALU.subtract).then_inc(s_vlo, 1)
                if live(g, s):
                    eng.wait_ge(s_exp, n + 1)
                    wait(eng, s_norm, n - 1)
                    eng.reciprocal(rden[:, s % 2, :], total[:, s % 2, :]).then_inc(s_rden, 1)
                if live(g, s, 2):
                    m = n - 2
                    b = (s - 2) % B
                    eng.wait_ge(s_y, m + 1)
                    eng.tensor_tensor(y[:, b, :], yb[:, :], y[:, b, :], ALU.add).then_inc(s_add, 1)
                if live(g, s, 1):
                    eng.wait_ge(s_ohi, n)
                    eng.tensor_tensor(o[1][:, :], ov[:, :], o[0][:, :].bitcast(F32), ALU.subtract).then_inc(s_olo, 1)
                for what in splits(g, s):
                    if what[0] == "wo":
                        eng.wait_ge(s_whi, TILES + PER * g + what[1] + 1)
                        hi, lo = split_target(what)
                        eng.tensor_tensor(lo, stage[:, slot(what), :], hi.bitcast(F32), ALU.subtract).then_inc(s_wolo, 1)
                if projects(g, s):
                    for j in STEPS[u]:
                        if j < V:
                            rotate(H, j)

            for n in range(NX):
                eng.wait_ge(s_chi, n + 1)
                hi, lo = (t[:, n // 2, n % 2 * HALF:(n % 2 + 1) * HALF] for t in cT)
                eng.tensor_tensor(lo, stage[:, n % RING, :], hi.bitcast(F32), ALU.subtract).then_inc(s_clo, 1)
            eng.wait_ge(s_const, 32)
            for j in range(V):
                rotate(0, j)
            loop(eng, step)

        @block.gpsimd
        def _(eng):
            def tile_sum(H, j):
                r = 5 * H + j
                eng.wait_ge(s_cos, r + 1)
                eng.wait_ge(s_sin, r + 1)
                eng.tensor_tensor(t1[:, j % 2, :], t1[:, j % 2, :], t2[:, :], ALU.add).then_inc(s_sum, 1)

            def tile_lo(H, half, j):
                eng.wait_ge(s_qhi, 5 * H + j + 1)
                hi, lo = where(half, j)
                eng.tensor_tensor(lo, t1[:, j % 2, :], hi.bitcast(F32), ALU.subtract).then_inc(s_qlo, 1)

            def step(g, s):
                n = B * g + s
                H = half_cycle(g, s)
                u, half = s % 4, 1 - s // 4
                if live(g, s):
                    eng.wait_ge(s_rden, n + 1)
                    e = prob[:, s % 2, :].rearrange("p (h s) -> p h s", h=Q)
                    eng.tensor_tensor(e, e, rden[:, s % 2, :].unsqueeze(2).broadcast_to([P, Q, S]),
                                      ALU.mult).then_inc(s_norm, 1)
                if projects(g, s):
                    for j in STEPS.get(u - 1, ()):
                        if j < V:
                            tile_lo(H, half, j)
                for what in splits(g, s):
                    if what[0] == "w":
                        eng.wait_ge(s_whi, TILES + PER * g + Q + what[1] + 1)
                        hi, lo = split_target(what)
                        eng.tensor_tensor(lo, stage[:, slot(what), :], hi.bitcast(F32), ALU.subtract).then_inc(s_wlo, 1)
                if projects(g, s):
                    for j in STEPS[u]:
                        if j < V:
                            tile_sum(H, j)

            for j in range(TILES):
                eng.wait_ge(s_whi, j + 1)
                eng.tensor_tensor(w[1][:, j, :], stage[:, (NX + j) % RING, :], w[0][:, j, :].bitcast(F32),
                                  ALU.subtract).then_inc(s_wlo, 1)
            for j in range(V):
                tile_sum(0, j)
                tile_lo(0, 0, j)
            loop(eng, step)


def feed_forward(nc, up_d, down_d, fc1_d, fc2_d, expT_d, gate_d, gamma_d, beta_d, power, xT, x2, out_d):
    M = 8
    L = 2
    E = 8
    RING = 4
    pieces = [("exp", 0), ("fc2", 0), ("fc2", 1)] + [("up", c) for c in range(2 * C)] + \
             [("fc1", c) for c in range(2)] + [("down", m) for m in range(M)]
    at = {p: n for n, p in enumerate(pieces)}
    MT = M + L
    BANKS = 3
    with ExitStack() as ctx:
        sb = lambda name, shape, dt=F32: ctx.enter_context(nc.sbuf_tensor("D_" + name, shape, dt))
        pb = lambda name: ctx.enter_context(nc.psum_tensor("D_" + name, [P, D], F32))
        sem = lambda name: ctx.enter_context(nc.semaphore("D_" + name))
        pair = lambda name, shape: [sb(name + s, shape, F32R) for s in ("h", "l")]
        stage = sb("stage", [P, RING, D])
        wexp, wfc2 = pair("exp", [P, 1, D]), pair("fc2", [P, L, D])
        wup = pair("up", [P, 2 * C, D])
        wfc1 = pair("fc1", [P, 2, D])
        wdown = pair("down", [P, M, D])
        wlat = pair("lat", [P, L, D])
        gate = sb("gate", [P, C * E])
        ghl = sb("ghl", [P, C, 2 * E], F32R)
        hT = pair("hT", [P, MT, HALF])
        pos = sb("pos", [P, 2, D])
        sq = sb("sq", [P, 2, D])
        gamma, beta = sb("gamma", [P, D]), sb("beta", [P, D])
        shared = sb("shared", [P, D])
        glo, logit = sb("glo", [P, E]), sb("logit", [P, E])
        best, route = sb("best", [P, E]), sb("route", [P, 1])
        z = sb("z", [P, 2, D])
        stats, moments, rstd = sb("stats", [P, 6]), sb("moments", [P, 2]), sb("rstd", [P, 1])
        acc = [pb(f"acc{i}") for i in range(BANKS)]
        dn = [pb("dn0"), pb("dn1")]
        rt, gt = pb("rt"), pb("gt")
        s_piece = [sem(f"piece{i}") for i in range(RING)]
        s_small = sem("small")
        s_hi, s_lo, s_ghi, s_glo = sem("hi"), sem("lo"), sem("ghi"), sem("glo")
        s_acc, s_pos, s_sq, s_thi, s_tlo = sem("acc"), sem("pos"), sem("sq"), sem("thi"), sem("tlo")
        s_gt, s_gcopy, s_logit, s_best, s_route = sem("gt"), sem("gcopy"), sem("logit"), sem("best"), sem("route")
        s_dn, s_shared, s_z, s_ln1, s_gamma, s_beta, s_res, s_ln2 = (
            sem(n) for n in ("dn", "shared", "z", "ln1", "gamma", "beta", "res", "ln2"))
        s_out = sem("out")
        ln_sems = (sem("stats"), sem("moments"), sem("var"), sem("rstd"))
        block = ctx.enter_context(nc.Block())
        target = {"exp": wexp, "fc2": wfc2, "up": wup, "fc1": wfc1, "down": wdown}
        source = {"exp": expT_d, "fc2": fc2_d, "up": up_d, "fc1": fc1_d, "down": down_d}

        tiles = [("lat", l, 0) for l in range(L)] + [(kind, m, h) for h in range(2)
                 for kind, m in [("up", m) for m in range(M)] + [("fc1", l) for l in range(L)]]
        number = {t: i for i, t in enumerate(tiles)}
        plain = [i for i, t in enumerate(tiles) if t[0] != "up"]

        def dest(t):
            kind, m, h = t
            return [x[:, m, :] for x in wlat] if kind == "lat" else \
                [x[:, m if kind == "up" else M + m, :] for x in hT]

        def rank(i):
            return sum(t[0] == "up" for t in tiles[:i + 1])

        def seq_after(h):
            return 4 * h

        @block.sync
        def _(eng):
            for n, (kind, j) in enumerate(pieces):
                wait(eng, s_lo, n - RING + 1)
                eng.dma_start(stage[:, n % RING, :], source[kind][:, j, :]).then_inc(s_piece[n % RING], 16)
                if n == 0:
                    for t, d in ((gate, gate_d), (gamma, gamma_d), (beta, beta_d)):
                        eng.dma_start(t[:, :], d).then_inc(s_small, 16)
            for b in range(B):
                eng.wait_ge(s_ln2, b + 1)
                eng.dma_start(out_d[b], x2[:, b, :]).then_inc(s_out, 16)
            eng.wait_ge(s_out, 16 * B)

        @block.scalar
        def _(eng):
            def piece_hi(n):
                kind, j = pieces[n]
                eng.wait_ge(s_piece[n % RING], 16 * (n // RING + 1))
                eng.activation(target[kind][0][:, j, :], stage[:, n % RING, :], ACT.Copy).then_inc(s_hi, 1)

            def relu(i):
                r = rank(i)
                eng.wait_ge(s_acc, i + 1)
                wait(eng, s_sq, r - 2)
                eng.activation(pos[:, r % 2, :], acc[i % BANKS][:, :], ACT.Relu).then_inc(s_pos, 1)

            def tile_hi(i):
                t = tiles[i]
                hi = dest(t)[0]
                if t[2] == 1:
                    eng.wait_ge(s_dn, 4)
                if t[0] == "up":
                    eng.wait_ge(s_sq, rank(i))
                    eng.activation(hi, sq[:, rank(i) % 2, :], ACT.Copy).then_inc(s_thi, 1)
                else:
                    eng.wait_ge(s_acc, i + 1)
                    eng.activation(hi, acc[i % BANKS][:, :], ACT.Copy).then_inc(s_thi, 1)

            def sequence(b):
                eng.wait_ge(s_gt, b + 1)
                wait(eng, s_logit, b)
                eng.activation(glo[:, :], gt[:, E:2 * E], ACT.Copy).then_inc(s_gcopy, 1)
                eng.wait_ge(s_dn, b + 1)
                wait(eng, s_z, b)
                eng.activation(shared[:, :], dn[b % 2][:, :], ACT.Copy).then_inc(s_shared, 1)

            eng.wait_ge(s_small, 48)
            eng.activation(ghl[:, :, 0:E], gate[:, :].rearrange("p (c e) -> p c e", c=C), ACT.Copy).then_inc(s_ghi, 1)
            for n in range(len(pieces)):
                piece_hi(n)
                if n == 2:
                    tile_hi(0)
                    tile_hi(1)
                if pieces[n][0] == "down":
                    i = L + pieces[n][1]
                    relu(i)
                    if i > L:
                        tile_hi(i - 1)
            tile_hi(L + M - 1)
            for i in range(L + M, len(tiles)):
                if i == L + MT:
                    for b in range(4):
                        sequence(b)
                if tiles[i][0] == "up":
                    relu(i)
                    if tiles[i - 1][0] == "up":
                        tile_hi(i - 1)
                else:
                    if tiles[i - 1][0] == "up" and i >= L + MT:
                        tile_hi(i - 1)
                    tile_hi(i)
            for b in range(4, B):
                sequence(b)

        @block.tensor
        def _(eng):
            def tile(i):
                kind, m, h = tiles[i]
                out = acc[i % BANKS][:, :]
                j = i - BANKS
                if j >= 0:
                    if tiles[j][0] == "up":
                        eng.wait_ge(s_sq, rank(j))
                    else:
                        eng.wait_ge(s_tlo, j + 1)
                if kind == "lat":
                    eng.wait_ge(s_lo, at["fc2", 1] + 1)
                    for e in range(L):
                        mm = product(eng, out, [t[:, 0, e * 256 + m * P:e * 256 + (m + 1) * P] for t in wexp],
                                     [t[:, e, :] for t in wfc2], e == 0, e == L - 1)
                else:
                    for c in range(C):
                        if kind == "up":
                            eng.wait_ge(s_lo, at["up", 2 * c + m // 4] + 1)
                            st = [t[:, 2 * c + m // 4, m % 4 * P:(m % 4 + 1) * P] for t in wup]
                        else:
                            eng.wait_ge(s_lo, at["fc1", c // 2] + 1)
                            st = [t[:, c // 2, c % 2 * 256 + m * P:c % 2 * 256 + (m + 1) * P] for t in wfc1]
                        mm = product(eng, out, st, [t[:, c, h * HALF:(h + 1) * HALF] for t in xT], c == 0, c == C - 1)
                mm.then_inc(s_acc, 1)

            def sequence(b):
                h, tok, here = b // 4, slice(b * S, (b + 1) * S), slice(b % 4 * S, (b % 4 + 1) * S)
                wait(eng, s_logit, b)
                if b == 0:
                    eng.wait_ge(s_glo, 1)
                for c in range(C):
                    eng.matmul(gt[:, 0:2 * E], xT[0][:, c, tok], ghl[:, c, :], start=c == 0, stop=False)
                    mm = eng.matmul(gt[:, 0:E], xT[1][:, c, tok], ghl[:, c, 0:E], start=False, stop=c == C - 1)
                mm.then_inc(s_gt, 1)
                wait(eng, s_shared, b - 1)
                for m in range(M):
                    eng.wait_ge(s_lo, at["down", m] + 1)
                    eng.wait_ge(s_tlo, number["up", m, h] + 1)
                    product(eng, dn[b % 2][:, :], [t[:, m, here] for t in hT], [t[:, m, :] for t in wdown],
                            m == 0, m == M - 1)
                wait(eng, s_z, b)
                eng.wait_ge(s_tlo, number["fc1", L - 1, h] + 1)
                for l in range(L):
                    mm = product(eng, rt[:, :], [t[:, M + l, here] for t in hT], [t[:, l, :] for t in wlat],
                                 l == 0, l == L - 1)
                mm.then_inc(s_dn, 1)

            for i in range(L + MT):
                tile(i)
            for b in range(4):
                sequence(b)
            for i in range(L + MT, len(tiles)):
                tile(i)
            for b in range(4, B):
                sequence(b)

        @block.vector
        def _(eng):
            def piece_lo(n):
                kind, j = pieces[n]
                eng.wait_ge(s_hi, n + 1)
                hi, lo = (t[:, j, :] for t in target[kind])
                eng.tensor_tensor(lo, stage[:, n % RING, :], hi.bitcast(F32), ALU.subtract).then_inc(s_lo, 1)

            def square(i):
                r = rank(i)
                eng.wait_ge(s_pos, r)
                wait(eng, s_tlo, sq_free(i))
                eng.tensor_tensor(sq[:, r % 2, :], acc[i % BANKS][:, :], pos[:, r % 2, :], ALU.mult).then_inc(s_sq, 1)

            def sq_free(i):
                ups = [j for j in range(i) if tiles[j][0] == "up"]
                return ups[-2] + 1 if len(ups) > 1 else 0

            def tile_lo(i):
                t = tiles[i]
                hi, lo = dest(t)
                eng.wait_ge(s_thi, i + 1)
                src = sq[:, rank(i) % 2, :] if t[0] == "up" else acc[i % BANKS][:, :]
                eng.tensor_tensor(lo, src, hi.bitcast(F32), ALU.subtract).then_inc(s_tlo, 1)

            def sequence(b):
                eng.wait_ge(s_gcopy, b + 1)
                eng.tensor_tensor(logit[:, :], gt[:, 0:E], glo[:, :], ALU.add).then_inc(s_logit, 1)
                eng.wait_ge(s_logit, b + 1)
                eng.max(best[:, :], logit[:, :]).then_inc(s_best, 1)
                eng.wait_ge(s_best, b + 1)
                eng.tensor_tensor(route[:, :], best[:, 0:1], best[:, 1:2], ALU.add).then_inc(s_route, 1)
                eng.wait_ge(s_route, b + 1)
                eng.wait_ge(s_shared, b + 1)
                wait(eng, s_ln1, b)
                eng.scalar_tensor_tensor(out=z[:, 0, :], in0=rt[:, :], scalar=route[:, 0:1], in1=shared[:, :],
                                         op0=ALU.mult, op1=ALU.add).then_inc(s_z, 1)
                eng.wait_ge(s_z, b + 1)
                wait(eng, s_res, b)
                layer_norm(eng, z[:, 0, :], z[:, 1, :], stats[:, :], moments[:, :], rstd[:, :], ln_sems,
                           2 * b + 1).then_inc(s_ln1, 1)

            def finish(b):
                eng.wait_ge(s_beta, b + 1)
                eng.tensor_tensor(x2[:, b, :], x2[:, b, :], z[:, 1, :], ALU.add).then_inc(s_res, 1)
                eng.wait_ge(s_res, b + 1)
                layer_norm(eng, x2[:, b, :], x2[:, b, :], stats[:, :], moments[:, :], rstd[:, :], ln_sems,
                           2 * b + 2).then_inc(s_ln2, 1)

            eng.wait_ge(s_ghi, 1)
            eng.tensor_tensor(ghl[:, :, E:2 * E], gate[:, :].rearrange("p (c e) -> p c e", c=C),
                              ghl[:, :, 0:E].bitcast(F32), ALU.subtract).then_inc(s_glo, 1)
            for n in range(len(pieces)):
                piece_lo(n)
                if n == 2:
                    tile_lo(0)
                    tile_lo(1)
                if pieces[n][0] == "down":
                    i = L + pieces[n][1]
                    square(i)
                    if i > L:
                        tile_lo(i - 1)
            tile_lo(L + M - 1)
            for i in range(L + M, len(tiles)):
                if i == L + MT:
                    for b in range(4):
                        sequence(b)
                        finish(b)
                if tiles[i][0] == "up":
                    square(i)
                    if tiles[i - 1][0] == "up":
                        tile_lo(i - 1)
                else:
                    if tiles[i - 1][0] == "up" and i >= L + MT:
                        tile_lo(i - 1)
                    tile_lo(i)
            for b in range(4, B):
                sequence(b)
                finish(b)

        @block.gpsimd
        def _(eng):
            eng.wait_ge(s_small, 48)
            for b in range(B):
                inverse_root(eng, moments[:, :], rstd[:, :], power, ln_sems, 2 * b + 1)
                eng.wait_ge(s_ln1, b + 1)
                eng.tensor_tensor(z[:, 1, :], z[:, 1, :], gamma[:, :], ALU.mult).then_inc(s_gamma, 1)
                eng.wait_ge(s_gamma, b + 1)
                eng.tensor_tensor(z[:, 1, :], z[:, 1, :], beta[:, :], ALU.add).then_inc(s_beta, 1)
                inverse_root(eng, moments[:, :], rstd[:, :], power, ln_sems, 2 * b + 2)


def decoder_layer(nc, x_nat, xT0, ctxT, mask, wqkvT, bqk, bv, woutT, bout, wq, wk, wv, wo, gate, up, down, fc1, fc2,
                  expT, gamma, beta, alibi, trig, ident_d, out):
    with ExitStack() as ctx:
        sb = lambda name, shape, dt=F32: ctx.enter_context(nc.sbuf_tensor(name, shape, dt))
        ident = sb("ident", [P, P])
        power = sb("power", [P, 1])
        x1 = sb("x", [P, B, D])
        s_ident = ctx.enter_context(nc.semaphore("ident_landed"))
        with nc.Block() as block:
            @block.sync
            def _(eng):
                eng.dma_start(ident[:, :], ident_d).then_inc(s_ident, 16)
                eng.wait_ge(s_ident, 16)

            @block.vector
            def _(eng):
                eng.memset(power[:, :], -0.5)
        with ExitStack() as self_ctx:
            ssb = lambda name, shape: self_ctx.enter_context(nc.sbuf_tensor(name, shape, F32R))
            q = [ssb("q" + s, [P, C, NT]) for s in ("h", "l")]
            k = [ssb("k" + s, [P, C, NT]) for s in ("h", "l")]
            vhl = ssb("vhl", [P, B, HS, 2 * DH])
            project_self(nc, xT0, wqkvT, bqk, bv, q, k, vhl)
            attend_self(nc, x_nat, alibi, woutT, bout, ident[:, :], q, k, vhl, x1)
        xT = [sb("xT" + s, [P, C, NT], F32R) for s in ("h", "l")]
        turn(nc, "T1", x1, xT, ident[:, :], power[:, :])
        attend_cross(nc, ctxT, wq, wk, wv, wo, mask, trig, ident[:, :], xT, x1)
        turn(nc, "T2", x1, xT, ident[:, :], power[:, :])
        feed_forward(nc, up, down, fc1, fc2, expT, gate, gamma, beta, power[:, :], xT, x1, out)


def tables():
    import numpy as np
    slopes = (1.0 / np.power(np.float32(2.0), np.arange(1, HS + 1, dtype=np.float32) * np.float32(8 / HS))).astype(np.float32)
    bias = slopes[:, None] * np.arange(1 - S, 1, dtype=np.float32)[None, :]
    causal = np.arange(S)[:, None] >= np.arange(S)[None, :]
    alibi = np.where(causal[:, None, :], bias[None], np.float32(-1e9)).astype(np.float32)
    inv = (1.0 / np.float32(10000.0) ** (np.arange(0, P, 2, dtype=np.float32) / np.float32(P))).astype(np.float32)
    angle = (np.arange(S, dtype=np.float32)[:, None] * inv[None, :]).astype(np.float32).T
    cos, sin = np.cos(angle), np.sin(angle)
    cos = np.concatenate([cos, cos])
    sin = np.concatenate([-sin, sin])
    scale = np.sqrt(np.float32(P))
    trig = np.stack([cos / scale, sin / scale, cos, sin], 1).astype(np.float32)
    return alibi, trig, np.eye(P, dtype=np.float32)


def kernel(**inputs):
    import numpy as np
    import concourse.bacc as bacc
    from concourse.bass_utils import run_bass_kernel_spmd

    a = {n: np.asarray(v) for n, v in inputs.items()}
    rows = lambda w: w.reshape(-1, P, w.shape[1]).transpose(1, 0, 2)
    spread = lambda v: np.broadcast_to(v[None, :], (P, v.shape[0]))
    pre, xp, fp = "L0_attn_", "L0_xattn_", "L0_ffn_"
    alibi, trig, ident = tables()
    bqkv = a[pre + "b_qkv"]
    arrays = {
        "x_nat": a["x"].transpose(1, 0, 2),
        "xT": rows(a["x"].reshape(NT, D).T),
        "ctxT": rows(a["ctx_4096"].reshape(NT, D).T),
        "mask": a["mask_BxSxS2_ff0"].transpose(1, 0, 2),
        "wqkvT": rows(a[pre + "w_qkv"].T),
        "bqk": bqkv[:2 * D].reshape(2 * C, P).T,
        "bv": spread(bqkv[2 * D:]),
        "woutT": rows(a[pre + "w_out"].T),
        "bout": spread(a[pre + "b_out"]),
        "wq": a[xp + "wq"].reshape(C, P, NG, HG, P).transpose(2, 1, 3, 0, 4).reshape(NG, P, HG, C * P),
        "wk": a[xp + "wk"].reshape(C, P, NG, P).transpose(2, 1, 0, 3).reshape(NG, P, C * P),
        "wv": a[xp + "wv"].reshape(C, P, NG, P).transpose(2, 1, 0, 3).reshape(NG, P, C * P),
        "wo": a[xp + "wo"].reshape(NG, HG, P, D).transpose(0, 2, 1, 3),
        "gate": rows(a[fp + "gate_w"]).reshape(P, -1),
        "up": rows(a[fp + "up_w"]).reshape(P, 2 * C, D),
        "down": rows(a[fp + "down_w"]),
        "fc1": rows(a[fp + "fc1_w"]).reshape(P, 2, D),
        "fc2": rows(a[fp + "fc2_w"]),
        "expT": rows(a[fp + "expert_w"].T).reshape(P, 1, D),
        "gamma": spread(a[fp + "ln_gamma"]),
        "beta": spread(a[fp + "ln_beta"]),
        "alibi": alibi,
        "trig": trig,
        "ident": ident,
    }
    arrays = {n + "_dram": np.ascontiguousarray(v) for n, v in arrays.items()}
    nc = bacc.Bacc("TRN2", target_bir_lowering=False, num_devices=1)
    args = [nc.dram_tensor(n, v.shape, mybir.dt.from_np(v.dtype), kind="ExternalInput").ap() for n, v in arrays.items()]
    args.append(nc.dram_tensor("out_dram", (B, S, D), F32, kind="ExternalOutput").ap())
    decoder_layer(nc, *args)
    r = run_bass_kernel_spmd(nc, [arrays], core_ids=[0])
    return r.results[0]["out_dram"]
```

```python
from contextlib import ExitStack

import concourse.bass as bass
from concourse import mybir

F32 = mybir.dt.float32
F32R = mybir.dt.float32r
ALU = mybir.AluOpType
ACT = mybir.ActivationFunctionType
AX = mybir.AxisListType

P = 128
B = 8
S = 128
D = 512
C = D // P
NT = B * S
HALF = NT // 2
HS = 32
DH = D // HS
HG = 4
NG = 8
EPS = 1e-5

PASSES = ((0, 0), (0, 1), (1, 0))


def product(eng, out, stationary, moving, first, last):
    for n, (i, j) in enumerate(PASSES):
        mm = eng.matmul(out, stationary[i], moving[j], start=first and n == 0,
                        stop=last and n == len(PASSES) - 1)
    return mm


def layer_norm(eng, z, out, stats, moments, rstd, sems, count):
    s_stats, s_moments, s_var, s_rstd = sems
    eng.bn_stats(stats, z).then_inc(s_stats, 1)
    eng.wait_ge(s_stats, count)
    eng.bn_aggr(moments, stats).then_inc(s_moments, 1)
    eng.wait_ge(s_moments, count)
    eng.tensor_scalar(moments[:, 1:2], moments[:, 1:2], EPS, None, ALU.add).then_inc(s_var, 1)
    eng.wait_ge(s_rstd, count)
    return eng.tensor_scalar(out, z, moments[:, 0:1], rstd, ALU.subtract, ALU.mult)


def inverse_root(eng, moments, rstd, power, sems, count):
    eng.wait_ge(sems[2], count)
    eng.tensor_tensor(rstd, moments[:, 1:2], power, ALU.pow).then_inc(sems[3], 1)


class Turn:

    def __init__(self, nc, ctx, name, x_nat, xT, ident, power, banks):
        sb = lambda s, shape: ctx.enter_context(nc.sbuf_tensor(f"{name}_norm_{s}", shape, F32))
        sem = lambda s: ctx.enter_context(nc.semaphore(f"{name}_norm_{s}"))
        self.x, self.xT, self.ident, self.power, self.banks = x_nat, xT, ident, power, banks
        self.stats, self.moments, self.rstd = sb("stats", [P, B, 6]), sb("moments", [P, B, 2]), sb("rstd", [P, B])
        self.s_stats, self.s_moments, self.s_var, self.s_rstd = sem("stats"), sem("moments"), sem("var"), sem("rstd")
        self.s_row, self.s_tp, self.s_hi, self.s_lo = sem("row"), sem("tp"), sem("hi"), sem("lo")

    def statistics(self, eng, b):
        eng.bn_stats(self.stats[:, b, :], self.x[:, b, :]).then_inc(self.s_stats, 1)

    def moments_of_all(self, eng):
        eng.wait_ge(self.s_stats, B)
        for b in range(B):
            eng.bn_aggr(self.moments[:, b, :], self.stats[:, b, :]).then_inc(self.s_moments, 1)
        eng.wait_ge(self.s_moments, B)
        var = self.moments[:, :, 1]
        eng.tensor_scalar(var, var, EPS, None, ALU.add).then_inc(self.s_var, 1)

    def roots(self, eng):
        eng.wait_ge(self.s_var, 1)
        eng.tensor_tensor(self.rstd[:, :], self.moments[:, :, 1], self.power.broadcast_to([P, B]),
                          ALU.pow).then_inc(self.s_rstd, 1)

    def normalise(self, eng, b):
        if b == 0:
            eng.wait_ge(self.s_rstd, 1)
        eng.tensor_scalar(self.x[:, b, :], self.x[:, b, :], self.moments[:, b, 0:1], self.rstd[:, b:b + 1],
                          ALU.subtract, ALU.mult).then_inc(self.s_row, 1)

    def transpose(self, eng, b):
        eng.wait_ge(self.s_row, b + 1)
        n = len(self.banks)
        if b >= n:
            eng.wait_ge(self.s_lo, b - n + 1)
        for c in range(C):
            mm = eng.transpose(self.banks[b % n][:, c * S:(c + 1) * S], self.x[:, b, c * P:(c + 1) * P], self.ident)
        mm.then_inc(self.s_tp, 1)

    def _tile(self, b, part):
        bank = self.banks[b % len(self.banks)][:, :].rearrange("p (c s) -> p c s", c=C)
        return bank, self.xT[part][:, :, b * S:(b + 1) * S]

    def hi(self, eng, b):
        eng.wait_ge(self.s_tp, b + 1)
        bank, out = self._tile(b, 0)
        eng.activation(out, bank, ACT.Copy).then_inc(self.s_hi, 1)

    def lo(self, eng, b):
        eng.wait_ge(self.s_hi, b + 1)
        bank, out = self._tile(b, 1)
        eng.tensor_tensor(out, bank, self._tile(b, 0)[1].bitcast(F32), ALU.subtract).then_inc(self.s_lo, 1)


def wait(eng, sem, value):
    if not isinstance(value, int) or value > 0:
        eng.wait_ge(sem, value)


def project_self(nc, xT_d, wqkv_d, bqk_d, bv_d, alibi_d, q, k, vhl, alibi):
    RING = 3
    NX = C * 2
    NW = C * 3
    pieces = [("x", c, 0) for c in range(C)] + [("w", c, 0) for c in range(C)] + \
             [("w", c, 1) for c in range(C)] + [("x", c, 1) for c in range(C)] + \
             [("w", c, 2) for c in range(C)]
    at = {p: n for n, p in enumerate(pieces)}
    tiles = [("qk", m, h) for h, part in ((0, 0), (0, 1), (1, 0), (1, 1)) for m in range(part * C, part * C + C)] + \
            [("v", b, 0) for b in range(B)]
    order = tiles
    Q_DONE = 3 * C
    BANKS = 4
    with ExitStack() as ctx:
        sb = lambda name, shape, dt=F32: ctx.enter_context(nc.sbuf_tensor("A_" + name, shape, dt))
        sem = lambda name: ctx.enter_context(nc.semaphore("A_" + name))
        stage = sb("stage", [P, RING, D])
        xT = [sb("xT" + s, [P, C, NT], F32R) for s in ("h", "l")]
        w = [sb("w" + s, [P, C, 2 * D], F32R) for s in ("h", "l")]
        bqk = sb("bqk", [P, 2 * C])
        bv = sb("bv", [P, D])
        val = sb("val", [P, 2, D])
        acc = [ctx.enter_context(nc.psum_tensor(f"A_acc{i}", [P, D], F32)) for i in range(BANKS)]
        s_piece = [sem(f"piece{i}") for i in range(RING)]
        s_alibi = sem("alibi")
        s_bias, s_hi, s_lo, s_acc = sem("bias"), sem("hi"), sem("lo"), sem("acc")
        s_val, s_vhi, s_vlo = sem("val"), sem("vhi"), sem("vlo")
        block = ctx.enter_context(nc.Block())

        def place(t, piece):
            kind, c, n = piece
            if kind == "w":
                n %= 2
            return t[:, c, n * D:(n + 1) * D]

        AHEAD = 12

        def pieces_with(i):
            return [AHEAD + i] if i < C else [AHEAD + C + i - Q_DONE - 1] if 0 <= i - Q_DONE - 1 < C else []

        @block.sync
        def _(eng):
            for n, piece in enumerate(pieces):
                if n >= RING:
                    eng.wait_ge(s_lo, n - RING + 1)
                src = xT_d if piece[0] == "x" else wqkv_d
                eng.dma_start(stage[:, n % RING, :], src[:, piece[1], piece[2] * D:(piece[2] + 1) * D])\
                   .then_inc(s_piece[n % RING], 16)
                if n == 0:
                    eng.dma_start(bqk[:, :], bqk_d).then_inc(s_bias, 16)
                    eng.dma_start(bv[:, :], bv_d).then_inc(s_bias, 16)
            for c in range(C):
                eng.dma_start(alibi[:, c * 8:(c + 1) * 8, :], alibi_d[:, c * 8:(c + 1) * 8, :]).then_inc(s_alibi, 16)
            eng.wait_ge(s_alibi, 16 * C)

        @block.scalar
        def _(eng):
            def piece_hi(n):
                eng.wait_ge(s_piece[n % RING], 16 * (n // RING + 1))
                dst = xT if pieces[n][0] == "x" else w
                if pieces[n][0] == "w" and pieces[n][2] == 2:
                    eng.wait_ge(s_acc, Q_DONE)
                eng.activation(place(dst[0], pieces[n]), stage[:, n % RING, :], ACT.Copy).then_inc(s_hi, 1)

            def tile_hi(i):
                kind, m, h = order[i]
                eng.wait_ge(s_val, i + 1)
                src = val[:, i % 2, :]
                if kind == "qk":
                    dst = (q if m < C else k)[:, 2 * (m % C), h * HALF:(h + 1) * HALF]
                else:
                    dst = vhl[:, m, :, 0:DH]
                    src = src.rearrange("p (h d) -> p h d", d=DH)
                eng.activation(dst, src, ACT.Copy).then_inc(s_vhi, 1)

            for n in range(AHEAD):
                piece_hi(n)
            for i in range(len(order)):
                for n in pieces_with(i):
                    piece_hi(n)
                tile_hi(i)

        @block.tensor
        def _(eng):
            for i, (kind, m, h) in enumerate(order):
                out = acc[i % BANKS][:, :]
                if i >= BANKS:
                    eng.wait_ge(s_val, i - BANKS + 1)
                for c in range(C):
                    if kind == "qk":
                        eng.wait_ge(s_lo, max(at["w", c, m // C], at["x", c, h]) + 1)
                        st = [t[:, c, m * P:(m + 1) * P] for t in w]
                        mv = [t[:, c, h * HALF:(h + 1) * HALF] for t in xT]
                    else:
                        eng.wait_ge(s_lo, at["w", c, 2] + 1)
                        st = [t[:, c, m * S:(m + 1) * S] for t in xT]
                        mv = [t[:, c, 0:D] for t in w]
                    mm = product(eng, out, st, mv, c == 0, c == C - 1)
                mm.then_inc(s_acc, 1)

        @block.vector
        def _(eng):
            def piece_lo(n):
                eng.wait_ge(s_hi, n + 1)
                dst = xT if pieces[n][0] == "x" else w
                eng.tensor_tensor(place(dst[1], pieces[n]), stage[:, n % RING, :],
                                  place(dst[0], pieces[n]).bitcast(F32), ALU.subtract).then_inc(s_lo, 1)

            def tile(i):
                kind, m, h = order[i]
                eng.wait_ge(s_acc, i + 1)
                if i >= 2:
                    eng.wait_ge(s_vlo, i - 1)
                out = val[:, i % 2, :]
                if i == 0:
                    eng.wait_ge(s_bias, 32)
                if kind == "v":
                    eng.tensor_tensor(out, acc[i % BANKS][:, :], bv[:, :], ALU.add).then_inc(s_val, 1)
                elif m < C:
                    eng.tensor_scalar(out, acc[i % BANKS][:, :], bqk[:, m:m + 1], DH ** -0.5,
                                      ALU.add, ALU.mult).then_inc(s_val, 1)
                else:
                    eng.tensor_scalar(out, acc[i % BANKS][:, :], bqk[:, m:m + 1], None,
                                      ALU.add).then_inc(s_val, 1)

            for n in range(AHEAD):
                piece_lo(n)
            for i in range(len(order)):
                for n in pieces_with(i):
                    piece_lo(n)
                tile(i)

        @block.gpsimd
        def _(eng):
            for i, (kind, m, h) in enumerate(order):
                eng.wait_ge(s_vhi, i + 1)
                src = val[:, i % 2, :]
                if kind == "qk":
                    t = q if m < C else k
                    hi, lo = (t[:, 2 * (m % C) + j, h * HALF:(h + 1) * HALF] for j in range(2))
                else:
                    src = src.rearrange("p (h d) -> p h d", d=DH)
                    hi, lo = vhl[:, m, :, 0:DH], vhl[:, m, :, DH:2 * DH]
                eng.tensor_tensor(lo, src, hi.bitcast(F32), ALU.subtract).then_inc(s_vlo, 1)


def attend_self(nc, x_d, wout_d, bout_d, ident, q, k, vhl, alibi, x1):
    LT, LV = 2, 4
    NS = B * NG
    PAIR = NG // 2
    LOADS = 16 * (8 + 1)
    with ExitStack() as ctx:
        sb = lambda name, shape, dt=F32: ctx.enter_context(nc.sbuf_tensor("B_" + name, shape, dt))
        pb = lambda name: ctx.enter_context(nc.psum_tensor("B_" + name, [P, D], F32))
        sem = lambda name: ctx.enter_context(nc.semaphore("B_" + name))
        qs = sb("qs", [P, 2 * C, S], F32R)
        kd = sb("kd", [P, 2 * C, 8, S], F32R)
        wout = [sb("wout" + s, [P, C, D], F32R) for s in ("h", "l")]
        prob = sb("prob", [P, 4, HG * S])
        pT = [sb("pT" + s, [P, 2, HG * S], F32R) for s in ("h", "l")]
        top = sb("top", [P, 2, HG])
        carrier = sb("carrier", [P, 1])
        ntop = sb("ntop", [P, 4, HG])
        total = sb("total", [P, HS])
        rden = sb("rden", [P, HS])
        ohl = sb("ohl", [P, 16, DH])
        o = sb("o", [P, HS, DH])
        oT = [sb("oT" + s, [P, C, S], F32R) for s in ("h", "l")]
        wst = sb("wst", [P, D])
        bout = wst[:, :]
        sc = [pb("sc0"), pb("sc1")]
        tp = [pb("tp0"), pb("tp1")]
        ov = [pb("ov0"), pb("ov1")]
        ot, yb = pb("ot"), pb("yb")
        s_zero, s_x, s_wst, s_bout = sem("zero"), sem("x"), sem("wst"), sem("bout")
        s_whi, s_wlo, s_xb = sem("whi"), sem("wlo"), sem("xb")
        s_load = [sem("load0"), sem("load1")]
        s_sc, s_top, s_ntop, s_exp = sem("sc"), sem("top"), sem("ntop"), sem("exp")
        s_tp, s_phi, s_plo, s_pv = sem("tp"), sem("phi"), sem("plo"), sem("pv")
        s_rden, s_ohl, s_oadd, s_o = sem("rden"), sem("ohl"), sem("oadd"), sem("o")
        s_ot, s_ohi, s_olo, s_y, s_z = sem("ot"), sem("ohi"), sem("olo"), sem("y"), sem("z")
        block = ctx.enter_context(nc.Block())

        def live(b, G, lag=0):
            return not isinstance(b, int) or 0 <= NG * b + G - lag < NS

        def follows(b):
            return not isinstance(b, int) or 1 <= b <= B

        def loop(eng, step):
            for b in range(2):
                for G in range(NG):
                    step(b, G)
            with eng.Fori(2, B) as b:
                for G in range(NG):
                    step(b, G)
            for G in range(NG):
                step(B, G)

        @block.sync
        def _(eng):
            def load(b, pair):
                if not isinstance(b, int) or b > 0:
                    eng.wait_ge(s_sc, NG * (b - 1) + PAIR * (pair + 1))
                cs, tok = slice(4 * pair, 4 * pair + 4), bass.ts(b, S)
                eng.dma_start(qs[:, cs, :].bitcast(F32), q[:, cs, tok].bitcast(F32)).then_inc(s_load[pair], 16)
                for r in range(8):
                    rows = slice(r * DH, (r + 1) * DH)
                    eng.dma_start(kd[rows, cs, r, :].bitcast(F32),
                                  k[rows, cs, tok].bitcast(F32)).then_inc(s_load[pair], 16)

            eng.wait_ge(s_zero, 2)
            for pair in range(2):
                load(0, pair)
            eng.dma_start(bout, bout_d).then_inc(s_bout, 16)
            eng.dma_start(x1[:, :, :], x_d).then_inc(s_x, 16)
            for c in range(C):
                if c:
                    eng.wait_ge(s_wlo, c)
                else:
                    eng.wait_ge(s_xb, 1)
                eng.dma_start(wst[:, :], wout_d[:, c, :]).then_inc(s_wst, 16)
            for pair in range(2):
                load(1, pair)
            with eng.Fori(2, B) as b:
                for pair in range(2):
                    load(b, pair)

        @block.gpsimd
        def _(eng):
            eng.memset(kd[:, C:2 * C, :, :].bitcast(F32), 0.0).then_inc(s_zero, 1)
            eng.wait_ge(s_x, 16)
            eng.wait_ge(s_bout, 16)
            eng.tensor_tensor(x1[:, :, :], x1[:, :, :], bout.unsqueeze(1).broadcast_to([P, B, D]),
                              ALU.add).then_inc(s_xb, 1)

        @block.scalar
        def _(eng):
            def step(b, G):
                n = NG * b + G
                if G in (0, 4) and follows(b):
                    eng.wait_ge(s_pv, n - LV)
                    wait(eng, s_oadd, 2 * b - 2 + G // 4)
                    eng.activation(ohl[:, :, :],
                                   ov[G // 4][:, :].rearrange("p (h t d) -> p h t d", t=2, d=DH)[:, :, 1, :],
                                   ACT.Copy).then_inc(s_ohl, 1)
                if G == 6 and follows(b):
                    eng.wait_ge(s_ot, b)
                    wait(eng, s_y, b - 1)
                    eng.activation(oT[0][:, :, :], ot[:, :].rearrange("p (c s) -> p c s", c=C),
                                   ACT.Copy).then_inc(s_ohi, 1)
                if live(b, G, LT):
                    eng.wait_ge(s_tp, n - LT + 1)
                    wait(eng, s_pv, n - LT - 1)
                    eng.activation(pT[0][:, G % 2, :], tp[G % 2][:, :], ACT.Copy).then_inc(s_phi, 1)
                if live(b, G):
                    eng.wait_ge(s_ntop, n + 1)
                    if G % 4 == 0:
                        wait(eng, s_rden, 2 * b - 1 + G // 4)
                    for h in range(HG):
                        e = prob[:, G % 4, h * S:(h + 1) * S]
                        last = eng.activation(e, e, ACT.Exp, bias=ntop[:, G % 4, h:h + 1], scale=1.0,
                                              accum_out=total[:, HG * G + h:HG * G + h + 1])
                    last.then_inc(s_exp, 1)
                if isinstance(b, int) and b == 0 and G >= NG - C:
                    c = G - (NG - C)
                    eng.wait_ge(s_wst, 16 * (c + 1))
                    eng.activation(wout[0][:, c, :], wst[:, :], ACT.Copy).then_inc(s_whi, 1)

            loop(eng, step)

        @block.tensor
        def _(eng):
            def step(b, G):
                n = NG * b + G
                if live(b, G):
                    if G % PAIR == 0:
                        eng.wait_ge(s_load[G // PAIR], LOADS * (b + 1))
                    wait(eng, s_top, n - 1)
                    c, cols = G // 2, slice(4 * (G % 2), 4 * (G % 2) + 4)
                    product(eng, sc[G % 2][:, :].rearrange("p (h s) -> p h s", h=HG), [qs[:, 2 * c + j, :] for j in range(2)],
                            [kd[:, 2 * c + j, cols, :] for j in range(2)], True, True).then_inc(s_sc, 1)
                if live(b, G, LV):
                    g, bb = (G - LV) % NG, b if G >= LV else b - 1
                    m = n - LV
                    eng.wait_ge(s_phi, m + 1)
                    eng.wait_ge(s_plo, m + 1)
                    if g % 4 == 0:
                        wait(eng, s_oadd, 2 * bb - 1 + g // 4)
                    for h in range(HG):
                        head = HG * g + h
                        at = (head % 16) * 2 * DH
                        out = ov[g // 4]
                        v = vhl[:, bass.ds(bb, 1), head, :].rearrange("p a d -> p (a d)")
                        eng.matmul(out[:, at:at + 2 * DH], pT[0][:, G % 2, h * S:(h + 1) * S], v,
                                   start=True, stop=False)
                        mm = eng.matmul(out[:, at:at + DH], pT[1][:, G % 2, h * S:(h + 1) * S], v[:, 0:DH],
                                        start=False, stop=True)
                    mm.then_inc(s_pv, 1)
                if live(b, G, LT):
                    m = n - LT
                    eng.wait_ge(s_exp, m + 1)
                    wait(eng, s_phi, m - 1)
                    wait(eng, s_plo, m - 1)
                    for h in range(HG):
                        mm = eng.transpose(tp[G % 2][:, h * S:(h + 1) * S],
                                           prob[:, (G - LT) % 4, h * S:(h + 1) * S], ident)
                    mm.then_inc(s_tp, 1)
                if G == 5 and follows(b):
                    eng.wait_ge(s_o, 2 * b)
                    wait(eng, s_olo, b - 1)
                    for c in range(C):
                        mm = eng.transpose(ot[:, c * P:(c + 1) * P],
                                           o[:, 8 * c:8 * c + 8, :].rearrange("p h d -> p (h d)"), ident)
                    mm.then_inc(s_ot, 1)
                if G == 7 and follows(b):
                    eng.wait_ge(s_ohi, b)
                    eng.wait_ge(s_olo, b)
                    wait(eng, s_z, b - 1)
                    eng.wait_ge(s_wlo, C)
                    for c in range(C):
                        mm = product(eng, yb[:, :], [t[:, c, :] for t in oT], [t[:, c, :] for t in wout],
                                     c == 0, c == C - 1)
                    mm.then_inc(s_y, 1)

            loop(eng, step)

        @block.vector
        def _(eng):
            def step(b, G):
                n = NG * b + G
                if live(b, G):
                    eng.wait_ge(s_sc, n + 1)
                    wait(eng, s_tp, n - 3)
                    eng.memset(carrier[:, :], 0.0)
                    for h in range(HG):
                        last = eng.tensor_tensor_reduce(
                            prob[:, G % 4, h * S:(h + 1) * S], sc[G % 2][:, h * S:(h + 1) * S],
                            alibi[:, HG * G + h, :], 1.0, -3e38, ALU.add, ALU.max, top[:, G % 2, h:h + 1])
                    last.then_inc(s_top, 1)
                    eng.wait_ge(s_top, n + 1)
                    wait(eng, s_exp, n - 3)
                    eng.tensor_scalar(ntop[:, G % 4, :], top[:, G % 2, :], -1.0, None, ALU.mult).then_inc(s_ntop, 1)
                if G in (0, 4) and live(b, G, 1):
                    half = 1 - G // 4
                    eng.wait_ge(s_exp, n)
                    eng.reciprocal(rden[:, 16 * half:16 * half + 16],
                                   total[:, 16 * half:16 * half + 16]).then_inc(s_rden, 1)
                if G in (0, 4) and follows(b):
                    half, done = G // 4, 2 * b - 1 + G // 4
                    heads = slice(16 * half, 16 * half + 16)
                    eng.wait_ge(s_ohl, done)
                    wait(eng, s_ot, b - 1)
                    eng.tensor_tensor(o[:, heads, :],
                                      ov[half][:, :].rearrange("p (h t d) -> p h t d", t=2, d=DH)[:, :, 0, :],
                                      ohl[:, :, :], ALU.add).then_inc(s_oadd, 1)
                    eng.wait_ge(s_oadd, done)
                    eng.wait_ge(s_rden, done)
                    eng.tensor_tensor(o[:, heads, :], o[:, heads, :],
                                      rden[:, heads].unsqueeze(2).broadcast_to([P, 16, DH]),
                                      ALU.mult).then_inc(s_o, 1)
                if live(b, G, LT):
                    m = n - LT
                    eng.wait_ge(s_phi, m + 1)
                    eng.tensor_tensor(pT[1][:, G % 2, :], tp[G % 2][:, :], pT[0][:, G % 2, :].bitcast(F32),
                                      ALU.subtract).then_inc(s_plo, 1)
                if G == 6 and follows(b):
                    eng.wait_ge(s_ohi, b)
                    eng.tensor_tensor(oT[1][:, :, :], ot[:, :].rearrange("p (c s) -> p c s", c=C),
                                      oT[0][:, :, :].bitcast(F32), ALU.subtract).then_inc(s_olo, 1)
                if isinstance(b, int) and b == 0 and G >= NG - C:
                    c = G - (NG - C)
                    eng.wait_ge(s_whi, c + 1)
                    eng.tensor_tensor(wout[1][:, c, :], wst[:, :], wout[0][:, c, :].bitcast(F32),
                                      ALU.subtract).then_inc(s_wlo, 1)
                if G == 7 and follows(b):
                    eng.wait_ge(s_y, b)
                    eng.wait_ge(s_xb, 1)
                    row = x1[:, bass.ds(b - 1, 1), :].rearrange("p a d -> p (a d)")
                    eng.tensor_tensor(row, yb[:, :], row, ALU.add).then_inc(s_z, 1)

            eng.memset(kd[:, 0:C, :, :].bitcast(F32), 0.0).then_inc(s_zero, 1)
            loop(eng, step)


def attend_cross(nc, ctxT_d, wq_d, wk_d, wv_d, wo_d, mask_d, trig_d, ident, power, xT, y):
    G, Q = NG, HG
    NS = G * B
    RING = 5
    STEPS = {0: (0, 1), 1: (2,), 2: (3, 4), 3: (5,)}
    K, V, TILES = 4, 5, 6
    PER = 10
    with ExitStack() as ctx:
        sb = lambda name, shape, dt=F32: ctx.enter_context(nc.sbuf_tensor("C_" + name, shape, dt))
        pb = lambda name: ctx.enter_context(nc.psum_tensor("C_" + name, [P, D], F32))
        sem = lambda name: ctx.enter_context(nc.semaphore("C_" + name))
        pair = lambda name, shape: [sb(name + s, shape, F32R) for s in ("h", "l")]
        cT = pair("cT", [P, C, NT])
        q = pair("q", [P, Q, NT])
        k = sb("k", [P, B, 2, S], F32R)
        v = pair("v", [P, B, P])
        w = pair("w", [P, TILES, D])
        wo = pair("wo", [P, Q, D])
        stage = sb("stage", [P, RING, D])
        o = pair("o", [P, Q * S])
        pT = pair("pT", [P, Q * S])
        prob = sb("prob", [P, 2, Q * S])
        t1 = sb("t1", [P, 2, D])
        t2 = sb("t2", [P, 2, D])
        trig = sb("trig", [P, 4, S])
        mask = sb("mask", [P, B, S])
        carrier = sb("carrier", [P, 1])
        top, ntop = sb("top", [P, 2, Q]), sb("ntop", [P, 2, Q])
        total, rden = sb("total", [P, 2, Q]), sb("rden", [P, 2, Q])
        sc = ctx.enter_context(nc.psum_tensor("C_sc", [P, 2, 2, 2, S], F32))
        tp, ov, yb, vp = pb("tp"), pb("ov"), pb("yb"), pb("vp")
        pj = [pb("pj0"), pb("pj1")]
        s_const = sem("const")
        s_piece = [sem(f"piece{i}") for i in range(RING)]
        s_whi, s_wlo, s_wolo = sem("whi"), sem("wlo"), [sem("wolo0"), sem("wolo1")]
        s_chi, s_clo = sem("chi"), sem("clo")
        s_pj, s_cos, s_sin, s_sum, s_qhi, s_qlo = sem("pj"), sem("cos"), sem("sin"), sem("sum"), sem("qhi"), sem("qlo")
        s_vt, s_vp, s_vhi, s_vlo = sem("vt"), sem("vp"), sem("vhi"), sem("vlo")
        s_sc, s_top, s_ntop, s_exp, s_rden, s_norm = sem("sc"), sem("top"), sem("ntop"), sem("exp"), sem("rden"), sem("norm")
        s_tp, s_phi, s_plo, s_pv, s_ohi, s_olo = sem("tp"), sem("phi"), sem("plo"), sem("pv"), sem("ohi"), sem("olo")
        s_y, s_add, s_masked = sem("y"), sem("add"), sem("masked")
        NX = 2 * C
        FIRST = NX + TILES
        vt = t2[:, V % 2, :]
        norm = Turn(nc, ctx, "C", y, xT, ident, power, [tp, ov, yb, vp])
        block = ctx.enter_context(nc.Block())

        def live(g, s, lag=0):
            return not isinstance(g, int) or 0 <= B * g + s - lag < NS

        def loop(eng, step):
            for s in range(B):
                step(0, s)
            with eng.Fori(1, G - 1) as g:
                for s in range(B):
                    step(g, s)
            for g in (G - 1, G):
                for s in range(B):
                    step(g, s)

        def projects(g, s):
            return not isinstance(g, int) or g < G - 1 or (g == G - 1 and s < 4)

        def half_cycle(g, s):
            return 2 * g + 1 + s // 4

        def where(H_half, j):
            cols = slice(H_half * HALF, (H_half + 1) * HALF)
            return [t[:, j, cols].rearrange("p (b s) -> p b s", s=S) for t in q] if j < K else \
                [k[:, 4 * H_half:4 * H_half + 4, i, :] for i in range(2)]

        def lo_of(g, j):
            return TILES * g + j + 1

        SPLITS = {2: [("wo", h) for h in range(Q)] + [("w", 0)], 3: [("w", 1), ("w", 2)],
                  4: [("w", 3)], 5: [("w", K)], 6: [("w", V)]}

        def splits(g, s):
            return [x for x in SPLITS.get(s, ()) if not isinstance(g, int) or g < G - 1 or (g == G - 1 and x[0] == "wo")]

        def slot(what):
            kind, j = what
            return (FIRST + (j if kind == "wo" else Q + j)) % RING

        def landed(eng, g, what):
            kind, j = what
            at = FIRST + (j if kind == "wo" else Q + j)
            eng.wait_ge(s_piece[at % RING], 16 * (at // RING + 1 + (PER // RING) * g))

        @block.sync
        def _(eng):
            for n in range(FIRST):
                wait(eng, s_clo if n - RING < NX else s_wlo, n - RING + 1 if n - RING < NX else n - RING - NX + 1)
                src = ctxT_d[:, n // 2, n % 2 * HALF:(n % 2 + 1) * HALF] if n < NX else \
                    (wq_d[0, :, n - NX, :] if n < NX + K else (wk_d if n == NX + K else wv_d)[0])
                eng.dma_start(stage[:, n % RING, :], src).then_inc(s_piece[n % RING], 16)
                if n == 0:
                    eng.dma_start(trig[:, :, :], trig_d).then_inc(s_const, 16)
                    eng.dma_start(mask[:, :, :], mask_d).then_inc(s_const, 16)

            def cycle(g, last=False):
                for j in range(Q if last else PER):
                    what = ("wo", j) if j < Q else ("w", j - Q)
                    if j < RING:
                        eng.wait_ge(s_wlo, lo_of(g, j + 1))
                    elif j < PER - 1:
                        h = j - RING
                        eng.wait_ge(s_wolo[h // 2], 2 * g + h % 2 + 1)
                    else:
                        eng.wait_ge(s_wlo, lo_of(g + 1, 0))
                    src = wo_d[bass.ds(g, 1), :, j, :] if j < Q else \
                        wq_d[bass.ds(g + 1, 1), :, j - Q, :] if j < Q + K else (wk_d if j == Q + K else wv_d)[bass.ds(g + 1, 1)]
                    eng.dma_start(stage[:, slot(what), :], src.rearrange("a p n -> (a p) n")).then_inc(s_piece[slot(what)], 16)

            cycle(0)
            with eng.Fori(1, G - 1) as g:
                cycle(g)
            cycle(G - 1, last=True)

        def split_target(what):
            kind, j = what
            return [t[:, j, :] for t in (wo if kind == "wo" else w)]

        @block.scalar
        def _(eng):
            def tile_hi(H, half, j):
                r = 5 * H + j
                eng.wait_ge(s_sum, r + 1)
                eng.activation(where(half, j)[0], t1[:, j % 2, :].rearrange("p (b s) -> p b s", s=S),
                               ACT.Copy).then_inc(s_qhi, 1)

            def value_out(H):
                eng.wait_ge(s_pj, TILES * H + V + 1)
                eng.wait_ge(s_sum, 5 * H + V - 1)
                eng.activation(vt, pj[V % 2][:, :], ACT.Copy).then_inc(s_vt, 1)

            def value_hi(H, half):
                eng.wait_ge(s_vp, H + 1)
                eng.activation(v[0][:, 4 * half:4 * half + 4, :], vp[:, :].rearrange("p (b d) -> p b d", b=4),
                               ACT.Copy).then_inc(s_vhi, 1)

            def step(g, s):
                n = B * g + s
                H = half_cycle(g, s)
                u, half = s % 4, 1 - s // 4
                if live(g, s, 2):
                    eng.wait_ge(s_tp, n - 1)
                    wait(eng, s_pv, n - 2)
                    eng.activation(pT[0][:, :], tp[:, :], ACT.Copy).then_inc(s_phi, 1)
                if u == 0 and live(g, s):
                    value_hi(H - 1, 1 - half)
                if projects(g, s):
                    for j in STEPS.get(u - 1, ()):
                        if j < V:
                            tile_hi(H, half, j)
                if live(g, s):
                    eng.wait_ge(s_ntop, n + 1)
                    wait(eng, s_rden, n - 1)
                    for h in range(Q):
                        e = prob[:, s % 2, h * S:(h + 1) * S]
                        last = eng.activation(e, e, ACT.Exp, bias=ntop[:, s % 2, h:h + 1], scale=1.0,
                                              accum_out=total[:, s % 2, h:h + 1])
                    last.then_inc(s_exp, 1)
                if live(g, s, 2):
                    eng.wait_ge(s_pv, n - 1)
                    wait(eng, s_y, n - 2)
                    eng.activation(o[0][:, :], ov[:, :], ACT.Copy).then_inc(s_ohi, 1)
                for what in splits(g, s):
                    landed(eng, g, what)
                    if what[0] == "wo":
                        wait(eng, s_y, B * g)
                    else:
                        eng.wait_ge(s_pj, TILES * (2 * g + 1) + what[1] + 1)
                    eng.activation(split_target(what)[0], stage[:, slot(what), :], ACT.Copy).then_inc(s_whi, 1)
                if projects(g, s) and u == 3:
                    value_out(H)

            for n in range(NX):
                eng.wait_ge(s_piece[n % RING], 16 * (n // RING + 1))
                eng.activation(cT[0][:, n // 2, n % 2 * HALF:(n % 2 + 1) * HALF], stage[:, n % RING, :],
                               ACT.Copy).then_inc(s_chi, 1)
                if n >= RING - 1:
                    for b in range(2 * (n - RING + 1), 2 * (n - RING + 2)):
                        norm.hi(eng, b)
            for j in range(TILES):
                n = NX + j
                eng.wait_ge(s_piece[n % RING], 16 * (n // RING + 1))
                eng.activation(w[0][:, j, :], stage[:, n % RING, :], ACT.Copy).then_inc(s_whi, 1)
            for j in range(V):
                tile_hi(0, 0, j)
            value_out(0)
            loop(eng, step)

        @block.tensor
        def _(eng):
            def project(H, g, half, j):
                i = TILES * H + j
                eng.wait_ge(s_whi, PER * g + j + 1)
                eng.wait_ge(s_wlo, lo_of(g, j))
                if j == 0:
                    wait(eng, s_sin, 5 * H)
                elif j == 1:
                    wait(eng, s_vt, H)
                else:
                    eng.wait_ge(s_sin, 5 * H + j - 1)
                cols = slice(half * HALF, (half + 1) * HALF)
                for c in range(C):
                    mm = product(eng, pj[j % 2][:, :], [t[:, j, c * P:(c + 1) * P] for t in w],
                                 [t[:, c, cols] for t in (xT if j < K else cT)], c == 0, c == C - 1)
                mm.then_inc(s_pj, 1)

            def turn_values(H):
                eng.wait_ge(s_vt, H + 1)
                wait(eng, s_vlo, H)
                for t in range(4):
                    mm = eng.transpose(vp[:, t * P:(t + 1) * P], vt[:, t * S:(t + 1) * S], ident)
                mm.then_inc(s_vp, 1)

            def step(g, s):
                n = B * g + s
                H = half_cycle(g, s)
                u, half = s % 4, 1 - s // 4
                if live(g, s, 2):
                    eng.wait_ge(s_norm, n - 1)
                    wait(eng, s_plo, n - 2)
                    for h in range(Q):
                        mm = eng.transpose(tp[:, h * S:(h + 1) * S], prob[:, s % 2, h * S:(h + 1) * S], ident)
                    mm.then_inc(s_tp, 1)
                if live(g, s):
                    if u == 0:
                        eng.wait_ge(s_qlo, 5 * H)
                    wait(eng, s_top, n)
                    tok = slice(s * S, (s + 1) * S)
                    for h in range(Q):
                        out = sc[:, h // 2, h % 2, :, :].rearrange("p j s -> p (j s)")
                        both = k[:, s, :, :].rearrange("p j s -> p (j s)")
                        eng.matmul(out, q[0][:, h, tok], both, start=True, stop=False)
                        mm = eng.matmul(out[:, 0:S], q[1][:, h, tok], both[:, 0:S], start=False, stop=True)
                    mm.then_inc(s_sc, 1)
                if u == 0 and live(g, s):
                    turn_values(H - 1)
                if live(g, s, 3):
                    m = n - 3
                    eng.wait_ge(s_ohi, m + 1)
                    eng.wait_ge(s_olo, m + 1)
                    wait(eng, s_add, m)
                    if s == 3:
                        for i in range(2):
                            eng.wait_ge(s_wolo[i], 2 * (g + 1))
                    for h in range(Q):
                        mm = product(eng, yb[:, :], [t[:, h * S:(h + 1) * S] for t in o],
                                     [t[:, h, :] for t in wo], h == 0, h == Q - 1)
                    mm.then_inc(s_y, 1)
                if live(g, s, 2):
                    m = n - 2
                    eng.wait_ge(s_phi, m + 1)
                    eng.wait_ge(s_plo, m + 1)
                    wait(eng, s_olo, m)
                    if u == 2:
                        eng.wait_ge(s_vlo, 2 * g + 1 + s // 4)
                    mm = product(eng, ov[:, :], [t[:, (s - 2) % B, :] for t in v], [t[:, :] for t in pT], True, True)
                    mm.then_inc(s_pv, 1)
                if projects(g, s):
                    for j in STEPS[u]:
                        project(H, g + s // 4, half, j)

            for b in range(B):
                norm.transpose(eng, b)
            eng.wait_ge(norm.s_lo, B)
            eng.wait_ge(s_clo, NX)
            for j in range(TILES):
                project(0, 0, 0, j)
            loop(eng, step)

        @block.vector
        def _(eng):
            def rotate(H, j):
                r = 5 * H + j
                bank = pj[j % 2]
                cos, sin = (trig[:, 2 * (j == K) + i, :].unsqueeze(1).broadcast_to([P, 4, S]) for i in range(2))
                split = lambda t: t.rearrange("p (b s) -> p b s", b=4)
                eng.wait_ge(s_pj, TILES * H + j + 1)
                wait(eng, s_qlo, r if j == 0 else r - 2 if j == 1 else r - 1)
                eng.tensor_tensor(split(t1[:, j % 2, :]), split(bank[:, :]), cos, ALU.mult).then_inc(s_cos, 1)
                if j == V % 2:
                    wait(eng, s_vp, H)
                eng.tensor_tensor(split(t2[0:64, j % 2, :]), split(bank[64:128, :]), sin[0:64], ALU.mult)
                eng.tensor_tensor(split(t2[64:128, j % 2, :]), split(bank[0:64, :]), sin[64:128], ALU.mult).then_inc(s_sin, 1)

            def step(g, s):
                n = B * g + s
                H = half_cycle(g, s)
                u, half = s % 4, 1 - s // 4
                if live(g, s, 1):
                    eng.wait_ge(s_exp, n)
                    wait(eng, s_norm, n - 2)
                    eng.reciprocal(rden[:, (s - 1) % 2, :], total[:, (s - 1) % 2, :]).then_inc(s_rden, 1)
                if live(g, s, 2):
                    eng.wait_ge(s_phi, n - 1)
                    eng.tensor_tensor(pT[1][:, :], tp[:, :], pT[0][:, :].bitcast(F32), ALU.subtract).then_inc(s_plo, 1)
                if live(g, s):
                    eng.wait_ge(s_sc, n + 1)
                    wait(eng, s_tp, n - 1)
                    heads = prob[:, s % 2, :].rearrange("p (a h s) -> p a h s", a=2, h=2)
                    for a in range(2):
                        added = eng.tensor_tensor(heads[:, a], sc[:, a, :, 1, :],
                                                  mask[:, s, :].unsqueeze(1).broadcast_to([P, 2, S]), ALU.add)
                    added.then_inc(s_masked, 1)
                    eng.wait_ge(s_masked, n + 1)
                    eng.memset(carrier[:, :], 0.0)
                    for h in range(Q):
                        last = eng.tensor_tensor_reduce(
                            prob[:, s % 2, h * S:(h + 1) * S], sc[:, h // 2, h % 2, 0, :],
                            prob[:, s % 2, h * S:(h + 1) * S], 1.0, -3.4e38, ALU.add, ALU.max,
                            top[:, s % 2, h:h + 1])
                    last.then_inc(s_top, 1)
                    eng.wait_ge(s_top, n + 1)
                    wait(eng, s_exp, n - 1)
                    eng.tensor_scalar(ntop[:, s % 2, :], top[:, s % 2, :], -1.0, None, ALU.mult).then_inc(s_ntop, 1)
                if u == 0 and live(g, s):
                    eng.wait_ge(s_vhi, H)
                    vs = [t[:, 4 * (1 - half):4 * (1 - half) + 4, :] for t in v]
                    eng.tensor_tensor(vs[1], vp[:, :].rearrange("p (b d) -> p b d", b=4), vs[0].bitcast(F32),
                                      ALU.subtract).then_inc(s_vlo, 1)
                if live(g, s, 3):
                    m = n - 3
                    b = (s - 3) % B
                    eng.wait_ge(s_y, m + 1)
                    eng.tensor_tensor(y[:, b, :], yb[:, :], y[:, b, :], ALU.add).then_inc(s_add, 1)
                if live(g, s, 2):
                    eng.wait_ge(s_ohi, n - 1)
                    eng.tensor_tensor(o[1][:, :], ov[:, :], o[0][:, :].bitcast(F32), ALU.subtract).then_inc(s_olo, 1)
                for what in splits(g, s):
                    if what in (("wo", 0), ("wo", 1)):
                        eng.wait_ge(s_whi, TILES + PER * g + what[1] + 1)
                        hi, lo = split_target(what)
                        eng.tensor_tensor(lo, stage[:, slot(what), :], hi.bitcast(F32), ALU.subtract).then_inc(s_wolo[0], 1)
                if projects(g, s):
                    for j in STEPS[u]:
                        if j < V:
                            rotate(H, j)

            for b in range(B):
                norm.statistics(eng, b)
            norm.moments_of_all(eng)
            for n in range(NX):
                eng.wait_ge(s_chi, n + 1)
                hi, lo = (t[:, n // 2, n % 2 * HALF:(n % 2 + 1) * HALF] for t in cT)
                eng.tensor_tensor(lo, stage[:, n % RING, :], hi.bitcast(F32), ALU.subtract).then_inc(s_clo, 1)
                if n == 1:
                    for b in range(4):
                        norm.normalise(eng, b)
                if n >= RING - 1:
                    for b in range(2 * (n - RING + 1), 2 * (n - RING + 2)):
                        norm.lo(eng, b)
                        if b < 4:
                            norm.normalise(eng, b + 4)
            eng.wait_ge(s_const, 32)
            for j in range(V):
                rotate(0, j)
            loop(eng, step)

        @block.gpsimd
        def _(eng):
            norm.roots(eng)

            def tile_sum(H, j):
                r = 5 * H + j
                eng.wait_ge(s_cos, r + 1)
                eng.wait_ge(s_sin, r + 1)
                eng.tensor_tensor(t1[:, j % 2, :], t1[:, j % 2, :], t2[:, j % 2, :], ALU.add).then_inc(s_sum, 1)

            def tile_lo(H, half, j):
                eng.wait_ge(s_qhi, 5 * H + j + 1)
                hi, lo = where(half, j)
                eng.tensor_tensor(lo, t1[:, j % 2, :].rearrange("p (b s) -> p b s", s=S), hi.bitcast(F32),
                                  ALU.subtract).then_inc(s_qlo, 1)

            def step(g, s):
                n = B * g + s
                H = half_cycle(g, s)
                u, half = s % 4, 1 - s // 4
                if live(g, s, 1):
                    eng.wait_ge(s_rden, n)
                    e = prob[:, (s - 1) % 2, :].rearrange("p (h s) -> p h s", h=Q)
                    eng.tensor_tensor(e, e, rden[:, (s - 1) % 2, :].unsqueeze(2).broadcast_to([P, Q, S]),
                                      ALU.mult).then_inc(s_norm, 1)
                if projects(g, s):
                    for j in STEPS.get(u - 1, ()):
                        if j < V:
                            tile_lo(H, half, j)
                for what in splits(g, s):
                    if what not in (("wo", 0), ("wo", 1)):
                        kind, j = what
                        eng.wait_ge(s_whi, TILES + PER * g + (j if kind == "wo" else Q + j) + 1)
                        hi, lo = split_target(what)
                        eng.tensor_tensor(lo, stage[:, slot(what), :], hi.bitcast(F32),
                                          ALU.subtract).then_inc(s_wolo[1] if kind == "wo" else s_wlo, 1)
                if projects(g, s):
                    for j in STEPS[u]:
                        if j < V:
                            tile_sum(H, j)

            for j in range(TILES):
                eng.wait_ge(s_whi, j + 1)
                eng.tensor_tensor(w[1][:, j, :], stage[:, (NX + j) % RING, :], w[0][:, j, :].bitcast(F32),
                                  ALU.subtract).then_inc(s_wlo, 1)
            for j in range(V):
                tile_sum(0, j)
                tile_lo(0, 0, j)
            loop(eng, step)


def feed_forward(nc, up_d, down_d, fc1_d, fc2_d, expT_d, gate_d, gamma_d, beta_d, ident, power, xT, x2, out_d):
    M = 8
    L = 2
    E = 8
    RING = 4
    pieces = [("exp", 0), ("fc2", 0), ("fc2", 1)] + [("up", c) for c in range(2 * C)] + \
             [("fc1", c) for c in range(2)] + [("down", m) for m in range(M)]
    at = {p: n for n, p in enumerate(pieces)}
    MT = M + L
    BANKS = 3
    with ExitStack() as ctx:
        sb = lambda name, shape, dt=F32: ctx.enter_context(nc.sbuf_tensor("D_" + name, shape, dt))
        pb = lambda name: ctx.enter_context(nc.psum_tensor("D_" + name, [P, D], F32))
        sem = lambda name: ctx.enter_context(nc.semaphore("D_" + name))
        pair = lambda name, shape: [sb(name + s, shape, F32R) for s in ("h", "l")]
        stage = sb("stage", [P, RING, D])
        wexp, wfc2 = pair("exp", [P, 1, D]), pair("fc2", [P, L, D])
        wup = pair("up", [P, 2 * C, D])
        wfc1 = pair("fc1", [P, 2, D])
        wdown = pair("down", [P, M, D])
        wlat = pair("lat", [P, L, D])
        gate = sb("gate", [P, C * E])
        ghl = sb("ghl", [P, C, 2 * E], F32R)
        hT = pair("hT", [P, MT, HALF])
        pos = sb("pos", [P, 2, D])
        sq = sb("sq", [P, 2, D])
        gamma, beta = sb("gamma", [P, D]), sb("beta", [P, D])
        shared = sb("shared", [P, D])
        glo, logit = sb("glo", [P, E]), sb("logit", [P, E])
        best, route = sb("best", [P, E]), sb("route", [P, 1])
        z = sb("z", [P, 2, D])
        stats, moments, rstd = sb("stats", [P, 6]), sb("moments", [P, 2]), sb("rstd", [P, 1])
        acc = [pb(f"acc{i}") for i in range(BANKS)]
        dn = [pb("dn0"), pb("dn1")]
        rt, gt = pb("rt"), pb("gt")
        s_piece = [sem(f"piece{i}") for i in range(RING)]
        s_small = sem("small")
        s_hi, s_lo, s_ghi, s_glo = sem("hi"), sem("lo"), sem("ghi"), sem("glo")
        s_acc, s_pos, s_sq, s_thi, s_tlo = sem("acc"), sem("pos"), sem("sq"), sem("thi"), sem("tlo")
        s_gt, s_gcopy, s_logit, s_best, s_route = sem("gt"), sem("gcopy"), sem("logit"), sem("best"), sem("route")
        s_dn, s_shared, s_z, s_ln1, s_gamma, s_beta, s_res, s_ln2 = (
            sem(n) for n in ("dn", "shared", "z", "ln1", "gamma", "beta", "res", "ln2"))
        s_out = sem("out")
        ln_sems = (sem("stats"), sem("moments"), sem("var"), sem("rstd"))
        norm = Turn(nc, ctx, "DN", x2, xT, ident, power, [dn[0], dn[1], rt, gt])
        block = ctx.enter_context(nc.Block())
        target = {"exp": wexp, "fc2": wfc2, "up": wup, "fc1": wfc1, "down": wdown}
        source = {"exp": expT_d, "fc2": fc2_d, "up": up_d, "fc1": fc1_d, "down": down_d}

        tiles = [("lat", l, 0) for l in range(L)] + [(kind, m, h) for h in range(2)
                 for kind, m in [("up", m) for m in range(M)] + [("fc1", l) for l in range(L)]]
        number = {t: i for i, t in enumerate(tiles)}
        plain = [i for i, t in enumerate(tiles) if t[0] != "up"]

        def dest(t):
            kind, m, h = t
            return [x[:, m, :] for x in wlat] if kind == "lat" else \
                [x[:, m if kind == "up" else M + m, :] for x in hT]

        def rank(i):
            return sum(t[0] == "up" for t in tiles[:i + 1])

        def seq_after(h):
            return 4 * h

        @block.sync
        def _(eng):
            for n, (kind, j) in enumerate(pieces):
                wait(eng, s_lo, n - RING + 1)
                eng.dma_start(stage[:, n % RING, :], source[kind][:, j, :]).then_inc(s_piece[n % RING], 16)
                if n == 0:
                    for t, d in ((gate, gate_d), (gamma, gamma_d), (beta, beta_d)):
                        eng.dma_start(t[:, :], d).then_inc(s_small, 16)
            for b in range(B):
                eng.wait_ge(s_ln2, b + 1)
                eng.dma_start(out_d[b], x2[:, b, :]).then_inc(s_out, 16)
            eng.wait_ge(s_out, 16 * B)

        @block.scalar
        def _(eng):
            def piece_hi(n):
                kind, j = pieces[n]
                eng.wait_ge(s_piece[n % RING], 16 * (n // RING + 1))
                eng.activation(target[kind][0][:, j, :], stage[:, n % RING, :], ACT.Copy).then_inc(s_hi, 1)

            def relu(i):
                r = rank(i)
                eng.wait_ge(s_acc, i + 1)
                wait(eng, s_sq, r - 2)
                eng.activation(pos[:, r % 2, :], acc[i % BANKS][:, :], ACT.Relu).then_inc(s_pos, 1)

            def tile_hi(i):
                t = tiles[i]
                hi = dest(t)[0]
                if t[2] == 1:
                    eng.wait_ge(s_dn, 4)
                if t[0] == "up":
                    eng.wait_ge(s_sq, rank(i))
                    eng.activation(hi, sq[:, rank(i) % 2, :], ACT.Copy).then_inc(s_thi, 1)
                else:
                    eng.wait_ge(s_acc, i + 1)
                    eng.activation(hi, acc[i % BANKS][:, :], ACT.Copy).then_inc(s_thi, 1)

            def sequence(b):
                eng.wait_ge(s_gt, b + 1)
                wait(eng, s_logit, b)
                eng.activation(glo[:, :], gt[:, E:2 * E], ACT.Copy).then_inc(s_gcopy, 1)
                eng.wait_ge(s_dn, b + 1)
                wait(eng, s_z, b)
                eng.activation(shared[:, :], dn[b % 2][:, :], ACT.Copy).then_inc(s_shared, 1)

            eng.wait_ge(s_small, 48)
            eng.activation(ghl[:, :, 0:E], gate[:, :].rearrange("p (c e) -> p c e", c=C), ACT.Copy).then_inc(s_ghi, 1)
            for n in range(len(pieces)):
                piece_hi(n)
                if n == 2:
                    tile_hi(0)
                    tile_hi(1)
                if pieces[n][0] == "up":
                    norm.hi(eng, pieces[n][1])
                if pieces[n][0] == "down":
                    i = L + pieces[n][1]
                    relu(i)
                    if i > L:
                        tile_hi(i - 1)
            tile_hi(L + M - 1)
            for i in range(L + M, len(tiles)):
                if i == L + MT:
                    for b in range(4):
                        sequence(b)
                if tiles[i][0] == "up":
                    relu(i)
                    if tiles[i - 1][0] == "up":
                        tile_hi(i - 1)
                else:
                    if tiles[i - 1][0] == "up" and i >= L + MT:
                        tile_hi(i - 1)
                    tile_hi(i)
            for b in range(4, B):
                sequence(b)

        @block.tensor
        def _(eng):
            def tile(i):
                kind, m, h = tiles[i]
                out = acc[i % BANKS][:, :]
                j = i - BANKS
                if j >= 0:
                    if tiles[j][0] == "up":
                        eng.wait_ge(s_sq, rank(j))
                    else:
                        eng.wait_ge(s_tlo, j + 1)
                if kind == "lat":
                    eng.wait_ge(s_lo, at["fc2", 1] + 1)
                    for e in range(L):
                        mm = product(eng, out, [t[:, 0, e * 256 + m * P:e * 256 + (m + 1) * P] for t in wexp],
                                     [t[:, e, :] for t in wfc2], e == 0, e == L - 1)
                else:
                    for c in range(C):
                        if kind == "up":
                            eng.wait_ge(s_lo, at["up", 2 * c + m // 4] + 1)
                            st = [t[:, 2 * c + m // 4, m % 4 * P:(m % 4 + 1) * P] for t in wup]
                        else:
                            eng.wait_ge(s_lo, at["fc1", c // 2] + 1)
                            st = [t[:, c // 2, c % 2 * 256 + m * P:c % 2 * 256 + (m + 1) * P] for t in wfc1]
                        mm = product(eng, out, st, [t[:, c, h * HALF:(h + 1) * HALF] for t in xT], c == 0, c == C - 1)
                mm.then_inc(s_acc, 1)

            def sequence(b):
                h, tok, here = b // 4, slice(b * S, (b + 1) * S), slice(b % 4 * S, (b % 4 + 1) * S)
                wait(eng, s_logit, b)
                if b == 0:
                    eng.wait_ge(s_glo, 1)
                for c in range(C):
                    eng.matmul(gt[:, 0:2 * E], xT[0][:, c, tok], ghl[:, c, :], start=c == 0, stop=False)
                    mm = eng.matmul(gt[:, 0:E], xT[1][:, c, tok], ghl[:, c, 0:E], start=False, stop=c == C - 1)
                mm.then_inc(s_gt, 1)
                wait(eng, s_shared, b - 1)
                for m in range(M):
                    eng.wait_ge(s_lo, at["down", m] + 1)
                    eng.wait_ge(s_tlo, number["up", m, h] + 1)
                    product(eng, dn[b % 2][:, :], [t[:, m, here] for t in hT], [t[:, m, :] for t in wdown],
                            m == 0, m == M - 1)
                wait(eng, s_z, b)
                eng.wait_ge(s_tlo, number["fc1", L - 1, h] + 1)
                for l in range(L):
                    mm = product(eng, rt[:, :], [t[:, M + l, here] for t in hT], [t[:, l, :] for t in wlat],
                                 l == 0, l == L - 1)
                mm.then_inc(s_dn, 1)

            for i in range(L):
                tile(i)
            for b in range(B):
                norm.transpose(eng, b)
            eng.wait_ge(norm.s_lo, B)
            for i in range(L, L + MT):
                tile(i)
            for b in range(4):
                sequence(b)
            for i in range(L + MT, len(tiles)):
                tile(i)
            for b in range(4, B):
                sequence(b)

        @block.vector
        def _(eng):
            def piece_lo(n):
                kind, j = pieces[n]
                eng.wait_ge(s_hi, n + 1)
                hi, lo = (t[:, j, :] for t in target[kind])
                eng.tensor_tensor(lo, stage[:, n % RING, :], hi.bitcast(F32), ALU.subtract).then_inc(s_lo, 1)

            def square(i):
                r = rank(i)
                eng.wait_ge(s_pos, r)
                wait(eng, s_tlo, sq_free(i))
                eng.tensor_tensor(sq[:, r % 2, :], acc[i % BANKS][:, :], pos[:, r % 2, :], ALU.mult).then_inc(s_sq, 1)

            def sq_free(i):
                ups = [j for j in range(i) if tiles[j][0] == "up"]
                return ups[-2] + 1 if len(ups) > 1 else 0

            def tile_lo(i):
                t = tiles[i]
                hi, lo = dest(t)
                eng.wait_ge(s_thi, i + 1)
                src = sq[:, rank(i) % 2, :] if t[0] == "up" else acc[i % BANKS][:, :]
                eng.tensor_tensor(lo, src, hi.bitcast(F32), ALU.subtract).then_inc(s_tlo, 1)

            def sequence(b):
                eng.wait_ge(s_gcopy, b + 1)
                eng.tensor_tensor(logit[:, :], gt[:, 0:E], glo[:, :], ALU.add).then_inc(s_logit, 1)
                eng.wait_ge(s_logit, b + 1)
                eng.max(best[:, :], logit[:, :]).then_inc(s_best, 1)
                eng.wait_ge(s_best, b + 1)
                eng.tensor_tensor(route[:, :], best[:, 0:1], best[:, 1:2], ALU.add).then_inc(s_route, 1)
                eng.wait_ge(s_route, b + 1)
                eng.wait_ge(s_shared, b + 1)
                wait(eng, s_ln1, b)
                eng.scalar_tensor_tensor(out=z[:, 0, :], in0=rt[:, :], scalar=route[:, 0:1], in1=shared[:, :],
                                         op0=ALU.mult, op1=ALU.add).then_inc(s_z, 1)
                eng.wait_ge(s_z, b + 1)
                wait(eng, s_res, b)
                layer_norm(eng, z[:, 0, :], z[:, 1, :], stats[:, :], moments[:, :], rstd[:, :], ln_sems,
                           2 * b + 1).then_inc(s_ln1, 1)

            def finish(b):
                eng.wait_ge(s_beta, b + 1)
                eng.tensor_tensor(x2[:, b, :], x2[:, b, :], z[:, 1, :], ALU.add).then_inc(s_res, 1)
                eng.wait_ge(s_res, b + 1)
                layer_norm(eng, x2[:, b, :], x2[:, b, :], stats[:, :], moments[:, :], rstd[:, :], ln_sems,
                           2 * b + 2).then_inc(s_ln2, 1)

            eng.wait_ge(s_ghi, 1)
            eng.tensor_tensor(ghl[:, :, E:2 * E], gate[:, :].rearrange("p (c e) -> p c e", c=C),
                              ghl[:, :, 0:E].bitcast(F32), ALU.subtract).then_inc(s_glo, 1)
            for n in range(len(pieces)):
                piece_lo(n)
                if n == 0:
                    for b in range(B):
                        norm.statistics(eng, b)
                    norm.moments_of_all(eng)
                if n == 2:
                    tile_lo(0)
                    tile_lo(1)
                    for b in range(B):
                        norm.normalise(eng, b)
                if pieces[n][0] == "up":
                    norm.lo(eng, pieces[n][1])
                if pieces[n][0] == "down":
                    i = L + pieces[n][1]
                    square(i)
                    if i > L:
                        tile_lo(i - 1)
            tile_lo(L + M - 1)
            for i in range(L + M, len(tiles)):
                if i == L + MT:
                    for b in range(4):
                        sequence(b)
                        finish(b)
                if tiles[i][0] == "up":
                    square(i)
                    if tiles[i - 1][0] == "up":
                        tile_lo(i - 1)
                else:
                    if tiles[i - 1][0] == "up" and i >= L + MT:
                        tile_lo(i - 1)
                    tile_lo(i)
            for b in range(4, B):
                sequence(b)
                finish(b)

        @block.gpsimd
        def _(eng):
            norm.roots(eng)
            eng.wait_ge(s_small, 48)
            for b in range(B):
                inverse_root(eng, moments[:, :], rstd[:, :], power, ln_sems, 2 * b + 1)
                eng.wait_ge(s_ln1, b + 1)
                eng.tensor_tensor(z[:, 1, :], z[:, 1, :], gamma[:, :], ALU.mult).then_inc(s_gamma, 1)
                eng.wait_ge(s_gamma, b + 1)
                eng.tensor_tensor(z[:, 1, :], z[:, 1, :], beta[:, :], ALU.add).then_inc(s_beta, 1)
                inverse_root(eng, moments[:, :], rstd[:, :], power, ln_sems, 2 * b + 2)


def decoder_layer(nc, x_nat, xT0, ctxT, mask, wqkvT, bqk, bv, woutT, bout, wq, wk, wv, wo, gate, up, down, fc1, fc2,
                  expT, gamma, beta, alibi_d, trig, ident_d, out):
    with ExitStack() as ctx:
        sb = lambda name, shape, dt=F32: ctx.enter_context(nc.sbuf_tensor(name, shape, dt))
        ident = sb("ident", [P, P])
        power = sb("power", [P, 1])
        x1 = sb("x", [P, B, D])
        s_ident = ctx.enter_context(nc.semaphore("ident_landed"))
        with nc.Block() as block:
            @block.sync
            def _(eng):
                eng.dma_start(ident[:, :], ident_d).then_inc(s_ident, 16)
                eng.wait_ge(s_ident, 16)

            @block.vector
            def _(eng):
                eng.memset(power[:, :], -0.5)
        with ExitStack() as self_ctx:
            ssb = lambda name, shape: self_ctx.enter_context(nc.sbuf_tensor(name, shape, F32R))
            q, k = (ssb(n, [P, 2 * C, NT]) for n in ("q", "k"))
            vhl = ssb("vhl", [P, B, HS, 2 * DH])
            alibi = self_ctx.enter_context(nc.sbuf_tensor("alibi", [P, HS, S], F32))
            project_self(nc, xT0, wqkvT, bqk, bv, alibi_d, q, k, vhl, alibi)
            attend_self(nc, x_nat, woutT, bout, ident[:, :], q, k, vhl, alibi, x1)
        xT = [sb("xT" + s, [P, C, NT], F32R) for s in ("h", "l")]
        attend_cross(nc, ctxT, wq, wk, wv, wo, mask, trig, ident[:, :], power[:, :], xT, x1)
        feed_forward(nc, up, down, fc1, fc2, expT, gate, gamma, beta, ident[:, :], power[:, :], xT, x1, out)


def tables():
    import numpy as np
    slopes = (1.0 / np.power(np.float32(2.0), np.arange(1, HS + 1, dtype=np.float32) * np.float32(8 / HS))).astype(np.float32)
    bias = slopes[:, None] * np.arange(1 - S, 1, dtype=np.float32)[None, :]
    causal = np.arange(S)[:, None] >= np.arange(S)[None, :]
    alibi = np.where(causal[:, None, :], bias[None], np.float32(-1e9)).astype(np.float32)
    inv = (1.0 / np.float32(10000.0) ** (np.arange(0, P, 2, dtype=np.float32) / np.float32(P))).astype(np.float32)
    angle = (np.arange(S, dtype=np.float32)[:, None] * inv[None, :]).astype(np.float32).T
    cos, sin = np.cos(angle), np.sin(angle)
    cos = np.concatenate([cos, cos])
    sin = np.concatenate([-sin, sin])
    scale = np.sqrt(np.float32(P))
    trig = np.stack([cos / scale, sin / scale, cos, sin], 1).astype(np.float32)
    return alibi, trig, np.eye(P, dtype=np.float32)


def kernel(**inputs):
    import numpy as np
    import concourse.bacc as bacc
    from concourse.bass_utils import run_bass_kernel_spmd

    a = {n: np.asarray(v) for n, v in inputs.items()}
    rows = lambda w: w.reshape(-1, P, w.shape[1]).transpose(1, 0, 2)
    spread = lambda v: np.broadcast_to(v[None, :], (P, v.shape[0]))
    pre, xp, fp = "L0_attn_", "L0_xattn_", "L0_ffn_"
    alibi, trig, ident = tables()
    bqkv = a[pre + "b_qkv"]
    arrays = {
        "x_nat": a["x"].transpose(1, 0, 2),
        "xT": rows(a["x"].reshape(NT, D).T),
        "ctxT": rows(a["ctx_4096"].reshape(NT, D).T),
        "mask": a["mask_BxSxS2_ff0"].transpose(1, 0, 2),
        "wqkvT": rows(a[pre + "w_qkv"].T),
        "bqk": bqkv[:2 * D].reshape(2 * C, P).T,
        "bv": spread(bqkv[2 * D:]),
        "woutT": rows(a[pre + "w_out"].T),
        "bout": spread(a[pre + "b_out"]),
        "wq": a[xp + "wq"].reshape(C, P, NG, HG, P).transpose(2, 1, 3, 0, 4).reshape(NG, P, HG, C * P),
        "wk": a[xp + "wk"].reshape(C, P, NG, P).transpose(2, 1, 0, 3).reshape(NG, P, C * P),
        "wv": a[xp + "wv"].reshape(C, P, NG, P).transpose(2, 1, 0, 3).reshape(NG, P, C * P),
        "wo": a[xp + "wo"].reshape(NG, HG, P, D).transpose(0, 2, 1, 3),
        "gate": rows(a[fp + "gate_w"]).reshape(P, -1),
        "up": rows(a[fp + "up_w"]).reshape(P, 2 * C, D),
        "down": rows(a[fp + "down_w"]),
        "fc1": rows(a[fp + "fc1_w"]).reshape(P, 2, D),
        "fc2": rows(a[fp + "fc2_w"]),
        "expT": rows(a[fp + "expert_w"].T).reshape(P, 1, D),
        "gamma": spread(a[fp + "ln_gamma"]),
        "beta": spread(a[fp + "ln_beta"]),
        "alibi": alibi,
        "trig": trig,
        "ident": ident,
    }
    arrays = {n + "_dram": np.ascontiguousarray(v) for n, v in arrays.items()}
    nc = bacc.Bacc("TRN2", target_bir_lowering=False, num_devices=1)
    args = [nc.dram_tensor(n, v.shape, mybir.dt.from_np(v.dtype), kind="ExternalInput").ap() for n, v in arrays.items()]
    args.append(nc.dram_tensor("out_dram", (B, S, D), F32, kind="ExternalOutput").ap())
    decoder_layer(nc, *args)
    r = run_bass_kernel_spmd(nc, [arrays], core_ids=[0])
    return r.results[0]["out_dram"]
```

```python
from contextlib import ExitStack

import concourse.bass as bass
from concourse import mybir

F32 = mybir.dt.float32
F32R = mybir.dt.float32r
ALU = mybir.AluOpType
ACT = mybir.ActivationFunctionType
AX = mybir.AxisListType

P = 128
B = 8
S = 128
D = 512
C = D // P
NT = B * S
HALF = NT // 2
HS = 32
DH = D // HS
HG = 4
NG = 8
EPS = 1e-5

PASSES = ((0, 0), (0, 1), (1, 0))


def product(eng, out, stationary, moving, first, last):
    for n, (i, j) in enumerate(PASSES):
        mm = eng.matmul(out, stationary[i], moving[j], start=first and n == 0,
                        stop=last and n == len(PASSES) - 1)
    return mm


def mean_and_variance(eng, z, stats, moments, sems, count):
    s_stats, s_moments, s_var, _ = sems
    eng.bn_stats(stats, z).then_inc(s_stats, 1)
    eng.wait_ge(s_stats, count)
    eng.bn_aggr(moments, stats).then_inc(s_moments, 1)
    eng.wait_ge(s_moments, count)
    eng.tensor_scalar(moments[:, 1:2], moments[:, 1:2], EPS, None, ALU.add).then_inc(s_var, 1)


def layer_norm(eng, z, out, stats, moments, rstd, sems, count):
    mean_and_variance(eng, z, stats, moments, sems, count)
    eng.wait_ge(sems[3], count)
    return eng.tensor_scalar(out, z, moments[:, 0:1], rstd, ALU.subtract, ALU.mult)


def inverse_root(eng, moments, rstd, power, sems, count):
    eng.wait_ge(sems[2], count)
    eng.tensor_tensor(rstd, moments[:, 1:2], power, ALU.pow).then_inc(sems[3], 1)


class Turn:

    def __init__(self, nc, ctx, name, x_nat, ident, power):
        sb = lambda s, shape: ctx.enter_context(nc.sbuf_tensor(f"{name}_norm_{s}", shape, F32))
        sem = lambda s: ctx.enter_context(nc.semaphore(f"{name}_norm_{s}"))
        self.x, self.ident, self.power = x_nat, ident, power
        self.xT = self.banks = None
        self.stats, self.moments, self.rstd = sb("stats", [P, B, 6]), sb("moments", [P, B, 2]), sb("rstd", [P, B])
        self.s_stats, self.s_moments, self.s_var, self.s_rstd = sem("stats"), sem("moments"), sem("var"), sem("rstd")
        self.s_row, self.s_tp, self.s_hi, self.s_lo = sem("row"), sem("tp"), sem("hi"), sem("lo")

    def statistics(self, eng, b):
        eng.bn_stats(self.stats[:, b, :], self.x[:, b, :]).then_inc(self.s_stats, 1)

    def variances(self, eng, half):
        eng.wait_ge(self.s_stats, 4 * half + 4)
        for b in range(4 * half, 4 * half + 4):
            eng.bn_aggr(self.moments[:, b, :], self.stats[:, b, :]).then_inc(self.s_moments, 1)
        eng.wait_ge(self.s_moments, 4 * half + 4)
        var = self.moments[:, 4 * half:4 * half + 4, 1]
        eng.tensor_scalar(var, var, EPS, None, ALU.add).then_inc(self.s_var, 1)

    def normalise(self, eng, half):
        eng.wait_ge(self.s_rstd, half + 1)
        for b in range(4 * half, 4 * half + 4):
            eng.tensor_scalar(self.x[:, b, :], self.x[:, b, :], self.moments[:, b, 0:1], self.rstd[:, b:b + 1],
                              ALU.subtract, ALU.mult).then_inc(self.s_row, 1)

    def roots(self, eng, half):
        eng.wait_ge(self.s_var, half + 1)
        rows = slice(4 * half, 4 * half + 4)
        eng.tensor_tensor(self.rstd[:, rows], self.moments[:, rows, 1], self.power.broadcast_to([P, 4]),
                          ALU.pow).then_inc(self.s_rstd, 1)

    def transpose(self, eng, b):
        eng.wait_ge(self.s_row, b + 1)
        n = len(self.banks)
        if b >= n:
            eng.wait_ge(self.s_lo, b - n + 1)
        for c in range(C):
            mm = eng.transpose(self.banks[b % n][:, c * S:(c + 1) * S], self.x[:, b, c * P:(c + 1) * P], self.ident)
        mm.then_inc(self.s_tp, 1)

    def _tile(self, b, part):
        bank = self.banks[b % len(self.banks)][:, :].rearrange("p (c s) -> p c s", c=C)
        return bank, self.xT[part][:, :, b * S:(b + 1) * S]

    def hi(self, eng, b):
        eng.wait_ge(self.s_tp, b + 1)
        bank, out = self._tile(b, 0)
        eng.activation(out, bank, ACT.Copy).then_inc(self.s_hi, 1)

    def lo(self, eng, b):
        eng.wait_ge(self.s_hi, b + 1)
        bank, out = self._tile(b, 1)
        eng.tensor_tensor(out, bank, self._tile(b, 0)[1].bitcast(F32), ALU.subtract).then_inc(self.s_lo, 1)


class FirstPieces:
    RING = 5
    PIECES = [("w", j) for j in range(5)] + [("ctx", c) for c in range(C)] + [("w", 5)] + \
             [("ctx", C + c) for c in range(C)]

    def __init__(self, nc, ctx, stage, ctxT_d, wq_d, wk_d, wv_d):
        self.stage, self.ctxT_d = stage, ctxT_d
        self.w_d = [wq_d[0, :, j, :] for j in range(HG)] + [wk_d[0], wv_d[0]]
        self.s_piece = [ctx.enter_context(nc.semaphore(f"first_piece{i}")) for i in range(self.RING)]

    def load(self, eng, n):
        kind, j = self.PIECES[n]
        src = self.w_d[j] if kind == "w" else self.ctxT_d[:, j % C, j // C * HALF:(j // C + 1) * HALF]
        eng.dma_start(self.stage[:, n % self.RING, :], src).then_inc(self.s_piece[n % self.RING], 16)


class NextWeights:
    RING = 5
    PIECES = [("exp", 0), ("fc2", 0), ("fc2", 1)] + [("up", c) for c in range(2 * C)] + [("fc1", c) for c in range(2)]
    BASE = {"exp": 0, "fc2": 1, "fc1": 3}

    def __init__(self, nc, ctx, stage, w, cT, sources):
        sem = lambda s: ctx.enter_context(nc.semaphore(f"next_{s}"))
        self.stage, self.w, self.sources = stage, w, sources
        self.up = [t.rearrange("p c (h n) -> p (c h) n", h=2) for t in cT]
        self.s_piece = [sem(f"piece{i}") for i in range(self.RING)]
        self.s_hi, self.s_lo = sem("hi"), [sem("lo_pool"), sem("lo_vector")]

    def place(self, kind, j, lo):
        return self.up[lo][:, j, :] if kind == "up" else self.w[lo][:, self.BASE[kind] + j, :]

    def on_vector(self, n):
        return n % 3 == 2

    def wait_split(self, eng, count):
        for i in range(2):
            wait(eng, self.s_lo[i], sum(self.on_vector(n) == bool(i) for n in range(count)))

    def load(self, eng, n):
        kind, j = self.PIECES[n]
        self.wait_split(eng, n - self.RING + 1)
        eng.dma_start(self.stage[:, n % self.RING, :], self.sources[kind][:, j, :]).then_inc(self.s_piece[n % self.RING], 16)

    def hi(self, eng, n):
        eng.wait_ge(self.s_piece[n % self.RING], 16 * (n // self.RING + 1))
        eng.activation(self.place(*self.PIECES[n], 0), self.stage[:, n % self.RING, :], ACT.Copy).then_inc(self.s_hi, 1)

    def lo(self, eng, n):
        eng.wait_ge(self.s_hi, n + 1)
        eng.tensor_tensor(self.place(*self.PIECES[n], 1), self.stage[:, n % self.RING, :],
                          self.place(*self.PIECES[n], 0).bitcast(F32), ALU.subtract)\
           .then_inc(self.s_lo[self.on_vector(n)], 1)


def wait(eng, sem, value):
    if not isinstance(value, int) or value > 0:
        eng.wait_ge(sem, value)


def load_heads(eng, b, pair, q, k, qs, kd, s_load):
    cs, tok = slice(4 * pair, 4 * pair + 4), bass.ts(b, S)
    eng.dma_start(qs[:, cs, :].bitcast(F32), q[:, cs, tok].bitcast(F32)).then_inc(s_load[pair], 16)
    for r in range(8):
        rows = slice(r * DH, (r + 1) * DH)
        eng.dma_start(kd[rows, cs, r, :].bitcast(F32), k[rows, cs, tok].bitcast(F32)).then_inc(s_load[pair], 16)


def project_self(nc, xT_d, wqkv_d, bqk_d, bv_d, alibi_d, x_d, bout_d, ident_d, ident, power, q, k, vhl, slots,
                 x1, qs, kd, s_load):
    RING = 8
    NX = C * 2
    NW = C * 3
    pieces = [(kind, c, 0) for c in range(C) for kind in ("x", "w")] + \
             [("w", c, 1) for c in range(C)] + [("x", c, 1) for c in range(C)] + \
             [("w", c, 2) for c in range(C)]
    at = {p: n for n, p in enumerate(pieces)}
    tiles = [("qk", m, h) for h, part in ((0, 0), (0, 1), (1, 0), (1, 1)) for m in range(part * C, part * C + C)] + \
            [("v", b, 0) for b in range(B)]
    order = tiles
    Q_DONE = 3 * C
    BANKS = 4
    with ExitStack() as ctx:
        sb = lambda name, shape, dt=F32: ctx.enter_context(nc.sbuf_tensor("A_" + name, shape, dt))
        sem = lambda name: ctx.enter_context(nc.semaphore("A_" + name))
        xT = [sb("xT" + s, [P, C, NT], F32R) for s in ("h", "l")]
        bout = sb("bout", [P, D])
        bqk = sb("bqk", [P, 2 * C])
        bv = sb("bv", [P, D])
        val = sb("val", [P, 2, D])
        acc = [ctx.enter_context(nc.psum_tensor(f"A_acc{i}", [P, D], F32)) for i in range(BANKS)]
        s_piece = [sem(f"piece{i}") for i in range(RING)]
        s_ident, s_alibi, s_x, s_zero = (sem(n) for n in ("ident", "alibi", "x", "zero"))
        s_bias, s_hi, s_lo, s_acc = sem("bias"), sem("hi"), sem("lo"), sem("acc")
        s_val, s_vhi, s_vlo = sem("val"), sem("vhi"), sem("vlo")
        block = ctx.enter_context(nc.Block())

        def weights(part, c, lo):
            return kd[:, (0 if part == 1 else C) + c, 4 * lo:4 * lo + 4, :].rearrange("p r s -> p (r s)")

        def place(piece, lo):
            kind, c, n = piece
            return weights(n, c, lo) if kind == "w" else xT[lo][:, c, n * D:(n + 1) * D]

        AHEAD = 12

        def pieces_with(i):
            return [AHEAD + i] if i < C else [AHEAD + C + i - Q_DONE - 1] if 0 <= i - Q_DONE - 1 < C else []

        @block.sync
        def _(eng):
            for n, piece in enumerate(pieces):
                if n >= RING:
                    eng.wait_ge(s_lo, n - RING + 1)
                src = xT_d if piece[0] == "x" else wqkv_d
                eng.dma_start(slots[n % RING], src[:, piece[1], piece[2] * D:(piece[2] + 1) * D])\
                   .then_inc(s_piece[n % RING], 16)
                if n == RING:
                    eng.dma_start(bqk[:, :], bqk_d).then_inc(s_bias, 16)
                    eng.dma_start(bv[:, :], bv_d).then_inc(s_bias, 16)
                if n == AHEAD:
                    eng.dma_start(ident, ident_d).then_inc(s_ident, 16)
                    eng.dma_start(bout[:, :], bout_d).then_inc(s_x, 16)
                    eng.dma_start(x1[:, :, :], x_d).then_inc(s_x, 16)
            eng.wait_ge(s_lo, len(pieces))
            for n in range(NG):
                eng.dma_start(slots[n], alibi_d[:, n, :]).then_inc(s_alibi, 16)
            eng.wait_ge(s_zero, 1)
            eng.wait_ge(s_vhi, 4 * C)
            eng.wait_ge(s_vlo, 4 * C)
            load_heads(eng, 0, 0, q, k, qs, kd, s_load)
            eng.wait_ge(s_ident, 16)
            eng.wait_ge(s_alibi, 16 * NG)

        @block.scalar
        def _(eng):
            def piece_hi(n):
                eng.wait_ge(s_piece[n % RING], 16 * (n // RING + 1))
                if pieces[n][0] == "w" and pieces[n][2] == 2:
                    eng.wait_ge(s_acc, Q_DONE)
                eng.activation(place(pieces[n], 0), slots[n % RING], ACT.Copy).then_inc(s_hi, 1)

            def tile_hi(i):
                kind, m, h = order[i]
                eng.wait_ge(s_val, i + 1)
                src = val[:, i % 2, :]
                if kind == "qk":
                    dst = (q if m < C else k)[:, 2 * (m % C), h * HALF:(h + 1) * HALF]
                else:
                    dst = vhl[:, m, :, 0:DH]
                    src = src.rearrange("p (h d) -> p h d", d=DH)
                eng.activation(dst, src, ACT.Copy).then_inc(s_vhi, 1)

            for n in range(AHEAD):
                piece_hi(n)
            for i in range(len(order)):
                for n in pieces_with(i):
                    piece_hi(n)
                tile_hi(i)

        @block.tensor
        def _(eng):
            def chunk(i, c):
                kind, m, h = order[i]
                if kind == "qk":
                    eng.wait_ge(s_lo, max(at["w", c, m // C], at["x", c, h]) + 1)
                    st = [weights(m // C, c, j)[:, m % C * P:(m % C + 1) * P] for j in range(2)]
                    mv = [t[:, c, h * HALF:(h + 1) * HALF] for t in xT]
                else:
                    eng.wait_ge(s_lo, at["w", c, 2] + 1)
                    st = [t[:, c, m * S:(m + 1) * S] for t in xT]
                    mv = [weights(2, c, j) for j in range(2)]
                mm = product(eng, acc[i % BANKS][:, :], st, mv, c == 0, c == C - 1)
                if c == C - 1:
                    mm.then_inc(s_acc, 1)

            for c in range(C):
                for i in range(BANKS):
                    chunk(i, c)
            for i in range(BANKS, len(order)):
                eng.wait_ge(s_val, i - BANKS + 1)
                for c in range(C):
                    chunk(i, c)

        @block.vector
        def _(eng):
            def piece_lo(n):
                eng.wait_ge(s_hi, n + 1)
                eng.tensor_tensor(place(pieces[n], 1), slots[n % RING], place(pieces[n], 0).bitcast(F32),
                                  ALU.subtract).then_inc(s_lo, 1)

            def tile(i):
                kind, m, h = order[i]
                eng.wait_ge(s_acc, i + 1)
                if i >= 2:
                    eng.wait_ge(s_vlo, i - 1)
                out = val[:, i % 2, :]
                if i == 0:
                    eng.wait_ge(s_bias, 32)
                if kind == "v":
                    eng.tensor_tensor(out, acc[i % BANKS][:, :], bv[:, :], ALU.add).then_inc(s_val, 1)
                elif m < C:
                    eng.tensor_scalar(out, acc[i % BANKS][:, :], bqk[:, m:m + 1], DH ** -0.5,
                                      ALU.add, ALU.mult).then_inc(s_val, 1)
                else:
                    eng.tensor_scalar(out, acc[i % BANKS][:, :], bqk[:, m:m + 1], None,
                                      ALU.add).then_inc(s_val, 1)

            for n in range(AHEAD):
                piece_lo(n)
            for i in range(len(order)):
                for n in pieces_with(i):
                    piece_lo(n)
                tile(i)
                if i == 4 * C:
                    eng.memset(kd[:, 0:C, :, :].bitcast(F32), 0.0).then_inc(s_zero, 1)

        @block.gpsimd
        def _(eng):
            eng.memset(power, -0.5)
            for i, (kind, m, h) in enumerate(order):
                eng.wait_ge(s_vhi, i + 1)
                src = val[:, i % 2, :]
                if kind == "qk":
                    t = q if m < C else k
                    hi, lo = (t[:, 2 * (m % C) + j, h * HALF:(h + 1) * HALF] for j in range(2))
                else:
                    src = src.rearrange("p (h d) -> p h d", d=DH)
                    hi, lo = vhl[:, m, :, 0:DH], vhl[:, m, :, DH:2 * DH]
                eng.tensor_tensor(lo, src, hi.bitcast(F32), ALU.subtract).then_inc(s_vlo, 1)
                if i % 2 == 1 and i // 2 in range(2, 2 + B):
                    b = i // 2 - 2
                    eng.wait_ge(s_x, 32)
                    eng.tensor_tensor(x1[:, b, :], x1[:, b, :], bout[:, :], ALU.add)


def attend_self(nc, wout_d, ident, q, k, vhl, slots, x1, qs, kd, s_load, norm, first):
    LT, LV = 2, 4
    NS = B * NG
    PAIR = NG // 2
    LOADS = 16 * (8 + 1)
    with ExitStack() as ctx:
        sb = lambda name, shape, dt=F32: ctx.enter_context(nc.sbuf_tensor("B_" + name, shape, dt))
        pb = lambda name: ctx.enter_context(nc.psum_tensor("B_" + name, [P, D], F32))
        sem = lambda name: ctx.enter_context(nc.semaphore("B_" + name))
        wout = [sb("wout" + s, [P, C, D], F32R) for s in ("h", "l")]
        prob = sb("prob", [P, 4, HG * S])
        pT = [sb("pT" + s, [P, 2, HG * S], F32R) for s in ("h", "l")]
        top = sb("top", [P, 2, HG])
        carrier = sb("carrier", [P, 1])
        ntop = sb("ntop", [P, 4, HG])
        total = sb("total", [P, HS])
        rden = sb("rden", [P, HS])
        ohl = sb("ohl", [P, 16, DH])
        o = sb("o", [P, HS, DH])
        oT = [sb("oT" + s, [P, C, S], F32R) for s in ("h", "l")]
        wst = sb("wst", [P, D])
        sc = [pb("sc0"), pb("sc1")]
        tp = [pb("tp0"), pb("tp1")]
        ov = [pb("ov0"), pb("ov1")]
        ot, yb = pb("ot"), pb("yb")
        s_zero, s_wst, s_whi, s_wlo = sem("zero"), sem("wst"), sem("whi"), sem("wlo")
        s_sc, s_top, s_ntop, s_exp = sem("sc"), sem("top"), sem("ntop"), sem("exp")
        s_tp, s_phi, s_plo, s_pv = sem("tp"), sem("phi"), sem("plo"), sem("pv")
        s_rden, s_ohl, s_oadd, s_o = sem("rden"), sem("ohl"), sem("oadd"), sem("o")
        s_ot, s_ohi, s_olo, s_y, s_z = sem("ot"), sem("ohi"), sem("olo"), sem("y"), sem("z")
        block = ctx.enter_context(nc.Block())

        SPLIT = [(0, 4), (0, 7), (1, 1), (1, 3)]

        def live(b, G, lag=0):
            return not isinstance(b, int) or 0 <= NG * b + G - lag < NS

        def follows(b):
            return not isinstance(b, int) or 1 <= b <= B

        def loop(eng, step):
            for b in range(3):
                for G in range(NG):
                    step(b, G)
            with eng.Fori(3, B) as b:
                for G in range(NG):
                    step(b, G)
            for G in range(NG):
                step(B, G)
            step(B + 1, 0)

        @block.sync
        def _(eng):
            def load(b, pair):
                eng.wait_ge(s_sc, NG * (b - 1) + PAIR * (pair + 1))
                load_heads(eng, b, pair, q, k, qs, kd, s_load)

            eng.wait_ge(s_zero, 2)
            load_heads(eng, 0, 1, q, k, qs, kd, s_load)
            for b in range(1, 3):
                for pair in range(2):
                    load(b, pair)
            with eng.Fori(3, B) as b:
                for pair in range(2):
                    load(b, pair)
            eng.wait_ge(s_top, NS - 3)
            for n in range(first.RING):
                first.load(eng, n)

        @block.gpsimd
        def _(eng):
            eng.memset(kd[:, C:C + 2, :, :].bitcast(F32), 0.0).then_inc(s_zero, 1)
            for c in range(C):
                if c:
                    eng.wait_ge(s_wlo, c)
                eng.dma_start(wst[:, :], wout_d[:, c, :]).then_inc(s_wst, 16)
            norm.roots(eng, 0)

        @block.scalar
        def _(eng):
            def step(b, G):
                n = NG * b + G
                if G in (0, 4) and follows(b):
                    eng.wait_ge(s_pv, n - LV)
                    wait(eng, s_oadd, 2 * b - 2 + G // 4)
                    eng.activation(ohl[:, :, :],
                                   ov[G // 4][:, :].rearrange("p (h t d) -> p h t d", t=2, d=DH)[:, :, 1, :],
                                   ACT.Copy).then_inc(s_ohl, 1)
                if G == 6 and follows(b):
                    eng.wait_ge(s_ot, b)
                    wait(eng, s_y, b - 1)
                    eng.activation(oT[0][:, :, :], ot[:, :].rearrange("p (c s) -> p c s", c=C),
                                   ACT.Copy).then_inc(s_ohi, 1)
                if live(b, G, LT):
                    eng.wait_ge(s_tp, n - LT + 1)
                    wait(eng, s_pv, n - LT - 1)
                    eng.activation(pT[0][:, G % 2, :], tp[G % 2][:, :], ACT.Copy).then_inc(s_phi, 1)
                if live(b, G):
                    eng.wait_ge(s_ntop, n + 1)
                    if G % 4 == 0:
                        wait(eng, s_rden, 2 * b - 1 + G // 4)
                    for h in range(HG):
                        e = prob[:, G % 4, h * S:(h + 1) * S]
                        last = eng.activation(e, e, ACT.Exp, bias=ntop[:, G % 4, h:h + 1], scale=1.0,
                                              accum_out=total[:, HG * G + h:HG * G + h + 1])
                    last.then_inc(s_exp, 1)
                if isinstance(b, int) and (b, G) in SPLIT:
                    c = SPLIT.index((b, G))
                    eng.wait_ge(s_wst, 16 * (c + 1))
                    eng.activation(wout[0][:, c, :], wst[:, :], ACT.Copy).then_inc(s_whi, 1)

            loop(eng, step)

        @block.tensor
        def _(eng):
            def step(b, G):
                n = NG * b + G
                if live(b, G):
                    if G % PAIR == 0:
                        eng.wait_ge(s_load[G // PAIR], LOADS * (b + 1))
                    wait(eng, s_top, n - 1)
                    c, cols = G // 2, slice(4 * (G % 2), 4 * (G % 2) + 4)
                    product(eng, sc[G % 2][:, :].rearrange("p (h s) -> p h s", h=HG), [qs[:, 2 * c + j, :] for j in range(2)],
                            [kd[:, 2 * c + j, cols, :] for j in range(2)], True, True).then_inc(s_sc, 1)
                if live(b, G, LV):
                    g, bb = (G - LV) % NG, b if G >= LV else b - 1
                    m = n - LV
                    eng.wait_ge(s_phi, m + 1)
                    eng.wait_ge(s_plo, m + 1)
                    if g % 4 == 0:
                        wait(eng, s_oadd, 2 * bb - 1 + g // 4)
                    for h in range(HG):
                        head = HG * g + h
                        at = (head % 16) * 2 * DH
                        out = ov[g // 4]
                        v = vhl[:, bass.ds(bb, 1), head, :].rearrange("p a d -> p (a d)")
                        eng.matmul(out[:, at:at + 2 * DH], pT[0][:, G % 2, h * S:(h + 1) * S], v,
                                   start=True, stop=False)
                        mm = eng.matmul(out[:, at:at + DH], pT[1][:, G % 2, h * S:(h + 1) * S], v[:, 0:DH],
                                        start=False, stop=True)
                    mm.then_inc(s_pv, 1)
                if live(b, G, LT):
                    m = n - LT
                    eng.wait_ge(s_exp, m + 1)
                    wait(eng, s_phi, m - 1)
                    wait(eng, s_plo, m - 1)
                    for h in range(HG):
                        mm = eng.transpose(tp[G % 2][:, h * S:(h + 1) * S],
                                           prob[:, (G - LT) % 4, h * S:(h + 1) * S], ident)
                    mm.then_inc(s_tp, 1)
                if G == 5 and follows(b):
                    eng.wait_ge(s_o, 2 * b)
                    wait(eng, s_olo, b - 1)
                    for c in range(C):
                        mm = eng.transpose(ot[:, c * P:(c + 1) * P],
                                           o[:, 8 * c:8 * c + 8, :].rearrange("p h d -> p (h d)"), ident)
                    mm.then_inc(s_ot, 1)
                if G == 0 and follows(b - 1):
                    eng.wait_ge(s_ohi, b - 1)
                    eng.wait_ge(s_olo, b - 1)
                    wait(eng, s_z, b - 2)
                    eng.wait_ge(s_wlo, C)
                    for c in range(C):
                        mm = product(eng, yb[:, :], [t[:, c, :] for t in oT], [t[:, c, :] for t in wout],
                                     c == 0, c == C - 1)
                    mm.then_inc(s_y, 1)

            loop(eng, step)

        @block.vector
        def _(eng):
            def step(b, G):
                n = NG * b + G
                if live(b, G):
                    eng.wait_ge(s_sc, n + 1)
                    wait(eng, s_tp, n - 3)
                    eng.memset(carrier[:, :], 0.0)
                    for h in range(HG):
                        last = eng.tensor_tensor_reduce(
                            prob[:, G % 4, h * S:(h + 1) * S], sc[G % 2][:, h * S:(h + 1) * S],
                            slots[G][:, h * S:(h + 1) * S], 1.0, -3e38, ALU.add, ALU.max, top[:, G % 2, h:h + 1])
                    last.then_inc(s_top, 1)
                    eng.wait_ge(s_top, n + 1)
                    wait(eng, s_exp, n - 3)
                    eng.tensor_scalar(ntop[:, G % 4, :], top[:, G % 2, :], -1.0, None, ALU.mult).then_inc(s_ntop, 1)
                if G in (0, 4) and live(b, G, 1):
                    half = 1 - G // 4
                    eng.wait_ge(s_exp, n)
                    eng.reciprocal(rden[:, 16 * half:16 * half + 16],
                                   total[:, 16 * half:16 * half + 16]).then_inc(s_rden, 1)
                if G in (0, 4) and follows(b):
                    half, done = G // 4, 2 * b - 1 + G // 4
                    heads = slice(16 * half, 16 * half + 16)
                    eng.wait_ge(s_ohl, done)
                    wait(eng, s_ot, b - 1)
                    eng.tensor_tensor(o[:, heads, :],
                                      ov[half][:, :].rearrange("p (h t d) -> p h t d", t=2, d=DH)[:, :, 0, :],
                                      ohl[:, :, :], ALU.add).then_inc(s_oadd, 1)
                    eng.wait_ge(s_oadd, done)
                    eng.wait_ge(s_rden, done)
                    eng.tensor_tensor(o[:, heads, :], o[:, heads, :],
                                      rden[:, heads].unsqueeze(2).broadcast_to([P, 16, DH]),
                                      ALU.mult).then_inc(s_o, 1)
                if live(b, G, LT):
                    m = n - LT
                    eng.wait_ge(s_phi, m + 1)
                    eng.tensor_tensor(pT[1][:, G % 2, :], tp[G % 2][:, :], pT[0][:, G % 2, :].bitcast(F32),
                                      ALU.subtract).then_inc(s_plo, 1)
                if G == 6 and follows(b):
                    eng.wait_ge(s_ohi, b)
                    eng.tensor_tensor(oT[1][:, :, :], ot[:, :].rearrange("p (c s) -> p c s", c=C),
                                      oT[0][:, :, :].bitcast(F32), ALU.subtract).then_inc(s_olo, 1)
                if isinstance(b, int) and (b, G) in SPLIT:
                    c = SPLIT.index((b, G))
                    eng.wait_ge(s_whi, c + 1)
                    eng.tensor_tensor(wout[1][:, c, :], wst[:, :], wout[0][:, c, :].bitcast(F32),
                                      ALU.subtract).then_inc(s_wlo, 1)
                if G == 0 and follows(b - 1):
                    eng.wait_ge(s_y, b - 1)
                    row = x1[:, bass.ds(b - 2, 1), :].rearrange("p a d -> p (a d)")
                    eng.tensor_tensor(row, yb[:, :], row, ALU.add).then_inc(s_z, 1)
                if isinstance(b, int) and b == B:
                    for i in {1: (0, 1), 5: (2, 3), 7: (4, 5, 6)}.get(G, ()):
                        eng.wait_ge(s_z, i + 1)
                        norm.statistics(eng, i)
                    if G == 5:
                        norm.variances(eng, 0)
                    if G == 7:
                        norm.normalise(eng, 0)
            eng.memset(kd[:, C + 2:2 * C, :, :].bitcast(F32), 0.0).then_inc(s_zero, 1)
            loop(eng, step)


def attend_cross(nc, first, wq_d, wk_d, wv_d, wo_d, mask_d, trig_d, ident, xT, cT, w, stage, y, norm, next_norm, weights):
    G, Q = NG, HG
    NS = G * B
    RING = first.RING
    STEPS = {0: (0, 1), 1: (2,), 2: (3, 4), 3: (5,)}
    K, V, TILES = 4, 5, 6
    PER = 10
    with ExitStack() as ctx:
        sb = lambda name, shape, dt=F32: ctx.enter_context(nc.sbuf_tensor("C_" + name, shape, dt))
        pb = lambda name: ctx.enter_context(nc.psum_tensor("C_" + name, [P, D], F32))
        sem = lambda name: ctx.enter_context(nc.semaphore("C_" + name))
        pair = lambda name, shape: [sb(name + s, shape, F32R) for s in ("h", "l")]
        q = pair("q", [P, Q, NT])
        k = sb("k", [P, B, 2, S], F32R)
        v = pair("v", [P, B, P])
        wo = pair("wo", [P, Q, D])
        o = pair("o", [P, Q * S])
        pT = pair("pT", [P, Q * S])
        prob = sb("prob", [P, 2, Q * S])
        t1 = sb("t1", [P, 2, D])
        t2 = sb("t2", [P, 2, D])
        trig = sb("trig", [P, 4, S])
        mask = sb("mask", [P, B, S])
        carrier = sb("carrier", [P, 1])
        top, ntop = sb("top", [P, 2, Q]), sb("ntop", [P, 2, Q])
        total, rden = sb("total", [P, 2, Q]), sb("rden", [P, 2, Q])
        sc = ctx.enter_context(nc.psum_tensor("C_sc", [P, 2, 2, 2, S], F32))
        tp, ov, yb, vp = pb("tp"), pb("ov"), pb("yb"), pb("vp")
        pj = [pb("pj0"), pb("pj1")]
        s_const = sem("const")
        s_piece = first.s_piece
        s_whi, s_wlo, s_wolo = sem("whi"), sem("wlo"), [sem("wolo0"), sem("wolo1")]
        s_chi, s_clo = sem("chi"), sem("clo")
        s_pj, s_cos, s_sin, s_sum, s_qhi, s_qlo = sem("pj"), sem("cos"), sem("sin"), sem("sum"), sem("qhi"), sem("qlo")
        s_vt, s_vp, s_vhi, s_vlo = sem("vt"), sem("vp"), sem("vhi"), sem("vlo")
        s_sc, s_top, s_ntop, s_exp, s_rden, s_norm = sem("sc"), sem("top"), sem("ntop"), sem("exp"), sem("rden"), sem("norm")
        s_tp, s_phi, s_plo, s_pv, s_ohi, s_olo = sem("tp"), sem("phi"), sem("plo"), sem("pv"), sem("ohi"), sem("olo")
        s_y, s_add, s_masked = sem("y"), sem("add"), sem("masked")
        NX = 2 * C
        FIRST = NX + TILES
        vt = t2[:, V % 2, :]
        norm.xT, norm.banks = xT, [tp, ov, yb, vp]
        block = ctx.enter_context(nc.Block())

        def live(g, s, lag=0):
            return not isinstance(g, int) or 0 <= B * g + s - lag < NS

        def loop(eng, step):
            for s in range(B):
                step(0, s)
            with eng.Fori(1, G - 1) as g:
                for s in range(B):
                    step(g, s)
            for g in (G - 1, G):
                for s in range(B):
                    step(g, s)

        def projects(g, s):
            return not isinstance(g, int) or g < G - 1 or (g == G - 1 and s < 4)

        def half_cycle(g, s):
            return 2 * g + 1 + s // 4

        def where(H_half, j):
            cols = slice(H_half * HALF, (H_half + 1) * HALF)
            return [t[:, j, cols].rearrange("p (b s) -> p b s", s=S) for t in q] if j < K else \
                [k[:, 4 * H_half:4 * H_half + 4, i, :] for i in range(2)]

        def lo_of(g, j):
            return TILES * g + j + 1

        SPLITS = {2: [("wo", h) for h in range(Q)] + [("w", 0)], 3: [("w", 1), ("w", 2)],
                  4: [("w", 3)], 5: [("w", K)], 6: [("w", V)]}

        def splits(g, s):
            return [x for x in SPLITS.get(s, ()) if not isinstance(g, int) or g < G - 1 or (g == G - 1 and x[0] == "wo")]

        def slot(what):
            kind, j = what
            return (FIRST + (j if kind == "wo" else Q + j)) % RING

        def next_pieces(g, s):
            first = 2 * (B * g + s - NS + 4) if isinstance(g, int) else -1
            return range(first, min(first + 2, len(weights.PIECES))) if first >= 0 else ()

        def landed(eng, g, what):
            kind, j = what
            at = FIRST + (j if kind == "wo" else Q + j)
            eng.wait_ge(s_piece[at % RING], 16 * (at // RING + 1 + (PER // RING) * g))

        @block.sync
        def _(eng):
            eng.dma_start(trig[:, :, :], trig_d).then_inc(s_const, 16)
            eng.dma_start(mask[:, :, :], mask_d).then_inc(s_const, 16)

            def wait_first(n):
                kind, j = first.PIECES[n]
                eng.wait_ge(s_wlo if kind == "w" else s_clo, j + 1)

            for n in range(RING, FIRST):
                wait_first(n - RING)
                first.load(eng, n)

            def cycle(g, last=False):
                for j in range(Q if last else PER):
                    what = ("wo", j) if j < Q else ("w", j - Q)
                    if j < RING and isinstance(g, int) and g == 0:
                        wait_first(FIRST + j - RING)
                    elif j < RING:
                        eng.wait_ge(s_wlo, lo_of(g, j + 1))
                    elif j < PER - 1:
                        h = j - RING
                        eng.wait_ge(s_wolo[h // 2], 2 * g + h % 2 + 1)
                    else:
                        eng.wait_ge(s_wlo, lo_of(g + 1, 0))
                    src = wo_d[bass.ds(g, 1), :, j, :] if j < Q else \
                        wq_d[bass.ds(g + 1, 1), :, j - Q, :] if j < Q + K else (wk_d if j == Q + K else wv_d)[bass.ds(g + 1, 1)]
                    eng.dma_start(stage[:, slot(what), :], src.rearrange("a p n -> (a p) n")).then_inc(s_piece[slot(what)], 16)

            cycle(0)
            with eng.Fori(1, G - 1) as g:
                cycle(g)
            cycle(G - 1, last=True)
            eng.wait_ge(s_wlo, TILES * G)
            for i in range(2):
                eng.wait_ge(s_wolo[i], 2 * G)
            for n in range(len(weights.PIECES)):
                weights.load(eng, n)

        def split_target(what):
            kind, j = what
            return [t[:, j, :] for t in (wo if kind == "wo" else w)]

        @block.scalar
        def _(eng):
            def tile_hi(H, half, j):
                r = 5 * H + j
                eng.wait_ge(s_sum, r + 1)
                eng.activation(where(half, j)[0], t1[:, j % 2, :].rearrange("p (b s) -> p b s", s=S),
                               ACT.Copy).then_inc(s_qhi, 1)

            def value_out(H):
                eng.wait_ge(s_pj, TILES * H + V + 1)
                eng.wait_ge(s_sum, 5 * H + V - 1)
                eng.activation(vt, pj[V % 2][:, :], ACT.Copy).then_inc(s_vt, 1)

            def value_hi(H, half):
                eng.wait_ge(s_vp, H + 1)
                eng.activation(v[0][:, 4 * half:4 * half + 4, :], vp[:, :].rearrange("p (b d) -> p b d", b=4),
                               ACT.Copy).then_inc(s_vhi, 1)

            def output_hi(g, s):
                n = B * g + s
                if live(g, s, 2):
                    eng.wait_ge(s_pv, n - 1)
                    wait(eng, s_y, n - 2)
                    eng.activation(o[0][:, :], ov[:, :], ACT.Copy).then_inc(s_ohi, 1)

            def step(g, s):
                n = B * g + s
                H = half_cycle(g, s)
                u, half = s % 4, 1 - s // 4
                if live(g, s, 2):
                    eng.wait_ge(s_tp, n - 1)
                    wait(eng, s_pv, n - 2)
                    eng.activation(pT[0][:, :], tp[:, :], ACT.Copy).then_inc(s_phi, 1)
                if u == 0 and live(g, s):
                    value_hi(H - 1, 1 - half)
                if projects(g, s):
                    for j in STEPS.get(u - 1, ()):
                        if j < V:
                            tile_hi(H, half, j)
                early = isinstance(g, int) and B * g + s >= NS - 4
                if early:
                    output_hi(g, s)
                if live(g, s):
                    eng.wait_ge(s_ntop, n + 1)
                    wait(eng, s_rden, n - 1)
                    for h in range(Q):
                        e = prob[:, s % 2, h * S:(h + 1) * S]
                        last = eng.activation(e, e, ACT.Exp, bias=ntop[:, s % 2, h:h + 1], scale=1.0,
                                              accum_out=total[:, s % 2, h:h + 1])
                    last.then_inc(s_exp, 1)
                if not early:
                    output_hi(g, s)
                for what in splits(g, s):
                    landed(eng, g, what)
                    if what[0] == "wo":
                        wait(eng, s_y, B * g)
                    else:
                        eng.wait_ge(s_pj, TILES * (2 * g + 1) + what[1] + 1)
                    eng.activation(split_target(what)[0], stage[:, slot(what), :], ACT.Copy).then_inc(s_whi, 1)
                if projects(g, s) and u == 3:
                    value_out(H)
                for n in next_pieces(g, s):
                    if n == 0:
                        eng.wait_ge(s_pj, 2 * TILES * G)
                    weights.hi(eng, n)

            def first_hi(n):
                kind, j = first.PIECES[n]
                eng.wait_ge(s_piece[n % RING], 16 * (n // RING + 1))
                if kind == "w":
                    eng.activation(w[0][:, j, :], stage[:, n % RING, :], ACT.Copy).then_inc(s_whi, 1)
                else:
                    eng.activation(cT[0][:, j % C, j // C * HALF:(j // C + 1) * HALF], stage[:, n % RING, :],
                                   ACT.Copy).then_inc(s_chi, 1)

            first_hi(0)
            first_hi(1)
            for b in range(4):
                norm.hi(eng, b)
            for n in range(2, RING):
                first_hi(n)
            for j in range(V):
                for n in {0: (5, 6), 1: (7, 8, 9), 2: (10, 11), 3: (12, 13)}.get(j, ()):
                    first_hi(n)
                tile_hi(0, 0, j)
            for b in range(4, B):
                norm.hi(eng, b)
            value_out(0)
            loop(eng, step)

        @block.tensor
        def _(eng):
            def project(H, g, half, j):
                i = TILES * H + j
                eng.wait_ge(s_whi, PER * g + j + 1)
                eng.wait_ge(s_wlo, lo_of(g, j))
                if j == 0:
                    wait(eng, s_sin, 5 * H)
                elif j == 1:
                    wait(eng, s_vt, H)
                else:
                    eng.wait_ge(s_sin, 5 * H + j - 1)
                cols = slice(half * HALF, (half + 1) * HALF)
                for c in range(C):
                    mm = product(eng, pj[j % 2][:, :], [t[:, j, c * P:(c + 1) * P] for t in w],
                                 [t[:, c, cols] for t in (xT if j < K else cT)], c == 0, c == C - 1)
                mm.then_inc(s_pj, 1)

            def turn_values(H):
                eng.wait_ge(s_vt, H + 1)
                wait(eng, s_vlo, H)
                for t in range(4):
                    mm = eng.transpose(vp[:, t * P:(t + 1) * P], vt[:, t * S:(t + 1) * S], ident)
                mm.then_inc(s_vp, 1)

            def step(g, s):
                n = B * g + s
                H = half_cycle(g, s)
                u, half = s % 4, 1 - s // 4
                if live(g, s, 2):
                    eng.wait_ge(s_norm, n - 1)
                    wait(eng, s_plo, n - 2)
                    for h in range(Q):
                        mm = eng.transpose(tp[:, h * S:(h + 1) * S], prob[:, s % 2, h * S:(h + 1) * S], ident)
                    mm.then_inc(s_tp, 1)
                if live(g, s):
                    if u == 0:
                        eng.wait_ge(s_qlo, 5 * H)
                    wait(eng, s_top, n)
                    tok = slice(s * S, (s + 1) * S)
                    for h in range(Q):
                        out = sc[:, h // 2, h % 2, :, :].rearrange("p j s -> p (j s)")
                        both = k[:, s, :, :].rearrange("p j s -> p (j s)")
                        eng.matmul(out, q[0][:, h, tok], both, start=True, stop=False)
                        mm = eng.matmul(out[:, 0:S], q[1][:, h, tok], both[:, 0:S], start=False, stop=True)
                    mm.then_inc(s_sc, 1)
                if isinstance(g, int) and g == 0 and s == 0:
                    eng.wait_ge(norm.s_lo, B)
                    eng.wait_ge(s_clo, NX)
                if u == 0 and live(g, s):
                    turn_values(H - 1)
                if live(g, s, 3):
                    m = n - 3
                    eng.wait_ge(s_ohi, m + 1)
                    eng.wait_ge(s_olo, m + 1)
                    wait(eng, s_add, m)
                    if s == 3:
                        for i in range(2):
                            eng.wait_ge(s_wolo[i], 2 * (g + 1))
                    for h in range(Q):
                        mm = product(eng, yb[:, :], [t[:, h * S:(h + 1) * S] for t in o],
                                     [t[:, h, :] for t in wo], h == 0, h == Q - 1)
                    mm.then_inc(s_y, 1)
                if live(g, s, 2):
                    m = n - 2
                    eng.wait_ge(s_phi, m + 1)
                    eng.wait_ge(s_plo, m + 1)
                    wait(eng, s_olo, m)
                    if u == 2:
                        eng.wait_ge(s_vlo, 2 * g + 1 + s // 4)
                    mm = product(eng, ov[:, :], [t[:, (s - 2) % B, :] for t in v], [t[:, :] for t in pT], True, True)
                    mm.then_inc(s_pv, 1)
                if projects(g, s):
                    for j in STEPS[u]:
                        project(H, g + s // 4, half, j)

            for b in range(4):
                norm.transpose(eng, b)
            eng.wait_ge(norm.s_lo, 4)
            for j in range(TILES):
                if j == K:
                    eng.wait_ge(s_clo, C)
                project(0, 0, 0, j)
            for b in range(4, B):
                norm.transpose(eng, b)
            loop(eng, step)

        @block.vector
        def _(eng):
            def rotate(H, j):
                r = 5 * H + j
                bank = pj[j % 2]
                cos, sin = (trig[:, 2 * (j == K) + i, :].unsqueeze(1).broadcast_to([P, 4, S]) for i in range(2))
                split = lambda t: t.rearrange("p (b s) -> p b s", b=4)
                eng.wait_ge(s_pj, TILES * H + j + 1)
                wait(eng, s_qlo, r if j == 0 else r - 2 if j == 1 else r - 1)
                eng.tensor_tensor(split(t1[:, j % 2, :]), split(bank[:, :]), cos, ALU.mult).then_inc(s_cos, 1)
                if j == V % 2:
                    wait(eng, s_vp, H)
                eng.tensor_tensor(split(t2[0:64, j % 2, :]), split(bank[64:128, :]), sin[0:64], ALU.mult)
                eng.tensor_tensor(split(t2[64:128, j % 2, :]), split(bank[0:64, :]), sin[64:128], ALU.mult).then_inc(s_sin, 1)

            def step(g, s):
                n = B * g + s
                H = half_cycle(g, s)
                u, half = s % 4, 1 - s // 4
                if live(g, s, 1):
                    eng.wait_ge(s_exp, n)
                    wait(eng, s_norm, n - 2)
                    eng.reciprocal(rden[:, (s - 1) % 2, :], total[:, (s - 1) % 2, :]).then_inc(s_rden, 1)
                if live(g, s, 2):
                    eng.wait_ge(s_phi, n - 1)
                    eng.tensor_tensor(pT[1][:, :], tp[:, :], pT[0][:, :].bitcast(F32), ALU.subtract).then_inc(s_plo, 1)
                if live(g, s):
                    eng.wait_ge(s_sc, n + 1)
                    wait(eng, s_tp, n - 1)
                    heads = prob[:, s % 2, :].rearrange("p (a h s) -> p a h s", a=2, h=2)
                    for a in range(2):
                        added = eng.tensor_tensor(heads[:, a], sc[:, a, :, 1, :],
                                                  mask[:, s, :].unsqueeze(1).broadcast_to([P, 2, S]), ALU.add)
                    added.then_inc(s_masked, 1)
                    eng.wait_ge(s_masked, n + 1)
                    eng.memset(carrier[:, :], 0.0)
                    for h in range(Q):
                        last = eng.tensor_tensor_reduce(
                            prob[:, s % 2, h * S:(h + 1) * S], sc[:, h // 2, h % 2, 0, :],
                            prob[:, s % 2, h * S:(h + 1) * S], 1.0, -3.4e38, ALU.add, ALU.max,
                            top[:, s % 2, h:h + 1])
                    last.then_inc(s_top, 1)
                    eng.wait_ge(s_top, n + 1)
                    wait(eng, s_exp, n - 1)
                    eng.tensor_scalar(ntop[:, s % 2, :], top[:, s % 2, :], -1.0, None, ALU.mult).then_inc(s_ntop, 1)
                if u == 0 and live(g, s):
                    eng.wait_ge(s_vhi, H)
                    vs = [t[:, 4 * (1 - half):4 * (1 - half) + 4, :] for t in v]
                    eng.tensor_tensor(vs[1], vp[:, :].rearrange("p (b d) -> p b d", b=4), vs[0].bitcast(F32),
                                      ALU.subtract).then_inc(s_vlo, 1)
                if live(g, s, 3):
                    m = n - 3
                    b = (s - 3) % B
                    eng.wait_ge(s_y, m + 1)
                    eng.tensor_tensor(y[:, b, :], yb[:, :], y[:, b, :], ALU.add).then_inc(s_add, 1)
                if live(g, s, 2):
                    eng.wait_ge(s_ohi, n - 1)
                    eng.tensor_tensor(o[1][:, :], ov[:, :], o[0][:, :].bitcast(F32), ALU.subtract).then_inc(s_olo, 1)
                for what in splits(g, s):
                    if what in (("wo", 0), ("wo", 1)):
                        eng.wait_ge(s_whi, TILES + PER * g + what[1] + 1)
                        hi, lo = split_target(what)
                        eng.tensor_tensor(lo, stage[:, slot(what), :], hi.bitcast(F32), ALU.subtract).then_inc(s_wolo[0], 1)
                if projects(g, s):
                    for j in STEPS[u]:
                        if j < V:
                            rotate(H, j)
                if isinstance(g, int) and n - 3 >= NS - B and live(g, s, 3):
                    b = (s - 3) % B
                    eng.wait_ge(s_add, n - 2)
                    next_norm.statistics(eng, b)
                    if b == 3:
                        next_norm.variances(eng, 0)
                    if b == 4:
                        next_norm.normalise(eng, 0)
                for i in next_pieces(g, s):
                    if weights.on_vector(i):
                        weights.lo(eng, i)

            def ctx_lo(j):
                eng.wait_ge(s_chi, j + 1)
                hi, lo = (t[:, j % C, j // C * HALF:(j // C + 1) * HALF] for t in cT)
                n = first.PIECES.index(("ctx", j))
                eng.tensor_tensor(lo, stage[:, n % RING, :], hi.bitcast(F32), ALU.subtract).then_inc(s_clo, 1)

            for b in range(4):
                norm.lo(eng, b)
            eng.wait_ge(s_const, 32)
            for j in range(V):
                rotate(0, j)
                if j == 0:
                    norm.statistics(eng, B - 1)
                    norm.variances(eng, 1)
                if j < 4:
                    ctx_lo(2 * j)
                    ctx_lo(2 * j + 1)
            norm.normalise(eng, 1)
            for b in range(4, B):
                norm.lo(eng, b)
            loop(eng, step)

        @block.gpsimd
        def _(eng):
            def tile_sum(H, j):
                r = 5 * H + j
                eng.wait_ge(s_cos, r + 1)
                eng.wait_ge(s_sin, r + 1)
                eng.tensor_tensor(t1[:, j % 2, :], t1[:, j % 2, :], t2[:, j % 2, :], ALU.add).then_inc(s_sum, 1)

            def tile_lo(H, half, j):
                eng.wait_ge(s_qhi, 5 * H + j + 1)
                hi, lo = where(half, j)
                eng.tensor_tensor(lo, t1[:, j % 2, :].rearrange("p (b s) -> p b s", s=S), hi.bitcast(F32),
                                  ALU.subtract).then_inc(s_qlo, 1)

            def step(g, s):
                n = B * g + s
                H = half_cycle(g, s)
                u, half = s % 4, 1 - s // 4
                if live(g, s, 1):
                    eng.wait_ge(s_rden, n)
                    e = prob[:, (s - 1) % 2, :].rearrange("p (h s) -> p h s", h=Q)
                    eng.tensor_tensor(e, e, rden[:, (s - 1) % 2, :].unsqueeze(2).broadcast_to([P, Q, S]),
                                      ALU.mult).then_inc(s_norm, 1)
                if isinstance(g, int) and n == NS - B + 6:
                    next_norm.roots(eng, 0)
                if projects(g, s):
                    for j in STEPS.get(u - 1, ()):
                        if j < V:
                            tile_lo(H, half, j)
                for what in splits(g, s):
                    if what not in (("wo", 0), ("wo", 1)):
                        kind, j = what
                        eng.wait_ge(s_whi, TILES + PER * g + (j if kind == "wo" else Q + j) + 1)
                        hi, lo = split_target(what)
                        eng.tensor_tensor(lo, stage[:, slot(what), :], hi.bitcast(F32),
                                          ALU.subtract).then_inc(s_wolo[1] if kind == "wo" else s_wlo, 1)
                if projects(g, s):
                    for j in STEPS[u]:
                        if j < V:
                            tile_sum(H, j)
                for n in next_pieces(g, s):
                    if not weights.on_vector(n):
                        weights.lo(eng, n)

            def first_lo(j):
                eng.wait_ge(s_whi, j + 1)
                n = first.PIECES.index(("w", j))
                eng.tensor_tensor(w[1][:, j, :], stage[:, n % RING, :], w[0][:, j, :].bitcast(F32),
                                  ALU.subtract).then_inc(s_wlo, 1)

            for j in range(V):
                first_lo(j)
            for j in range(V):
                tile_sum(0, j)
                tile_lo(0, 0, j)
                if j == 0:
                    norm.roots(eng, 1)
                if j == 1:
                    first_lo(V)
            loop(eng, step)


def feed_forward(nc, down_d, gate_d, gamma_d, beta_d, power, xT, w, stage, x2, norm, weights, out_d):
    M = 8
    L = 2
    E = 8
    RING = 5
    MT = M + L
    BANKS = 3
    with ExitStack() as ctx:
        sb = lambda name, shape, dt=F32: ctx.enter_context(nc.sbuf_tensor("D_" + name, shape, dt))
        pb = lambda name: ctx.enter_context(nc.psum_tensor("D_" + name, [P, D], F32))
        sem = lambda name: ctx.enter_context(nc.semaphore("D_" + name))
        pair = lambda name, shape: [sb(name + s, shape, F32R) for s in ("h", "l")]
        tile_of = lambda kind, j: [weights.place(kind, j, lo) for lo in range(2)]
        wdown = pair("down", [P, M, D])
        wlat = [[t[:, j, :] for t in w] for j in (5, weights.BASE["exp"])]
        gate = sb("gate", [P, C * E])
        ghl = sb("ghl", [P, C, 2 * E], F32R)
        hT = pair("hT", [P, MT, HALF])
        pos = sb("pos", [P, 2, D])
        sq = sb("sq", [P, 2, D])
        gamma, beta = sb("gamma", [P, D]), sb("beta", [P, D])
        shared = sb("shared", [P, D])
        glo, logit = sb("glo", [P, E]), sb("logit", [P, E])
        best, route = sb("best", [P, E]), sb("route", [P, 1])
        z = sb("z", [P, D])
        zg = sb("zg", [P, D])
        stats, moments, rstd = sb("stats", [P, 6]), sb("moments", [P, 2]), sb("rstd", [P, 1])
        acc = [pb(f"acc{i}") for i in range(BANKS)]
        dn = [pb("dn0"), pb("dn1")]
        rt, gt = pb("rt"), pb("gt")
        s_piece = [sem(f"piece{i}") for i in range(RING)]
        s_small = sem("small")
        s_hi, s_lo, s_ghi, s_glo = sem("hi"), sem("lo"), sem("ghi"), sem("glo")
        s_acc, s_pos, s_sq, s_thi, s_tlo = sem("acc"), sem("pos"), sem("sq"), sem("thi"), sem("tlo")
        s_gt, s_gcopy, s_logit, s_best, s_route = sem("gt"), sem("gcopy"), sem("logit"), sem("best"), sem("route")
        s_dn, s_shared, s_z, s_gamma, s_beta, s_res, s_ln2 = (
            sem(n) for n in ("dn", "shared", "z", "gamma", "beta", "res", "ln2"))
        s_out = sem("out")
        ln_sems = (sem("stats"), sem("moments"), sem("var"), sem("rstd"))
        norm.xT, norm.banks = xT, [dn[0], dn[1], rt, gt]
        block = ctx.enter_context(nc.Block())
        tiles = [("lat", l, 0) for l in range(L)] + [(kind, m, h) for h in range(2)
                 for kind, m in [("up", m) for m in range(M)] + [("fc1", l) for l in range(L)]]
        number = {t: i for i, t in enumerate(tiles)}
        plain = [i for i, t in enumerate(tiles) if t[0] != "up"]

        def dest(t):
            kind, m, h = t
            return wlat[m] if kind == "lat" else \
                [x[:, m if kind == "up" else M + m, :] for x in hT]

        def rank(i):
            return sum(t[0] == "up" for t in tiles[:i + 1])

        @block.sync
        def _(eng):
            for n in range(M):
                wait(eng, s_lo, n - RING + 1)
                eng.dma_start(stage[:, n % RING, :], down_d[:, n, :]).then_inc(s_piece[n % RING], 16)
                if n == 0:
                    for t, d in ((gate, gate_d), (gamma, gamma_d), (beta, beta_d)):
                        eng.dma_start(t[:, :], d).then_inc(s_small, 16)
            for b in range(B):
                eng.wait_ge(s_ln2, b + 1)
                eng.dma_start(out_d[b], x2[:, b, :]).then_inc(s_out, 16)
            eng.wait_ge(s_out, 16 * B)

        @block.scalar
        def _(eng):
            def piece_hi(n):
                eng.wait_ge(s_piece[n % RING], 16 * (n // RING + 1))
                eng.activation(wdown[0][:, n, :], stage[:, n % RING, :], ACT.Copy).then_inc(s_hi, 1)

            def relu(i):
                r = rank(i)
                eng.wait_ge(s_acc, i + 1)
                wait(eng, s_sq, r - 2)
                eng.activation(pos[:, r % 2, :], acc[i % BANKS][:, :], ACT.Relu).then_inc(s_pos, 1)

            def tile_hi(i):
                t = tiles[i]
                hi = dest(t)[0]
                if t[2] == 1:
                    eng.wait_ge(s_dn, 4)
                if t[0] == "up":
                    eng.wait_ge(s_sq, rank(i))
                    eng.activation(hi, sq[:, rank(i) % 2, :], ACT.Copy).then_inc(s_thi, 1)
                else:
                    eng.wait_ge(s_acc, i + 1)
                    eng.activation(hi, acc[i % BANKS][:, :], ACT.Copy).then_inc(s_thi, 1)

            def sequence(b):
                eng.wait_ge(s_gt, b + 1)
                wait(eng, s_logit, b)
                eng.activation(glo[:, :], gt[:, E:2 * E], ACT.Copy).then_inc(s_gcopy, 1)
                eng.wait_ge(s_dn, b + 1)
                wait(eng, s_z, b)
                eng.activation(shared[:, :], dn[b % 2][:, :], ACT.Copy).then_inc(s_shared, 1)

            for b in range(4):
                norm.hi(eng, b)
            tile_hi(0)
            tile_hi(1)
            eng.wait_ge(s_small, 48)
            eng.activation(ghl[:, :, 0:E], gate[:, :].rearrange("p (c e) -> p c e", c=C), ACT.Copy).then_inc(s_ghi, 1)
            for n in range(M):
                piece_hi(n)
                relu(L + n)
                if n == 1:
                    for b in range(4, B):
                        norm.hi(eng, b)
                if n:
                    tile_hi(L + n - 1)
            tile_hi(L + M - 1)
            for i in range(L + M, len(tiles)):
                if i == L + MT:
                    for b in range(4):
                        sequence(b)
                if tiles[i][0] == "up":
                    relu(i)
                    if tiles[i - 1][0] == "up":
                        tile_hi(i - 1)
                else:
                    if tiles[i - 1][0] == "up" and i >= L + MT:
                        tile_hi(i - 1)
                    tile_hi(i)
            for b in range(4, B):
                sequence(b)

        @block.tensor
        def _(eng):
            def tile(i):
                kind, m, h = tiles[i]
                out = acc[i % BANKS][:, :]
                j = i - BANKS
                if j >= 0:
                    if tiles[j][0] == "up":
                        eng.wait_ge(s_sq, rank(j))
                    else:
                        eng.wait_ge(s_tlo, j + 1)
                if kind == "lat":
                    for e in range(L):
                        mm = product(eng, out, [t[:, e * 256 + m * P:e * 256 + (m + 1) * P] for t in tile_of("exp", 0)],
                                     tile_of("fc2", e), e == 0, e == L - 1)
                else:
                    for c in range(C):
                        if kind == "up":
                            st = [t[:, m % 4 * P:(m % 4 + 1) * P] for t in tile_of("up", 2 * c + m // 4)]
                        else:
                            st = [t[:, c % 2 * 256 + m * P:c % 2 * 256 + (m + 1) * P] for t in tile_of("fc1", c // 2)]
                        mm = product(eng, out, st, [t[:, c, h * HALF:(h + 1) * HALF] for t in xT], c == 0, c == C - 1)
                mm.then_inc(s_acc, 1)

            def sequence(b):
                h, tok, here = b // 4, slice(b * S, (b + 1) * S), slice(b % 4 * S, (b % 4 + 1) * S)
                wait(eng, s_logit, b)
                if b == 0:
                    eng.wait_ge(s_glo, 1)
                for c in range(C):
                    eng.matmul(gt[:, 0:2 * E], xT[0][:, c, tok], ghl[:, c, :], start=c == 0, stop=False)
                    mm = eng.matmul(gt[:, 0:E], xT[1][:, c, tok], ghl[:, c, 0:E], start=False, stop=c == C - 1)
                mm.then_inc(s_gt, 1)
                wait(eng, s_shared, b - 1)
                for m in range(M):
                    eng.wait_ge(s_lo, m + 1)
                    eng.wait_ge(s_tlo, number["up", m, h] + 1)
                    product(eng, dn[b % 2][:, :], [t[:, m, here] for t in hT], [t[:, m, :] for t in wdown],
                            m == 0, m == M - 1)
                wait(eng, s_z, b)
                eng.wait_ge(s_tlo, number["fc1", L - 1, h] + 1)
                for l in range(L):
                    mm = product(eng, rt[:, :], [t[:, M + l, here] for t in hT], wlat[l],
                                 l == 0, l == L - 1)
                mm.then_inc(s_dn, 1)

            for b in range(4):
                norm.transpose(eng, b)
            weights.wait_split(eng, len(weights.PIECES))
            for i in range(L):
                tile(i)
            eng.wait_ge(norm.s_lo, 4)
            tile(L)
            tile(L + 1)
            for b in range(4, B):
                norm.transpose(eng, b)
            for i in range(L + 2, L + MT):
                tile(i)
            eng.wait_ge(norm.s_lo, B)
            for b in range(4):
                sequence(b)
            for i in range(L + MT, len(tiles)):
                tile(i)
            for b in range(4, B):
                sequence(b)

        @block.vector
        def _(eng):
            def piece_lo(n):
                eng.wait_ge(s_hi, n + 1)
                hi, lo = (t[:, n, :] for t in wdown)
                eng.tensor_tensor(lo, stage[:, n % RING, :], hi.bitcast(F32), ALU.subtract).then_inc(s_lo, 1)

            def square(i):
                r = rank(i)
                eng.wait_ge(s_pos, r)
                wait(eng, s_tlo, sq_free(i))
                eng.tensor_tensor(sq[:, r % 2, :], acc[i % BANKS][:, :], pos[:, r % 2, :], ALU.mult).then_inc(s_sq, 1)

            def sq_free(i):
                ups = [j for j in range(i) if tiles[j][0] == "up"]
                return ups[-2] + 1 if len(ups) > 1 else 0

            def tile_lo(i):
                t = tiles[i]
                hi, lo = dest(t)
                eng.wait_ge(s_thi, i + 1)
                src = sq[:, rank(i) % 2, :] if t[0] == "up" else acc[i % BANKS][:, :]
                eng.tensor_tensor(lo, src, hi.bitcast(F32), ALU.subtract).then_inc(s_tlo, 1)

            def sequence(b):
                eng.wait_ge(s_gcopy, b + 1)
                eng.tensor_tensor(logit[:, :], gt[:, 0:E], glo[:, :], ALU.add).then_inc(s_logit, 1)
                eng.wait_ge(s_logit, b + 1)
                eng.max(best[:, :], logit[:, :]).then_inc(s_best, 1)
                eng.wait_ge(s_best, b + 1)
                eng.tensor_tensor(route[:, :], best[:, 0:1], best[:, 1:2], ALU.add).then_inc(s_route, 1)
                eng.wait_ge(s_route, b + 1)
                eng.wait_ge(s_shared, b + 1)
                wait(eng, s_gamma, b)
                eng.scalar_tensor_tensor(out=z[:, :], in0=rt[:, :], scalar=route[:, 0:1], in1=shared[:, :],
                                         op0=ALU.mult, op1=ALU.add).then_inc(s_z, 1)
                eng.wait_ge(s_z, b + 1)
                mean_and_variance(eng, z[:, :], stats[:, :], moments[:, :], ln_sems, 2 * b + 1)
                wait(eng, s_res, b)
                eng.scalar_tensor_tensor(out=zg[:, :], in0=z[:, :], scalar=moments[:, 0:1], in1=gamma[:, :],
                                         op0=ALU.subtract, op1=ALU.mult).then_inc(s_gamma, 1)
                eng.wait_ge(s_gamma, b + 1)
                eng.wait_ge(ln_sems[3], 2 * b + 1)
                eng.wait_ge(s_beta, b + 1)
                eng.scalar_tensor_tensor(out=x2[:, b, :], in0=zg[:, :], scalar=rstd[:, 0:1], in1=x2[:, b, :],
                                         op0=ALU.mult, op1=ALU.add).then_inc(s_res, 1)
                eng.wait_ge(s_res, b + 1)
                layer_norm(eng, x2[:, b, :], x2[:, b, :], stats[:, :], moments[:, :], rstd[:, :], ln_sems,
                           2 * b + 2).then_inc(s_ln2, 1)

            for b in range(4):
                norm.lo(eng, b)
            norm.variances(eng, 1)
            norm.normalise(eng, 1)
            tile_lo(0)
            tile_lo(1)
            eng.wait_ge(s_ghi, 1)
            eng.tensor_tensor(ghl[:, :, E:2 * E], gate[:, :].rearrange("p (c e) -> p c e", c=C),
                              ghl[:, :, 0:E].bitcast(F32), ALU.subtract).then_inc(s_glo, 1)
            for n in range(M):
                piece_lo(n)
                square(L + n)
                if n == 1:
                    for b in range(4, B):
                        norm.lo(eng, b)
                if n:
                    tile_lo(L + n - 1)
            tile_lo(L + M - 1)
            for i in range(L + M, len(tiles)):
                if i == L + MT:
                    for b in range(4):
                        sequence(b)
                if tiles[i][0] == "up":
                    square(i)
                    if tiles[i - 1][0] == "up":
                        tile_lo(i - 1)
                else:
                    if tiles[i - 1][0] == "up" and i >= L + MT:
                        tile_lo(i - 1)
                    tile_lo(i)
            for b in range(4, B):
                sequence(b)

        @block.gpsimd
        def _(eng):
            norm.roots(eng, 1)
            eng.wait_ge(s_small, 48)
            for b in range(B):
                eng.wait_ge(norm.s_tp, b + 1)
                eng.tensor_tensor(x2[:, b, :], x2[:, b, :], beta[:, :], ALU.add).then_inc(s_beta, 1)
            for count in range(1, 2 * B + 1):
                inverse_root(eng, moments[:, :], rstd[:, :], power, ln_sems, count)


def decoder_layer(nc, x_nat, xT0, ctxT, mask, wqkvT, bqk, bv, woutT, bout, wq, wk, wv, wo, gate, up, down, fc1, fc2,
                  expT, gamma, beta, alibi_d, trig, ident_d, out):
    with ExitStack() as ctx:
        sb = lambda name, shape, dt=F32: ctx.enter_context(nc.sbuf_tensor(name, shape, dt))
        ident = sb("ident", [P, P])
        power = sb("power", [P, 1])
        x1 = sb("x", [P, B, D])
        norms = [Turn(nc, ctx, n, x1, ident[:, :], power[:, :]) for n in ("first", "second")]
        stage = sb("stage", [P, FirstPieces.RING, D])
        first = FirstPieces(nc, ctx, stage, ctxT, wq, wk, wv)
        with ExitStack() as self_ctx:
            ssb = lambda name, shape, dt=F32R: self_ctx.enter_context(nc.sbuf_tensor(name, shape, dt))
            q, k = (ssb(n, [P, 2 * C, NT]) for n in ("q", "k"))
            vhl = ssb("vhl", [P, B, HS, 2 * DH])
            rest = ssb("alibi_rest", [P, NG - FirstPieces.RING, D], F32)
            slots = [stage[:, n, :] for n in range(FirstPieces.RING)] + \
                    [rest[:, n, :] for n in range(NG - FirstPieces.RING)]
            qs = ssb("qs", [P, 2 * C, S])
            kd = ssb("kd", [P, 2 * C, 8, S])
            s_load = [self_ctx.enter_context(nc.semaphore(f"heads_loaded{i}")) for i in range(2)]
            project_self(nc, xT0, wqkvT, bqk, bv, alibi_d, x_nat, bout, ident_d, ident[:, :], power[:, :], q, k, vhl,
                         slots, x1, qs, kd, s_load)
            attend_self(nc, woutT, ident[:, :], q, k, vhl, slots, x1, qs, kd, s_load, norms[0], first)
        xT, cT = ([sb(n + s, [P, C, NT], F32R) for s in ("h", "l")] for n in ("xT", "cT"))
        w = [sb("w" + s, [P, 6, D], F32R) for s in ("h", "l")]
        weights = NextWeights(nc, ctx, stage, w, cT, {"exp": expT, "fc2": fc2, "up": up, "fc1": fc1})
        attend_cross(nc, first, wq, wk, wv, wo, mask, trig, ident[:, :], xT, cT, w, stage, x1, norms[0], norms[1], weights)
        feed_forward(nc, down, gate, gamma, beta, power[:, :], xT, w, stage, x1, norms[1], weights, out)


def tables():
    import numpy as np
    slopes = (1.0 / np.power(np.float32(2.0), np.arange(1, HS + 1, dtype=np.float32) * np.float32(8 / HS))).astype(np.float32)
    bias = slopes[:, None] * np.arange(1 - S, 1, dtype=np.float32)[None, :]
    causal = np.arange(S)[:, None] >= np.arange(S)[None, :]
    alibi = np.where(causal[:, None, :], bias[None], np.float32(-1e9)).astype(np.float32)
    inv = (1.0 / np.float32(10000.0) ** (np.arange(0, P, 2, dtype=np.float32) / np.float32(P))).astype(np.float32)
    angle = (np.arange(S, dtype=np.float32)[:, None] * inv[None, :]).astype(np.float32).T
    cos, sin = np.cos(angle), np.sin(angle)
    cos = np.concatenate([cos, cos])
    sin = np.concatenate([-sin, sin])
    scale = np.sqrt(np.float32(P))
    trig = np.stack([cos / scale, sin / scale, cos, sin], 1).astype(np.float32)
    return alibi, trig, np.eye(P, dtype=np.float32)


def kernel(**inputs):
    import numpy as np
    import concourse.bacc as bacc
    from concourse.bass_utils import run_bass_kernel_spmd

    a = {n: np.asarray(v) for n, v in inputs.items()}
    rows = lambda w: w.reshape(-1, P, w.shape[1]).transpose(1, 0, 2)
    spread = lambda v: np.broadcast_to(v[None, :], (P, v.shape[0]))
    pre, xp, fp = "L0_attn_", "L0_xattn_", "L0_ffn_"
    alibi, trig, ident = tables()
    bqkv = a[pre + "b_qkv"]
    arrays = {
        "x_nat": a["x"].transpose(1, 0, 2),
        "xT": rows(a["x"].reshape(NT, D).T),
        "ctxT": rows(a["ctx_4096"].reshape(NT, D).T),
        "mask": a["mask_BxSxS2_ff0"].transpose(1, 0, 2),
        "wqkvT": rows(a[pre + "w_qkv"].T),
        "bqk": bqkv[:2 * D].reshape(2 * C, P).T,
        "bv": spread(bqkv[2 * D:]),
        "woutT": rows(a[pre + "w_out"].T),
        "bout": spread(a[pre + "b_out"]),
        "wq": a[xp + "wq"].reshape(C, P, NG, HG, P).transpose(2, 1, 3, 0, 4).reshape(NG, P, HG, C * P),
        "wk": a[xp + "wk"].reshape(C, P, NG, P).transpose(2, 1, 0, 3).reshape(NG, P, C * P),
        "wv": a[xp + "wv"].reshape(C, P, NG, P).transpose(2, 1, 0, 3).reshape(NG, P, C * P),
        "wo": a[xp + "wo"].reshape(NG, HG, P, D).transpose(0, 2, 1, 3),
        "gate": rows(a[fp + "gate_w"]).reshape(P, -1),
        "up": rows(a[fp + "up_w"]).reshape(P, 2 * C, D),
        "down": rows(a[fp + "down_w"]),
        "fc1": rows(a[fp + "fc1_w"]).reshape(P, 2, D),
        "fc2": rows(a[fp + "fc2_w"]),
        "expT": rows(a[fp + "expert_w"].T).reshape(P, 1, D),
        "gamma": spread(a[fp + "ln_gamma"]),
        "beta": spread(a[fp + "ln_beta"]),
        "alibi": alibi.reshape(S, NG, HG * S),
        "trig": trig,
        "ident": ident,
    }
    arrays = {n + "_dram": np.ascontiguousarray(v) for n, v in arrays.items()}
    nc = bacc.Bacc("TRN2", target_bir_lowering=False, num_devices=1)
    args = [nc.dram_tensor(n, v.shape, mybir.dt.from_np(v.dtype), kind="ExternalInput").ap() for n, v in arrays.items()]
    args.append(nc.dram_tensor("out_dram", (B, S, D), F32, kind="ExternalOutput").ap())
    decoder_layer(nc, *args)
    r = run_bass_kernel_spmd(nc, [arrays], core_ids=[0])
    return r.results[0]["out_dram"]
```
